# Optimizing a Trainium2 kernel written in Bass

```python
import numpy as np
import jax
import jax.numpy as jnp

def _softmax(x, axis=-1):
    return jax.nn.softmax(x, axis=axis)

def _gelu(x):
    return jax.nn.gelu(x, approximate=True)

def _silu(x):
    return jax.nn.silu(x)

def _sigmoid(x):
    return jax.nn.sigmoid(x)

def _layernorm(x, axis=-1, eps=1e-05):
    m = jnp.mean(x, axis=axis, keepdims=True)
    v = jnp.var(x, axis=axis, keepdims=True)
    return (x - m) / jnp.sqrt(v + eps)

def _scatter_add(tgt, idx, src, axis=0):
    return tgt.at[idx].add(src)

def _segment_sum(src, seg, n):
    return jax.ops.segment_sum(src, seg, n)
kernel_name = 'mk_xattn_ffn_d2_seqx_r8_fd5d6e'

def setup_inputs(seed: int=0):
    np.random.seed(seed)
    _w = jnp.asarray

    def _rec_inputs():
        import jax
        import jax.numpy as jnp
        _rk = jax.random.key(seed)
        x = 7.22e-05 + 1 * jax.random.normal(jax.random.fold_in(_rk, 1), (64, 64, 128), jnp.float32)
        _lenS = 64 - jax.random.randint(jax.random.fold_in(_rk, 7), (64,), 0, max(1, 64 // 4) + 1, jnp.int32)
        _lenS2 = 64 - jax.random.randint(jax.random.fold_in(_rk, 8), (64,), 0, max(1, 64 // 4) + 1, jnp.int32)
        _ctx_1024P = jax.random.normal(jax.random.fold_in(_rk, 11), (64, 16, 128), jnp.float32)
        _ctx_1024c = jax.random.dirichlet(jax.random.fold_in(_rk, 511), 0.3 * jnp.ones((16,), jnp.float32), (64, 64))
        _ctx_1024t = jnp.einsum('bsk,bkd->bsd', _ctx_1024c, _ctx_1024P)
        _ctx_1024t = _ctx_1024t * jax.lax.rsqrt(jnp.mean(jnp.square(_ctx_1024t)) + 1e-12) * 0.953939
        ctx_1024 = 4.13588e-05 + 0.999923 * (_ctx_1024t + 0.3 * jax.random.normal(jax.random.fold_in(_rk, 611), (64, 64, 128), jnp.float32))
        _validS = jnp.arange(64)[None, :] < _lenS[:, None]
        _validS2 = jnp.arange(64)[None, :] < _lenS2[:, None]
        _causal = jnp.tril(jnp.ones((64, 64), dtype=bool))
        mask_BxS2_fk1 = jnp.where(jnp.broadcast_to(_validS2[:, :], (64, 64)), 1.0, 0.0).astype(jnp.float32)
        mask_BxS2_if1 = jnp.where(jnp.ones((64, 64), dtype=bool), 1, 0).astype(jnp.int32)
        return (x, ctx_1024, mask_BxS2_fk1, mask_BxS2_if1)
    x, ctx_1024, mask_BxS2_fk1, mask_BxS2_if1 = _rec_inputs()

    def _L0_xattn_setup():
        import jax, jax.numpy as jnp
        import numpy as np
        HEADS = 16
        DIM_HEAD = 64
        DIM = 128
        INNER = HEADS * DIM_HEAD

        def _split_heads(t):
            b, n, _ = t.shape
            return t.reshape(b, n, HEADS, DIM_HEAD).transpose(0, 2, 1, 3)
        key = jax.random.key(seed)
        ks = jax.random.split(key, 8)
        B, N, M = (4, 256, 256)
        x = jax.random.normal(ks[0], (B, N, DIM), dtype=jnp.float32)
        context = jax.random.normal(ks[1], (B, M, DIM), dtype=jnp.float32)
        x_mask = (jax.random.uniform(ks[2], (B, N)) > 0.1).astype(jnp.float32)
        context_mask = (jax.random.uniform(ks[3], (B, M)) > 0.1).astype(jnp.float32)
        s = 0.02
        Wq = jax.random.normal(ks[4], (DIM, INNER), dtype=jnp.float32) * s
        Wkv = jax.random.normal(ks[5], (DIM, 2 * INNER), dtype=jnp.float32) * s
        Wo = jax.random.normal(ks[6], (INNER, DIM), dtype=jnp.float32) * s
        bo = jnp.zeros((DIM,), dtype=jnp.float32)
        return {'x': x, 'context': context, 'x_mask': x_mask, 'context_mask': context_mask, 'Wq': Wq, 'Wkv': Wkv, 'Wo': Wo, 'bo': bo}
    _L0_xattn_all = _L0_xattn_setup()
    _L0_xattn_in = {k: v for k, v in _L0_xattn_all.items() if k in ('Wq', 'Wkv', 'Wo', 'bo')}
    del _L0_xattn_all

    def _L0_ffn_setup():
        import jax, jax.numpy as jnp
        import numpy as np
        D = 128
        H = 96
        E = 8
        K = 2
        NS = 2
        ROUTE_SCALE = 1.0

        def _gated_mlp(x, w1, w2):
            h = x @ w1.T
            y, g = jnp.split(h, 2, axis=-1)
            return y * jax.nn.silu(g) @ w2.T
        key = jax.random.key(seed)
        ks = jax.random.split(key, 6)
        s = 0.02
        return {'x': jax.random.normal(ks[0], (2, 128, D), jnp.float32), 'gate_w': jax.random.normal(ks[1], (E, D), jnp.float32) * s, 'W1': jax.random.normal(ks[2], (E, 2 * H, D), jnp.float32) * s, 'W2': jax.random.normal(ks[3], (E, D, H), jnp.float32) * s, 'Ws1': jax.random.normal(ks[4], (2 * NS * H, D), jnp.float32) * s, 'Ws2': jax.random.normal(ks[5], (D, NS * H), jnp.float32) * s}
    _L0_ffn_all = _L0_ffn_setup()
    _L0_ffn_in = {k: v for k, v in _L0_ffn_all.items() if k in ('gate_w', 'W1', 'W2', 'Ws1', 'Ws2')}
    del _L0_ffn_all

    def _L1_xattn_setup():
        import jax, jax.numpy as jnp
        import numpy as np
        D_MODEL = 128
        N_HEADS = 16
        HEAD_DIM = D_MODEL // N_HEADS
        ROPE_BASE = 10000.0

        def apply_rope(x):
            b, s, h, d = x.shape
            h_half = d // 2
            theta = 1.0 / ROPE_BASE ** (jnp.arange(0, d, 2, dtype=jnp.float32) / d)
            idx_theta = jnp.arange(s, dtype=jnp.float32)[:, None] * theta[None, :]
            cos = jnp.cos(idx_theta)[None, :, None, :]
            sin = jnp.sin(idx_theta)[None, :, None, :]
            xs = x.reshape(b, s, h, h_half, 2)
            x0, x1 = (xs[..., 0], xs[..., 1])
            out = jnp.stack((x0 * cos - x1 * sin, x1 * cos + x0 * sin), axis=-1)
            return out.reshape(b, s, h, d)
        key = jax.random.key(seed)
        ks = jax.random.split(key, 8)
        B, S, D = (2, 256, D_MODEL)
        scale = 0.02
        return {'Q': jax.random.normal(ks[0], (B, S, D), dtype=jnp.float32), 'K': jax.random.normal(ks[1], (B, S, D), dtype=jnp.float32), 'V': jax.random.normal(ks[2], (B, S, D), dtype=jnp.float32), 'attention_mask': jnp.ones((B, S), dtype=jnp.int32), 'Wq': jax.random.normal(ks[3], (D, D), dtype=jnp.float32) * scale, 'Wk': jax.random.normal(ks[4], (D, D), dtype=jnp.float32) * scale, 'Wv': jax.random.normal(ks[5], (D, D), dtype=jnp.float32) * scale, 'Wo': jax.random.normal(ks[6], (D, D), dtype=jnp.float32) * scale, 'bo': jax.random.normal(ks[7], (D,), dtype=jnp.float32) * scale}
    _L1_xattn_all = _L1_xattn_setup()
    _L1_xattn_in = {k: v for k, v in _L1_xattn_all.items() if k in ('Wq', 'Wk', 'Wv', 'Wo', 'bo')}
    del _L1_xattn_all

    def _L1_ffn_setup():
        import jax, jax.numpy as jnp
        import numpy as np
        EMB_DIM = 128
        HIDDEN = int(2 / 3 * 4 * EMB_DIM)
        NUM_EXPERTS = 8
        TOP_K = 2
        B, S = (4, 128)
        key = jax.random.key(seed)
        ks = jax.random.split(key, 5)
        sc = 1.0 / np.sqrt(EMB_DIM)
        sh = 1.0 / np.sqrt(HIDDEN)
        return {'x': jax.random.normal(ks[0], (B, S, EMB_DIM), dtype=jnp.float32), 'Wg': jax.random.normal(ks[1], (NUM_EXPERTS, EMB_DIM), dtype=jnp.float32) * sc, 'W1': jax.random.normal(ks[2], (NUM_EXPERTS, HIDDEN, EMB_DIM), dtype=jnp.float32) * sc, 'W2': jax.random.normal(ks[3], (NUM_EXPERTS, HIDDEN, EMB_DIM), dtype=jnp.float32) * sc, 'W3': jax.random.normal(ks[4], (NUM_EXPERTS, EMB_DIM, HIDDEN), dtype=jnp.float32) * sh}
    _L1_ffn_all = _L1_ffn_setup()
    _L1_ffn_in = {k: v for k, v in _L1_ffn_all.items() if k in ('Wg', 'W1', 'W2', 'W3')}
    del _L1_ffn_all
    return {'x': x, 'ctx_1024': ctx_1024, 'mask_BxS2_fk1': mask_BxS2_fk1, 'mask_BxS2_if1': mask_BxS2_if1, 'L0_xattn_Wq': _L0_xattn_in['Wq'], 'L0_xattn_Wkv': _L0_xattn_in['Wkv'], 'L0_xattn_Wo': _L0_xattn_in['Wo'], 'L0_xattn_bo': _L0_xattn_in['bo'], 'L0_ffn_gate_w': _L0_ffn_in['gate_w'], 'L0_ffn_W1': _L0_ffn_in['W1'], 'L0_ffn_W2': _L0_ffn_in['W2'], 'L0_ffn_Ws1': _L0_ffn_in['Ws1'], 'L0_ffn_Ws2': _L0_ffn_in['Ws2'], 'L1_xattn_Wq': _L1_xattn_in['Wq'], 'L1_xattn_Wk': _L1_xattn_in['Wk'], 'L1_xattn_Wv': _L1_xattn_in['Wv'], 'L1_xattn_Wo': _L1_xattn_in['Wo'], 'L1_xattn_bo': _L1_xattn_in['bo'], 'L1_ffn_Wg': _L1_ffn_in['Wg'], 'L1_ffn_W1': _L1_ffn_in['W1'], 'L1_ffn_W2': _L1_ffn_in['W2'], 'L1_ffn_W3': _L1_ffn_in['W3']}

def reference(x, ctx_1024, mask_BxS2_fk1, mask_BxS2_if1, L0_xattn_Wq, L0_xattn_Wkv, L0_xattn_Wo, L0_xattn_bo, L0_ffn_gate_w, L0_ffn_W1, L0_ffn_W2, L0_ffn_Ws1, L0_ffn_Ws2, L1_xattn_Wq, L1_xattn_Wk, L1_xattn_Wv, L1_xattn_Wo, L1_xattn_bo, L1_ffn_Wg, L1_ffn_W1, L1_ffn_W2, L1_ffn_W3):
    import jax
    import jax.numpy as jnp

    def _L0_xattn_ref(x, context, x_mask, context_mask, Wq, Wkv, Wo, bo):
        import jax, jax.numpy as jnp
        import numpy as np
        HEADS = 16
        DIM_HEAD = 64
        DIM = 128
        INNER = HEADS * DIM_HEAD

        def _split_heads(t):
            b, n, _ = t.shape
            return t.reshape(b, n, HEADS, DIM_HEAD).transpose(0, 2, 1, 3)
        scale = DIM_HEAD ** (-0.5)
        q = _split_heads(x @ Wq)
        kv = context @ Wkv
        k = _split_heads(kv[..., :INNER])
        v = _split_heads(kv[..., INNER:])
        dots = jnp.einsum('bhnd,bhmd->bhnm', q, k) * scale
        prod = x_mask[:, None, :, None] * context_mask[:, None, None, :]
        masked = jnp.isclose(1.0 - prod, 1.0)
        dots = jnp.where(masked, -jnp.inf, dots)
        valid = jnp.any(~masked, axis=-1, keepdims=True)
        dots = jnp.where(valid, dots, 0.0)
        attn = jax.nn.softmax(dots, axis=-1)
        attn = jnp.where(valid, attn, 0.0)
        out = jnp.einsum('bhnm,bhmd->bhnd', attn, v)
        b, h, n, d = out.shape
        out = out.transpose(0, 2, 1, 3).reshape(b, n, h * d)
        return out @ Wo + bo

    def _L0_ffn_ref(x, gate_w, W1, W2, Ws1, Ws2):
        import jax, jax.numpy as jnp
        import numpy as np
        D = 128
        H = 96
        E = 8
        K = 2
        NS = 2
        ROUTE_SCALE = 1.0

        def _gated_mlp(x, w1, w2):
            h = x @ w1.T
            y, g = jnp.split(h, 2, axis=-1)
            return y * jax.nn.silu(g) @ w2.T
        x_shape = x.shape
        xf = x.reshape(-1, D)
        T = xf.shape[0]
        scores = jax.nn.softmax((xf @ gate_w.T).astype(jnp.float32), axis=-1)
        top_vals, top_idx = jax.lax.top_k(scores, K)
        weights = (top_vals * ROUTE_SCALE).astype(x.dtype)
        w_dense = jnp.zeros((T, E), x.dtype).at[jnp.arange(T)[:, None], top_idx].set(weights)
        h = jnp.einsum('td,ehd->teh', xf, W1)
        y, g = jnp.split(h, 2, axis=-1)
        eo = jnp.einsum('teh,edh->ted', y * jax.nn.silu(g), W2)
        z = jnp.einsum('te,ted->td', w_dense, eo)
        z = z + _gated_mlp(xf, Ws1, Ws2)
        return z.reshape(x_shape)

    def _L1_xattn_ref(Q, K, V, attention_mask, Wq, Wk, Wv, Wo, bo):
        import jax, jax.numpy as jnp
        import numpy as np
        D_MODEL = 128
        N_HEADS = 16
        HEAD_DIM = D_MODEL // N_HEADS
        ROPE_BASE = 10000.0

        def apply_rope(x):
            b, s, h, d = x.shape
            h_half = d // 2
            theta = 1.0 / ROPE_BASE ** (jnp.arange(0, d, 2, dtype=jnp.float32) / d)
            idx_theta = jnp.arange(s, dtype=jnp.float32)[:, None] * theta[None, :]
            cos = jnp.cos(idx_theta)[None, :, None, :]
            sin = jnp.sin(idx_theta)[None, :, None, :]
            xs = x.reshape(b, s, h, h_half, 2)
            x0, x1 = (xs[..., 0], xs[..., 1])
            out = jnp.stack((x0 * cos - x1 * sin, x1 * cos + x0 * sin), axis=-1)
            return out.reshape(b, s, h, d)
        b, s, d = Q.shape
        q = (Q @ Wq.T).reshape(b, s, N_HEADS, HEAD_DIM)
        k = (K @ Wk.T).reshape(b, s, N_HEADS, HEAD_DIM)
        v = (V @ Wv.T).reshape(b, s, N_HEADS, HEAD_DIM)
        q = apply_rope(q)
        k = apply_rope(k)
        scores = jnp.einsum('bnhd,bmhd->bhnm', q, k) / jnp.sqrt(jnp.float32(HEAD_DIM))
        pad = (attention_mask != 0)[:, None, None, :]
        scores = jnp.where(pad, scores, -jnp.inf)
        causal = jnp.tril(jnp.ones((s, s), dtype=bool))[None, None]
        scores = jnp.where(causal, scores, -jnp.inf)
        attn = jax.nn.softmax(scores, axis=-1)
        out = jnp.einsum('bhnm,bmhd->bnhd', attn, v).reshape(b, s, d)
        return out @ Wo.T + bo

    def _L1_ffn_ref(x, Wg, W1, W2, W3):
        import jax, jax.numpy as jnp
        import numpy as np
        EMB_DIM = 128
        HIDDEN = int(2 / 3 * 4 * EMB_DIM)
        NUM_EXPERTS = 8
        TOP_K = 2
        B, S = (4, 128)
        gate_logits = jnp.einsum('bsd,ed->bse', x, Wg)
        top_v, top_i = jax.lax.top_k(gate_logits, TOP_K)
        mask = jnp.any(top_i[..., :, None] == jnp.arange(NUM_EXPERTS), axis=-2)
        sparse_logits = jnp.where(mask, gate_logits, -jnp.inf)
        gating = jax.nn.softmax(sparse_logits, axis=-1)
        h1 = jnp.einsum('bsd,ehd->bseh', x, W1)
        h2 = jnp.einsum('bsd,ehd->bseh', x, W2)
        hidden = jax.nn.silu(h1) * h2
        expert_out = jnp.einsum('bseh,edh->bsed', hidden, W3)
        return jnp.einsum('bsed,bse->bsd', expert_out, gating)
    x = x + _L0_xattn_ref(_layernorm(x, axis=-1), ctx_1024, mask_BxS2_fk1, mask_BxS2_fk1, L0_xattn_Wq, L0_xattn_Wkv, L0_xattn_Wo, L0_xattn_bo)
    x = x + _L0_ffn_ref(_layernorm(x, axis=-1), L0_ffn_gate_w, L0_ffn_W1, L0_ffn_W2, L0_ffn_Ws1, L0_ffn_Ws2)
    x = x + _L1_xattn_ref(_layernorm(x, axis=-1), ctx_1024, ctx_1024, mask_BxS2_if1, L1_xattn_Wq, L1_xattn_Wk, L1_xattn_Wv, L1_xattn_Wo, L1_xattn_bo)
    x = x + _L1_ffn_ref(_layernorm(x, axis=-1), L1_ffn_Wg, L1_ffn_W1, L1_ffn_W2, L1_ffn_W3)
    return x

_drawn_inputs = setup_inputs


def setup_inputs(seed=0):
    import zlib

    import numpy as np

    out = dict(_drawn_inputs(seed))
    spreads = {'L0_xattn_bo': (0.0, 0.1)}
    factors = {'L0_xattn_Wq': 5.956,
     'L0_ffn_gate_w': 7.261,
     'L0_ffn_W1': 6.792,
     'L0_ffn_W2': 6.59,
     'L1_xattn_Wq': 8.0,
     'L1_xattn_Wk': 8.0,
     'L0_ffn_Ws1': 3.551,
     'L0_ffn_Ws2': 3.942}
    for name, (base, spread) in spreads.items():
        noise = np.random.default_rng([zlib.crc32(name.encode()), seed]).standard_normal(out[name].shape)
        drawn = base * np.exp(spread * noise) if base else spread * noise
        out[name] = jnp.asarray(drawn.astype(out[name].dtype))
    for name, factor in factors.items():
        out[name] = (out[name] * factor).astype(out[name].dtype)
    return out
```

```python
from contextlib import ExitStack

import numpy as np

import concourse.bass as bass
from concourse import mybir

F32 = mybir.dt.float32
F32R = mybir.dt.float32r
I32 = mybir.dt.int32
U32 = mybir.dt.uint32
ALU = mybir.AluOpType
ACT = mybir.ActivationFunctionType
AX_X = mybir.AxisListType.X

P = 128
B, S, D = 64, 64, 128
TOK = B * S
TILES = TOK // P
GROUPS = TILES // 2
GT = 2 * P
GB = GT // S
HEADS = 16
HP = HEADS // 2
DH0 = 64
INNER = HEADS * DH0
DH1 = D // HEADS
E = 8
HID0 = 96
E0 = E + 2
HID1 = 341
PAD1 = 342
CH0, CHN0 = 5 * HID0, 2
CH1, CHN1 = PAD1, E
BL0, BN0 = CH0 // 4, 4
BL1, BN1 = CH1 // 3, 3
EPS = 1e-5
NEG = -1e30
MASK_TOL = 1e-8 + 1e-5


class Step:

    def __init__(self, first, reg=None, per=0):
        self.first, self.reg, self.per = first, reg, per

    def times(self, m, add=0):
        c = self.first * m + add
        return c if self.reg is None or not self.per * m else self.reg * (self.per * m) + c

    def plus(self, n):
        return Step(self.first + n, self.reg, self.per)

    def halved(self, add=0):
        c = (self.first + add) // 2
        return c if self.reg is None else self.reg * (self.per // 2) + c

    @property
    def parity(self):
        return self.first % 2


class Slots:

    def __init__(self, base, sizes, has, first_body, last_body):
        self.sizes, self.has, self.before = sizes, has, {}
        for g in range(first_body, last_body + 1):
            self.before[g] = base
            base += sum(n for k, n in sizes if has(g, k))
        self.end = base
        self.per_body = sum(n for _, n in sizes)

    def turn(self, g, part, n=0):
        k = self.before[g.first] + n
        for name, size in self.sizes:
            if name == part:
                break
            if self.has(g.first, name):
                k += size
        return Step(k, g.reg, self.per_body * g.per)


def has_attn(g, part):
    return {"ln": 0 <= g + 2 < GROUPS, "X": 0 <= g + 1 < GROUPS, "QK": 0 <= g + 1 < GROUPS,
            "V": 0 <= g + 1 < GROUPS, "S": 0 <= g < GROUPS, "PTodd": 1 <= g <= GROUPS,
            "Wo": 1 <= g <= GROUPS, "tail": 1 <= g <= GROUPS, "PTeven": 0 <= g < GROUPS}[part]


def has_ffn(g, part):
    return {"ln": 0 <= g + 2 < GROUPS, "X": 0 <= g + 1 < GROUPS, "Tp": 1 <= g <= GROUPS,
            "T0": 0 <= g < GROUPS, "L": 0 <= g + 1 < GROUPS, "T": 0 <= g < GROUPS}[part]


SLOTS = []
_base = 0
for _ph in range(4):
    if _ph % 2 == 0:
        _sizes = [("X", 1), ("QK", (8, 2)[_ph // 2]), ("PTodd", 2), ("Wo", 1), ("V", (4, 1)[_ph // 2]),
                  ("tail", 1), ("PTeven", 2)]
    else:
        _sizes = [("X", 1), ("Tp", 1), ("T0", 1), ("L", 1), ("T", 2 * (CHN0, CHN1)[_ph // 2] - 2)]
    SLOTS.append(Slots(_base, _sizes, (has_attn, has_ffn)[_ph % 2], -2, GROUPS))
    _base = SLOTS[-1].end

LOOP_FIRST, LOOP_PAIRS = 1, 6
CHUNKS = [2 * CHN0 * GROUPS, 2 * CHN1 * GROUPS]


def run_bodies(eng, first, body):
    for g in range(first, LOOP_FIRST):
        body(Step(g))
    with eng.Fori(0, LOOP_PAIRS) as i:
        for p in range(2):
            body(Step(LOOP_FIRST + p, i, 2))
    for g in range(LOOP_FIRST + 2 * LOOP_PAIRS, GROUPS + 1):
        body(Step(g))


def build(nc, x, ctxT, maskT, mask_rows, imask_rows, wa, woa, boa, wfa, wfo,
          wbg, wob, bob, wfb, wfbo, cosT, sinT, hm, vm, cz, out, upto=4):
    phases = range(upto)
    with ExitStack() as ctx:
        def sb(name, shape, dt=F32):
            return ctx.enter_context(nc.sbuf_tensor(name, shape, dt))

        def ps(name, shape):
            return ctx.enter_context(nc.psum_tensor(name, shape, F32))

        def sem(name):
            return ctx.enter_context(nc.semaphore(name))

        xs = sb("xs", [P, TILES, D])
        ident = sb("ident", [P, P])
        causal = sb("causal", [P, S])
        headmask = sb("headmask", [P, 8])
        vmask = sb("vmask", [P, 4, D])
        iota8 = sb("iota8", [P, E])
        mhalf = sb("mhalf", [P, 2])
        qmask = sb("qmask", [P, B])
        bo = [sb("bo0", [P, 1]), sb("bo1", [P, 1])]
        ropec = sb("ropec", [P, S])
        ropes = sb("ropes", [P, S])
        big_h = sb("big_h", [P, 2 * E * PAD1], F32R)
        big_l = sb("big_l", [P, 2 * E * PAD1], F32R)
        mid_h = sb("mid_h", [P, 2 * E0 * HID0], F32R)
        mid_l = sb("mid_l", [P, 2 * E0 * HID0], F32R)
        sml_h = sb("sml_h", [P, 5 * D + 2 * E], F32R)
        sml_l = sb("sml_l", [P, 5 * D + 2 * E], F32R)
        wob_sb = sb("wob_sb", [P, D])
        w2a = sb("w2a", [BL0, CHN0 * BN0, D])
        w2b = sb("w2b", [BL1, CHN1 * BN1, D])
        wst = sb("wst", [P, 2, 1024])
        xn = sb("xn", [P, 2, D])
        stats = sb("stats", [P, 2, 6])
        mv = sb("mv", [P, 2, 2])
        var = sb("var", [P, 2])
        rstd = sb("rstd", [P, 2])
        xh = sb("xh", [P, 2, GT], F32R)
        xl = sb("xl", [P, 2, GT], F32R)
        cst = sb("cst", [P, 2, GT])
        ch = sb("ch", [P, 2, GT], F32R)
        cl = sb("cl", [P, 2, GT], F32R)
        qT = sb("qT", [P, 2, HP, GT])
        kT = sb("kT", [P, 2, HP, GT])
        v = sb("v", [P, 2, 2, INNER])
        sm = sb("sm", [P, 2, HP, P])
        pT = sb("pT", [P, 2, HP, P])
        mx = sb("mx", [P, 2, HEADS])
        sums = sb("sums", [P, 2, HEADS])
        rinv = sb("rinv", [P, 2, HEADS])
        mrow = sb("mrow", [P, 2, GT])
        bias = sb("bias", [P, 2, GT])
        vmx = sb("vmx", [P, 2, GB])
        valid = sb("valid", [P, 2, GB])
        oh = sb("oh", [P, HP, GT], F32R)
        ol = sb("ol", [P, HP, GT], F32R)
        yT = sb("yT", [P, GT])
        lg = sb("lg", [P, 2, E])
        top = sb("top", [P, 2, E])
        topi = sb("topi", [P, 2, E], U32)
        topf = sb("topf", [P, 2, E])
        sel0 = sb("sel0", [P, 2, E])
        sel1 = sb("sel1", [P, 2, E])
        ex = sb("ex", [P, 2, E])
        gs = sb("gs", [P, 2])
        gr = sb("gr", [P, 2])
        wts = sb("wts", [P, 2, 2, E0])
        rope_t = v[:, 0, 1, :].rearrange("p (n t) -> p n t", n=4)
        qr = v[:, 1, 1, 0:GT]
        oT1 = v[:, 1, 1, GT:2 * GT]
        hbuf = sm[:].rearrange("p a h q -> p (a h q)")[:, 0:4 * CH0].rearrange("p (n c) -> p n c", n=4)
        flat = pT[:].rearrange("p a h q -> p (a h q)")
        th = flat[:, 0:2 * CH0].rearrange("p (n c) -> p n c", n=2)
        ub = kT[:, 0].rearrange("p h t -> p (h t)")[:, 0:2 * CH0].rearrange("p (n c) -> p n c", n=2)
        hT = qT[:, 0].rearrange("p h t -> p (h t)")[:, 0:1024].rearrange("p (n c) -> p n c", n=2)

        SC = ps("SC", [P, 2, 1024])
        AO = ps("AO", [P, 2, 512])
        ST = ps("ST", [P, 2, 512])

        class Sems:
            pass
        s = Sems()
        s.x_first = sem("x_first")
        s.x_rest = sem("x_rest")
        s.w_landed0 = sem("w_landed0")
        s.w_landed1 = sem("w_landed1")
        s.w_high = sem("w_high")
        s.w_split = sem("w_split")
        s.consts = sem("consts")
        s.misc_in = sem("misc_in")
        s.fixed = sem("fixed")
        s.stage_full0 = sem("stage_full0")
        s.stage_full1 = sem("stage_full1")
        s.stage_free0 = sem("stage_free0")
        s.stage_free1 = sem("stage_free1")
        s.bn_done = sem("bn_done")
        s.ln_stats = sem("ln_stats")
        s.var_ready = sem("var_ready")
        s.rstd_ready = sem("rstd_ready")
        s.xn_ready = sem("xn_ready")
        s.xh_ready = sem("xh_ready")
        s.ctx_in0 = sem("ctx_in0")
        s.ctx_in1 = sem("ctx_in1")
        s.ch_ready = sem("ch_ready")
        s.cl_ready = sem("cl_ready")
        s.mrow_in0 = sem("mrow_in0")
        s.mrow_in1 = sem("mrow_in1")
        s.bias_step = sem("bias_step")
        s.bias_ready = sem("bias_ready")
        s.scores = sem("scores")
        s.masked = sem("masked")
        s.maxed = sem("maxed")
        s.centred = sem("centred")
        s.expd = sem("expd")
        s.summed = sem("summed")
        s.inverted = sem("inverted")
        s.sum_ready = sem("sum_ready")
        s.probs = sem("probs")
        s.attn_out = sem("attn_out")
        s.oh_ready = sem("oh_ready")
        s.ol_ready = sem("ol_ready")
        s.rope_done = sem("rope_done")
        s.qz_ready = sem("qz_ready")
        s.gy_ready = sem("gy_ready")
        s.tanh_ready = sem("tanh_ready")
        s.gated = sem("gated")
        s.h_ready = sem("h_ready")
        s.out_done = sem("out_done")
        s.x_added = sem("x_added")
        s.pe_waited = sem("pe_waited")
        s.dve_waited = sem("dve_waited")
        s.pool_waited = sem("pool_waited")
        s.gate_step = sem("gate_step")
        s.gate_exp_in = sem("gate_exp_in")
        s.gate_exp = sem("gate_exp")
        s.w_ready = sem("w_ready")
        s.stored = sem("stored")
        stage_full = [s.stage_full0, s.stage_full1]
        stage_free = [s.stage_free0, s.stage_free1]
        w_landed = [s.w_landed0, s.w_landed1]
        ctx_in = [s.ctx_in0, s.ctx_in1]
        mrow_in = [s.mrow_in0, s.mrow_in1]
        MISC = 16 * 12

        def wchunk(src, h, l, a, n, b=0):
            return src[:, b:b + n], h[:, a:a + n], l[:, a:a + n], n
        wchunks = [wchunk(wa, big_h, big_l, c * 1024, 1024, c * 1024) for c in range(3)]
        wchunks.append(wchunk(woa, big_h, big_l, 3072, 1024))
        wchunks += [wchunk(wfa, mid_h, mid_l, c * 960, 960, c * 960) for c in range(2)]
        wchunks.append(wchunk(wbg, sml_h, sml_l, 0, 5 * D + 2 * E))
        wchunks += [wchunk(wfb, big_h, big_l, c * 912, 912, c * 912) for c in range(6)]
        if upto < 4:
            wchunks = wchunks[:7]

        def chunks_at(ph, g):
            if ph == 0 and g == 0:
                return [4, 5, 6]
            if ph == 2 and g in (14, 15, 16) and upto == 4:
                return [7 + 2 * (g - 14), 8 + 2 * (g - 14)]
            return []

        def turn_of(ph, g, part, n=0):
            return SLOTS[ph].turn(g, part, n)

        block = ctx.enter_context(nc.Block())

        @block.sync
        def _(sp):
            def load_w(c):
                if c >= 2:
                    sp.wait_ge(s.w_split, c - 1)
                src, _, _, n = wchunks[c]
                sp.dma_start(wst[:, c % 2, 0:n], src).then_inc(w_landed[c % 2], 16)

            def loads(ph, g):
                if not has_attn(g.first, "ln"):
                    return
                p, a = g.parity, ph // 2 * GROUPS
                if g.first >= 0 or ph:
                    sp.wait_ge(s.cl_ready, g.times(1, a + 1))
                    sp.wait_ge(s.bias_ready, g.times(1, a + 1))
                sp.dma_start(cst[:, p, :], ctxT[:, bass.ds(g.times(GT, 2 * GT), GT)]).then_inc(ctx_in[p], 16)
                rows = mask_rows if ph == 0 else imask_rows
                dst = mrow[:, p, :] if ph == 0 else mrow[:, p, :].bitcast(I32)
                sp.dma_start(dst, rows[0:1, bass.ds(g.times(GT, 2 * GT), GT)].broadcast_to([P, GT])
                             ).then_inc(mrow_in[p], 16)

            xd = x.rearrange("(t p) d -> p t d", p=P)
            sp.dma_start(xs[:, 0:4, :], xd[:, 0:4, :]).then_inc(s.x_first, 16)
            load_w(0)
            load_w(1)
            for dst, src in ((bo[0][:], boa), (bo[1][:], bob), (qmask[0:S, :], maskT), (qmask[S:P, :], maskT),
                             (ropec[:], cosT), (ropes[:], sinT), (headmask[:], hm), (causal[:], cz), (vmask[:], vm),
                             (wob_sb[:], wob), (w2a[:], wfo), (w2b[:], wfbo)):
                sp.dma_start(dst, src).then_inc(s.misc_in, 16)
            loads(0, Step(-2))
            loads(0, Step(-1))
            load_w(2)
            load_w(3)
            sp.dma_start(xs[:, 4:TILES, :], xd[:, 4:TILES, :]).then_inc(s.x_rest, 16)
            load_w(4)
            load_w(5)
            loads(0, Step(0))
            load_w(6)
            run_bodies(sp, 1, lambda g: loads(0, g))
            if upto > 2:
                if upto == 4:
                    load_w(7)
                    load_w(8)
                run_bodies(sp, -2, lambda g: loads(2, g))
                if upto == 4:
                    for c in range(9, 13):
                        load_w(c)
            if upto % 2:
                last = turn_of(upto - 1, Step(GROUPS), "tail")
                sp.wait_ge(stage_free[last.parity], last.halved(2))
            else:
                sp.wait_ge(s.x_added, TILES * (upto // 2) + 1)
            sp.dma_start(out.rearrange("(t p) d -> p t d", p=P), xs[:, :, :]).then_inc(s.stored, 16)
            sp.wait_ge(s.stored, 16)

        @block.gpsimd
        def _(pool):
            nc.gpsimd.memset(ident[:], 0.0).then_inc(s.fixed, 1)
            pool.wait_ge(s.fixed, 1)
            nc.gpsimd.affine_select(out=ident[:], in_=ident[:], compare_op=ALU.not_equal, fill=1.0, base=0,
                                    pattern=[[-1, P]], channel_multiplier=1).then_inc(s.consts, 1)
            nc.gpsimd.memset(mhalf[:], -0.5).then_inc(s.consts, 1)
            for e in range(E):
                nc.gpsimd.memset(iota8[:, e:e + 1], float(e)).then_inc(s.consts, 1)
            nc.gpsimd.memset(wts[:], 0.5).then_inc(s.consts, 1)
            pool.wait_ge(s.consts, 3 + E)

            def rstd_of(ph, g):
                n = ph * GROUPS + 2
                pool.wait_ge(s.ln_stats, g.times(1, n + 1))
                pool.sem_inc(s.pool_waited, 1)
                nc.gpsimd.tensor_scalar(var[:, :], mv[:, :, 1], EPS, None, ALU.add).then_inc(s.var_ready, 1)
                pool.wait_ge(s.var_ready, g.times(1, n + 1))
                nc.gpsimd.tensor_tensor(rstd[:, :], var[:, :], mhalf[:, 0:2], ALU.pow).then_inc(s.rstd_ready, 1)

            def over_keys(t, p):
                return t[:, p, :].unsqueeze(2).broadcast_to([P, HEADS, S])

            def centre(tile, p):
                pool.wait_ge(s.maxed, tile + 1)
                t = sm[:, p].rearrange("p h (b k) -> p (h b) k", b=2)
                nc.gpsimd.tensor_tensor(t, t, over_keys(mx, p), ALU.subtract).then_inc(s.centred, 1)

            def normalise(tile, p):
                pool.wait_ge(s.sum_ready, tile + 1)
                t = sm[:, p].rearrange("p h (b k) -> p (h b) k", b=2)
                nc.gpsimd.tensor_tensor(t, t, over_keys(rinv, p), ALU.mult).then_inc(s.probs, 1)

            def attn_body(ph, g):
                f, n = g.first, ph // 2 * TILES
                if has_attn(f, "PTodd"):
                    normalise(g.times(2, n - 1), 1)
                if has_attn(f, "S"):
                    centre(g.times(2, n), 0)
                if has_attn(f, "X") and ph == 2:
                    for u, dst in enumerate((qr, kT[:, (f + 1) % 2, 0, :])):
                        k = turn_of(ph, g, "QK", u)
                        pool.wait_ge(stage_free[k.parity], k.halved(2))
                        nc.gpsimd.tensor_tensor(dst, rope_t[:, 2 * u, :], rope_t[:, 2 * u + 1, :],
                                                ALU.add).then_inc(s.rope_done, 1)
                if has_attn(f, "S"):
                    normalise(g.times(2, n), 0)
                if has_attn(f, "ln"):
                    rstd_of(ph, g)
                if has_attn(f, "S"):
                    centre(g.times(2, n + 1), 1)

            for ph in phases:
                if ph % 2 == 0:
                    run_bodies(pool, -2, lambda g: attn_body(ph, g))
                else:
                    run_bodies(pool, -2, lambda g: rstd_of(ph, g) if has_ffn(g.first, "ln") else None)

        @block.scalar
        def _(act):
            def take(k):
                act.wait_ge(stage_full[k.parity], k.halved(2))
                return ST[:, k.parity, :]

            def copy(o, i):
                return nc.scalar.activation(o, i, ACT.Copy)

            def split_high(c):
                _, h, _, n = wchunks[c]
                act.wait_ge(w_landed[c % 2], 16 * (c // 2 + 1))
                copy(h, wst[:, c % 2, 0:n]).then_inc(s.w_high, 1)

            def x_high(ph, g):
                k = turn_of(ph, g, "X")
                copy(xh[:, (g.first + 1) % 2, :], take(k)[:, 0:GT]).then_inc(s.xh_ready, 1)

            def exp(tile, p):
                act.wait_ge(s.centred, tile + 1)
                nc.scalar.activation(sm[:, p], sm[:, p], ACT.Exp).then_inc(s.expd, 1)

            def probs_turned(ph, g, part, p):
                for u in range(2):
                    k = turn_of(ph, g, part, u)
                    copy(pT[:, p, 4 * u:4 * u + 4, :], take(k).rearrange("p (h q) -> p h q", h=4)
                         ).then_inc(stage_free[k.parity], 1)

            def out_high(ph, tile, p):
                act.wait_ge(s.attn_out, tile + 1)
                if ph == 0:
                    copy(oh[:, :, p * P:(p + 1) * P].rearrange("p h (b q) -> p b h q", b=2),
                         AO[:, :, :].rearrange("p b (h q) -> p b h q", h=HP)).then_inc(s.oh_ready, 1)
                else:
                    copy(oT1[:, p * P:(p + 1) * P].rearrange("p (b q) -> p b q", b=2), AO[:, :, 0:S]
                         ).then_inc(s.oh_ready, 1)

            def attn_body(ph, g):
                f, n, a = g.first, ph // 2 * TILES, ph // 2 * GROUPS
                if has_attn(f, "PTodd"):
                    exp(g.times(2, n - 1), 1)
                if has_attn(f, "X"):
                    b = (f + 1) % 2
                    x_high(ph, g)
                    act.wait_ge(ctx_in[b], g.plus(1).halved(a) * 16 + 16)
                    copy(ch[:, b, :], cst[:, b, :]).then_inc(s.ch_ready, 1)
                    if ph == 0:
                        for u in range(4):
                            k = turn_of(ph, g, "QK", 2 * u)
                            copy(qT[:, b, 2 * u:2 * u + 2, :], take(k).rearrange("p (h t) -> p h t", h=2)
                                 ).then_inc(stage_free[k.parity], 1)
                if has_attn(f, "S"):
                    exp(g.times(2, n), 0)
                if has_attn(f, "PTodd"):
                    probs_turned(ph, g, "PTodd", 1)
                    out_high(ph, g.times(2, n - 1), 1)
                if has_attn(f, "Wo"):
                    k = turn_of(ph, g, "Wo")
                    nc.scalar.activation(yT[:, :], take(k)[:, 0:GT], ACT.Identity, bias=bo[ph // 2][:, 0:1]
                                         ).then_inc(stage_free[k.parity], 1)
                if has_attn(f, "V") and ph == 0:
                    for t in range(2):
                        k = turn_of(ph, g, "V", 2 * t)
                        copy(v[:, (f + 1) % 2, t, 0:512], take(k)).then_inc(stage_free[k.parity], 1)
                if has_attn(f, "PTeven"):
                    probs_turned(ph, g, "PTeven", 0)
                    out_high(ph, g.times(2, n), 0)
                for c in chunks_at(ph, f if g.reg is None else None):
                    split_high(c)

            def ffn_body(ph, g):
                f, lay = g.first, ph // 2
                cn, w, bl, bn = ((CHN0, CH0, BL0, BN0), (CHN1, CH1, BL1, BN1))[lay]
                nj, m0 = 2 * cn, lay * CHUNKS[0]
                if has_ffn(f, "X"):
                    x_high(ph, g)
                    if f < 0:
                        gate_exp(lay, g)
                for j in range(nj):
                    if has_ffn(f, "T0"):
                        act.wait_ge(s.gy_ready, g.times(nj, m0 + j + 1))
                        nc.scalar.activation(th[:, j % 2, 0:w], SC[:, j % 2, 0:w], ACT.Tanh, scale=0.5
                                             ).then_inc(s.tanh_ready, 1)
                    turned = (turn_of(ph, g, "Tp") if j == 0 else turn_of(ph, g, "T0") if j == 1
                              else turn_of(ph, g, "T", j - 2))
                    if has_ffn(f, "Tp" if j == 0 else "T0"):
                        i = take(turned)
                        before = g.times(nj, m0 + j - 2)
                        if not (lay == 0 and f == 0 and j <= 2):
                            act.wait_ge(s.out_done, before)
                        copy(hT[0:bl, (j + 1) % 2, 0:bn * P], i[0:bl, 0:bn * P]).then_inc(stage_free[turned.parity], 1)
                    if j == 2 and has_ffn(f, "X") and f >= 0:
                        gate_exp(lay, g)

            def gate_exp(lay, g):
                act.wait_ge(s.gate_exp_in, g.times(1, lay * GROUPS + 2))
                nc.scalar.activation(ex[:], ex[:], ACT.Exp).then_inc(s.gate_exp, 1)

            for c in range(4):
                split_high(c)
            act.wait_ge(s.misc_in, MISC)
            for ph in phases:
                run_bodies(act, -2, lambda g: (attn_body, ffn_body)[ph % 2](ph, g))

        @block.vector
        def _(dve):
            V = nc.vector

            def take(k):
                dve.wait_ge(stage_full[k.parity], k.halved(2))
                return ST[:, k.parity, :]

            def split_low(c):
                _, h, l, n = wchunks[c]
                dve.wait_ge(s.w_high, c + 1)
                V.tensor_tensor(l, wst[:, c % 2, 0:n], h.bitcast(F32), ALU.subtract).then_inc(s.w_split, 1)

            def ln_stats(ph, g):
                f, n = g.first, ph * GROUPS + 2
                if f == -2:
                    if ph == 0:
                        dve.wait_ge(s.x_first, 16)
                    elif ph % 2:
                        last = turn_of(ph - 1, Step(GROUPS), "tail")
                        dve.wait_ge(stage_free[last.parity], last.halved(2))
                    else:
                        dve.wait_ge(s.x_added, TILES * (ph // 2) + 1)
                if f == 0 and ph == 0:
                    dve.wait_ge(s.x_rest, 16)
                for t in range(2):
                    V.bn_stats(stats[:, t, :], xs[:, bass.ds(g.times(2, 4 + t), 1), :].rearrange("p a d -> p (a d)")
                               ).then_inc(s.bn_done, 1)
                dve.wait_ge(s.bn_done, g.times(2, 2 * n + 2))
                dve.sem_inc(s.dve_waited, 1)
                V.bn_aggr(mv[:, 0, :], stats[:, 0, :])
                V.bn_aggr(mv[:, 1, :], stats[:, 1, :]).then_inc(s.ln_stats, 1)

            def ln_norm(ph, g):
                n = ph * GROUPS + 2
                dve.wait_ge(s.rstd_ready, g.times(1, n + 1))
                dve.wait_ge(s.ln_stats, g.times(1, n + 1))
                for t in range(2):
                    ins = V.tensor_scalar(xn[:, t, :], xs[:, bass.ds(g.times(2, 4 + t), 1), :].rearrange("p a d -> p (a d)"),
                                          mv[:, t, 0:1], rstd[:, t:t + 1], ALU.subtract, ALU.mult)
                ins.then_inc(s.xn_ready, 1)

            def x_low(ph, g):
                k = turn_of(ph, g, "X")
                b = (g.first + 1) % 2
                dve.wait_ge(s.xh_ready, g.times(1, ph * GROUPS + 2))
                V.tensor_tensor(xl[:, b, :], take(k)[:, 0:GT], xh[:, b, :].bitcast(F32), ALU.subtract
                                ).then_inc(stage_free[k.parity], 1)

            def mask_and_max(ph, tile, g, p):
                b = g.parity
                dve.wait_ge(s.scores, tile + 1)
                dve.wait_ge(s.bias_ready, g.times(1, ph // 2 * GROUPS + 1))
                V.scalar_tensor_tensor(out=sm[:, p], in0=SC[:, p].rearrange("p (h k) -> p h k", h=HP),
                                       scalar=float((DH0, DH1)[ph // 2]) ** -0.5,
                                       in1=bias[:, b, p * P:(p + 1) * P].unsqueeze(1).broadcast_to([P, HP, P]),
                                       op0=ALU.mult, op1=ALU.add).then_inc(s.masked, 1)
                dve.wait_ge(s.masked, tile + 1)
                V.tensor_reduce(mx[:, p, :], sm[:, p].rearrange("p h (b k) -> p (h b) k", b=2), AX_X, ALU.max
                                ).then_inc(s.maxed, 1)

            def sum_inverse(ph, tile, g, p):
                dve.wait_ge(s.expd, tile + 1)
                V.tensor_reduce(sums[:, p, :], sm[:, p].rearrange("p h (b k) -> p (h b) k", b=2), AX_X, ALU.add
                                ).then_inc(s.summed, 1)
                dve.wait_ge(s.summed, tile + 1)
                if ph:
                    V.reciprocal(rinv[:, p, :], sums[:, p, :]).then_inc(s.sum_ready, 1)
                    return
                V.reciprocal(rinv[:, p, :], sums[:, p, :]).then_inc(s.inverted, 1)
                dve.wait_ge(s.inverted, tile + 1)
                r = rinv[:, p, :].rearrange("p (h b) -> p h b", b=2)
                V.tensor_tensor(r, r, valid[:, g.parity, 2 * p:2 * p + 2].unsqueeze(1).broadcast_to([P, HP, 2]),
                                ALU.mult).then_inc(s.sum_ready, 1)

            def masks(ph, g):
                p, lay = 1 - g.parity, ph // 2
                dve.wait_ge(mrow_in[p], g.plus(1).halved(lay * GROUPS) * 16 + 16)
                m, o = mrow[:, p, :], bias[:, p, :]
                m4, o4 = (t.rearrange("p (b k) -> p b k", b=GB) for t in (m, o))
                done = [0]

                def link(ins):
                    done[0] += 1
                    ins.then_inc(s.bias_step, 1)
                    n = 6 if ph == 0 else 1
                    base = 0 if ph == 0 else 6 * GROUPS
                    dve.wait_ge(s.bias_step, g.times(n, base + n + done[0]))

                if ph == 0:
                    q = qmask[:, bass.ds(g.times(GB, GB), GB)].unsqueeze(2).broadcast_to([P, GB, S])
                    link(V.tensor_tensor(o4, m4, q, ALU.mult))
                    link(V.tensor_scalar(o, o, -1.0, 1.0, ALU.mult, ALU.add))
                    link(V.tensor_scalar(o, o, -1.0, None, ALU.add))
                    link(V.tensor_tensor(o, o, o, ALU.mult))
                    link(V.tensor_scalar(o, o, MASK_TOL ** 2, NEG, ALU.is_le, ALU.mult))
                    link(V.tensor_reduce(vmx[:, p, :], o4, AX_X, ALU.max))
                    V.tensor_scalar(valid[:, p, :], vmx[:, p, :], NEG / 2, None, ALU.is_ge).then_inc(s.bias_ready, 1)
                else:
                    link(V.tensor_scalar(o, m.bitcast(I32), 0.0, NEG, ALU.is_equal, ALU.mult))
                    V.tensor_tensor(o4, o4, causal[:, :].unsqueeze(1).broadcast_to([P, GB, S]), ALU.add
                                    ).then_inc(s.bias_ready, 1)

            def out_low(ph, tile, p):
                if ph:
                    return
                dve.wait_ge(s.oh_ready, tile + 1)
                hi = oh[:, :, p * P:(p + 1) * P].bitcast(F32).rearrange("p h (b q) -> p b h q", b=2)
                V.tensor_tensor(ol[:, :, p * P:(p + 1) * P].rearrange("p h (b q) -> p b h q", b=2),
                                AO[:, :, :].rearrange("p b (h q) -> p b h q", h=HP), hi, ALU.subtract
                                ).then_inc(s.ol_ready, 1)

            def attn_body(ph, g):
                f, n, a = g.first, ph // 2 * TILES, ph // 2 * GROUPS
                b = (f + 1) % 2
                if has_attn(f, "PTodd"):
                    sum_inverse(ph, g.times(2, n - 1), g.plus(-1), 1)
                if has_attn(f, "X"):
                    x_low(ph, g)
                    dve.wait_ge(s.ch_ready, g.times(1, a + 2))
                    V.tensor_tensor(cl[:, b, :], cst[:, b, :], ch[:, b, :].bitcast(F32), ALU.subtract
                                    ).then_inc(s.cl_ready, 1)
                if has_attn(f, "S"):
                    mask_and_max(ph, g.times(2, n), g, 0)
                if has_attn(f, "X"):
                    if ph == 0:
                        for u in range(4):
                            k = turn_of(ph, g, "QK", 2 * u + 1)
                            V.tensor_copy(kT[:, b, 2 * u:2 * u + 2, :], take(k).rearrange("p (h t) -> p h t", h=2)
                                          ).then_inc(stage_free[k.parity], 1)
                    else:
                        if f >= 0:
                            dve.wait_ge(s.rope_done, g.times(2, 2))
                        for u in range(2):
                            k = turn_of(ph, g, "QK", u)
                            i = take(k)
                            for r, tab in enumerate((ropec, ropes)):
                                ins = V.tensor_tensor(
                                    rope_t[:, 2 * u + r, :].rearrange("p (b k) -> p b k", b=GB),
                                    i[:, r * GT:(r + 1) * GT].rearrange("p (b k) -> p b k", b=GB),
                                    tab[:, :].unsqueeze(1).broadcast_to([P, GB, S]), ALU.mult)
                            ins.then_inc(stage_free[k.parity], 1)
                if has_attn(f, "PTodd"):
                    out_low(ph, g.times(2, n - 1), 1)
                if has_attn(f, "S"):
                    sum_inverse(ph, g.times(2, n), g, 0)
                if has_attn(f, "V"):
                    if ph == 0:
                        for t in range(2):
                            k = turn_of(ph, g, "V", 2 * t + 1)
                            V.tensor_copy(v[:, b, t, 512:1024], take(k)).then_inc(stage_free[k.parity], 1)
                    else:
                        k = turn_of(ph, g, "V")
                        i = take(k)
                        for t in range(2):
                            ins = V.tensor_tensor(
                                v[:, b, 0, t * 512:(t + 1) * 512].rearrange("p (j d) -> p j d", j=4),
                                i[:, t * D:(t + 1) * D].unsqueeze(1).broadcast_to([P, 4, D]), vmask[:, :, :], ALU.mult)
                        ins.then_inc(stage_free[k.parity], 1)
                        dve.wait_ge(s.rope_done, g.times(2, 3))
                        for j in range(8):
                            ins = V.tensor_scalar(qT[:, b, j, :], qr, headmask[:, j:j + 1], None, ALU.mult)
                        ins.then_inc(s.qz_ready, 1)
                if has_attn(f, "S"):
                    mask_and_max(ph, g.times(2, n + 1), g, 1)
                if has_attn(f, "tail"):
                    k = turn_of(ph, g, "tail")
                    xg = xs[:, bass.ds(g.times(2, -2), 2), :]
                    V.tensor_tensor(xg, take(k)[:, 0:GT].rearrange("p (t d) -> p t d", t=2), xg, ALU.add
                                    ).then_inc(stage_free[k.parity], 1)
                if has_attn(f, "ln"):
                    ln_stats(ph, g)
                if has_attn(f, "PTeven"):
                    out_low(ph, g.times(2, n), 0)
                if has_attn(f, "X"):
                    masks(ph, g)
                if has_attn(f, "ln"):
                    ln_norm(ph, g)
                for c in chunks_at(ph, f if g.reg is None else None):
                    split_low(c)

            def gate_top(ph, g):
                lay = ph // 2
                n0 = lay * GROUPS + 1
                k = turn_of(ph, g, "L")
                V.tensor_copy(lg[:], take(k)[:, 0:2 * E].rearrange("p (t e) -> p t e", t=2)
                              ).then_inc(stage_free[k.parity], 1)
                dve.wait_ge(stage_free[k.parity], k.halved(2))
                dve.sem_inc(s.dve_waited, 1)
                step = gate_link(g, n0)
                for t in range(2):
                    ins = V.max(top[:, t, :], lg[:, t, :])
                step(ins)
                V.tensor_tensor(ex[:], lg[:], top[:, :, 0:1].broadcast_to([P, 2, E]), ALU.subtract
                                ).then_inc(s.gate_exp_in, 1)
                for t in range(2):
                    ins = V.max_index(topi[:, t, :], top[:, t, :], lg[:, t, :])
                step(ins)
                step(V.tensor_copy(topf[:], topi[:]))
                io = iota8[:, :].unsqueeze(1).broadcast_to([P, 2, E])
                V.tensor_tensor(sel0[:], io, topf[:, :, 0:1].broadcast_to([P, 2, E]), ALU.is_equal)
                step(V.tensor_tensor(sel1[:], io, topf[:, :, 1:2].broadcast_to([P, 2, E]), ALU.is_equal))
                step(V.tensor_tensor(sel0[:], sel0[:], sel1[:], ALU.add))
                return step

            def gate_weights(ph, g, step):
                lay = ph // 2
                dve.wait_ge(s.gate_exp, g.times(1, lay * GROUPS + 2))
                step(V.tensor_tensor(sel1[:], ex[:], sel0[:], ALU.mult))
                step(V.tensor_reduce(gs[:, :], (ex, sel1)[lay][:], AX_X, ALU.add))
                step(V.reciprocal(gr[:, :], gs[:, :]))
                V.scalar_tensor_tensor(out=wts[:, (g.first + 1) % 2, :, 0:E], in0=sel1[:], scalar=0.5,
                                       in1=gr[:, :].unsqueeze(2).broadcast_to([P, 2, E]),
                                       op0=ALU.mult, op1=ALU.mult).then_inc(s.w_ready, 1)

            GATE_STEPS = 8

            def gate_link(g, n0):
                done = [0]

                def step(ins):
                    done[0] += 1
                    ins.then_inc(s.gate_step, 1)
                    dve.wait_ge(s.gate_step, g.times(GATE_STEPS, n0 * GATE_STEPS + done[0]))
                return step

            def ffn_body(ph, g):
                f, lay = g.first, ph // 2
                cn, w = ((CHN0, CH0), (CHN1, CH1))[lay]
                nj, m0, t0 = 2 * cn, lay * CHUNKS[0], lay * TILES
                if has_ffn(f, "X"):
                    x_low(ph, g)
                    if f < 0:
                        gate_weights(ph, g, gate_top(ph, g))
                for j in range(nj):
                    t, c = j // cn, j % cn
                    if has_ffn(f, "T0"):
                        m = g.times(nj, m0 + j)
                        gate, y, u, h = SC[:, j % 2, 0:w], SC[:, j % 2, 512:512 + w], ub[:, j % 2, 0:w], hbuf[:, j % 4, 0:w]
                        if j == 0:
                            dve.wait_ge(s.w_ready, g.times(1, lay * GROUPS + 1))
                        dve.wait_ge(s.tanh_ready, m + 1)
                        V.scalar_tensor_tensor(out=u, in0=th[:, j % 2, 0:w], scalar=1.0, in1=gate,
                                               op0=ALU.add, op1=ALU.mult).then_inc(s.gated, 1)
                        dve.wait_ge(s.gated, m + 1)
                        if not (lay == 0 and f == 0):
                            dve.wait_ge(s.out_done, m - 3)
                        for q in range(w // HID0 if lay == 0 else 1):
                            a, z = (q * HID0, (q + 1) * HID0) if lay == 0 else (0, w)
                            e = c * 5 + q if lay == 0 else c
                            ins = V.scalar_tensor_tensor(out=h[:, a:z], in0=y[:, a:z],
                                                         scalar=wts[:, g.parity, t, e:e + 1], in1=u[:, a:z],
                                                         op0=ALU.mult, op1=ALU.mult)
                        ins.then_inc(s.h_ready, 1)
                    if (j == 1 and has_ffn(f, "Tp")) or (j == cn + 1 and has_ffn(f, "T0")):
                        tile = g.times(2, -1 if j == 1 else 0)
                        dve.wait_ge(s.out_done, g.times(nj, m0 + (0 if j == 1 else cn)))
                        xt = xs[:, bass.ds(tile, 1), :].rearrange("p a d -> p (a d)")
                        V.tensor_tensor(xt, AO[:, 1 if j == 1 else 0, 0:D], xt, ALU.add).then_inc(s.x_added, 1)
                    if f >= 0 and has_ffn(f, "X") and j == 1:
                        step = gate_top(ph, g)
                    if f >= 0 and has_ffn(f, "X") and j == 2:
                        gate_weights(ph, g, step)
                    if has_ffn(f, "ln") and j == nj - 2:
                        ln_stats(ph, g)
                if has_ffn(f, "ln"):
                    ln_norm(ph, g)

            dve.sem_inc(s.x_added, 1)
            for c in range(4):
                split_low(c)
            dve.wait_ge(s.consts, 3 + E)
            dve.wait_ge(s.misc_in, MISC)
            for ph in phases:
                run_bodies(dve, -2, lambda g: (attn_body, ffn_body)[ph % 2](ph, g))

        @block.tensor
        def _(pe):
            T = nc.tensor

            def bank(k):
                if k.reg is not None or k.first >= 2:
                    pe.wait_ge(stage_free[k.parity], k.halved())
                return ST[:, k.parity, :]

            def taken(k):
                pe.wait_ge(stage_free[k.parity], k.halved(2))

            def waited():
                pe.sem_inc(s.pe_waited, 1)

            def split_product(o, wh, wl, mh, ml):
                T.matmul(o, wh, ml, start=True, stop=False)
                T.matmul(o, wh, mh, start=False, stop=False)
                return T.matmul(o, wl, mh, start=False, stop=True)

            def turn_x(ph, g):
                k = turn_of(ph, g, "X")
                o = bank(k)
                pe.wait_ge(s.xn_ready, g.times(1, ph * GROUPS + 2))
                for t in range(2):
                    ins = T.transpose(o[:, t * P:(t + 1) * P], xn[:, t, :], ident[:, :])
                ins.then_inc(stage_full[k.parity], 1)

            def project_qk(ph, g):
                b = (g.first + 1) % 2
                taken(turn_of(ph, g, "X"))
                for u in range(8 if ph == 0 else 2):
                    k = turn_of(ph, g, "QK", u)
                    o = bank(k)
                    if u == 1:
                        pe.wait_ge(s.cl_ready, g.times(1, ph // 2 * GROUPS + 2))
                    mh, ml = ((xh, xl), (ch, cl))[u % 2]
                    for r in range(2):
                        if ph == 0:
                            a, wh, wl = u % 2 * 1024 + (u // 2 * 2 + r) * P, big_h, big_l
                        else:
                            a, wh, wl = (2 * u + r) * P, sml_h, sml_l
                        ins = split_product(o[:, r * GT:(r + 1) * GT], wh[:, a:a + P], wl[:, a:a + P],
                                            mh[:, b, :], ml[:, b, :])
                    ins.then_inc(stage_full[k.parity], 1)

            def project_v(ph, g):
                b = (g.first + 1) % 2
                for t in range(2):
                    hi, lo = ch[:, b, t * P:(t + 1) * P], cl[:, b, t * P:(t + 1) * P]
                    if ph == 0:
                        for r in range(2):
                            k = turn_of(ph, g, "V", 2 * t + r)
                            o = bank(k)
                            a = 2048 + r * 512
                            split_product(o, hi, lo, big_h[:, a:a + 512], big_l[:, a:a + 512]
                                          ).then_inc(stage_full[k.parity], 1)
                    else:
                        k = turn_of(ph, g, "V")
                        o = bank(k) if t == 0 else o
                        ins = split_product(o[:, t * D:(t + 1) * D], hi, lo, sml_h[:, 4 * D:5 * D], sml_l[:, 4 * D:5 * D])
                if ph:
                    ins.then_inc(stage_full[k.parity], 1)

            def scores(ph, g, t):
                b, lay = g.parity, ph // 2
                tile = g.times(2, lay * TILES + t)
                if not (ph == 0 and g.first == 0):
                    pe.wait_ge(s.masked, tile - 1)
                if ph and t == 0:
                    pe.wait_ge(s.qz_ready, g.times(1, 1))
                    pe.wait_ge(s.rope_done, g.times(2, 2))
                waited()
                for i in range(HP):
                    for c in range(2):
                        for q in range(2):
                            tok = slice(t * P + c * S, t * P + (c + 1) * S)
                            if ph == 0:
                                hp, h2, row = i, q, q
                                lhsT, rhs = qT[row * 64:row * 64 + 64, b, hp, tok], kT[row * 64:row * 64 + 64, b, hp, tok]
                            else:
                                row, j = q, i
                                h = 8 * row + j
                                hp, h2 = h // 2, h % 2
                                lhsT, rhs = qT[row * 64:row * 64 + 64, b, j, tok], kT[row * 64:row * 64 + 64, b, 0, tok]
                            ins = T.matmul(SC[h2 * 64:h2 * 64 + 64, t, hp * P + c * S:hp * P + (c + 1) * S], lhsT, rhs,
                                           start=True, stop=True)
                ins.then_inc(s.scores, 1)

            def weight_values(ph, g, part, grp, t):
                lay = ph // 2
                tile = grp.times(2, lay * TILES + t)
                b = grp.parity
                pe.wait_ge(s.probs, tile + 1)
                for u in range(2):
                    k = turn_of(ph, g, part, u)
                    o = bank(k)
                    for i in range(4):
                        ins = T.transpose(o[:, i * P:(i + 1) * P], sm[:, t, 4 * u + i, :], ident[:, :])
                    ins.then_inc(stage_full[k.parity], 1)
                for u in range(2):
                    taken(turn_of(ph, g, part, u))
                if ph == 0:
                    if not (grp.first == 0 and grp.reg is None and t == 0):
                        pe.wait_ge(s.ol_ready, tile)
                    waited()
                    for hp in range(HP):
                        for h2 in range(2):
                            for c in range(2):
                                h = 2 * hp + h2
                                ins = T.matmul(AO[h2 * 64:h2 * 64 + 64, c, hp * S:(hp + 1) * S],
                                               v[c * S:c * S + S, b, t, h * 64:(h + 1) * 64],
                                               pT[c * S:c * S + S, t, hp, h2 * 64:h2 * 64 + 64], start=True, stop=True)
                else:
                    pe.wait_ge(s.oh_ready, tile)
                    waited()
                    for j in range(4):
                        for r in range(4):
                            for c in range(2):
                                h = 4 * r + j
                                ins = T.matmul(AO[32 * r:32 * r + 32, c, 0:S],
                                               v[c * S:c * S + S, b, 0, t * 512 + j * D + 32 * r:t * 512 + j * D + 32 * r + 32],
                                               pT[c * S:c * S + S, t, h // 2, h % 2 * 64:h % 2 * 64 + 64],
                                               start=(j == 0), stop=(j == 3))
                ins.then_inc(s.attn_out, 1)

            def project_out(ph, g):
                k = turn_of(ph, g, "Wo")
                o = bank(k)[:, 0:GT]
                if ph == 0:
                    pe.wait_ge(s.ol_ready, g.times(2, 0))
                    for hp in range(HP):
                        wh, wl = big_h[:, 3072 + hp * P:3072 + (hp + 1) * P], big_l[:, 3072 + hp * P:3072 + (hp + 1) * P]
                        T.matmul(o, wh, ol[:, hp, :], start=(hp == 0), stop=False)
                        T.matmul(o, wh, oh[:, hp, :], start=False, stop=False)
                        ins = T.matmul(o, wl, oh[:, hp, :], start=False, stop=(hp == HP - 1))
                else:
                    pe.wait_ge(s.oh_ready, g.times(2, TILES))
                    ins = T.matmul(o, wob_sb[:, :], oT1, start=True, stop=True)
                ins.then_inc(stage_full[k.parity], 1)

            def turn_back(ph, g):
                k = turn_of(ph, g, "tail")
                o = bank(k)
                taken(turn_of(ph, g, "Wo"))
                for t in range(2):
                    ins = T.transpose(o[:, t * P:(t + 1) * P], yT[:, t * P:(t + 1) * P], ident[:, :])
                ins.then_inc(stage_full[k.parity], 1)

            def attn_body(ph, g):
                f = g.first
                if has_attn(f, "X"):
                    turn_x(ph, g)
                if has_attn(f, "S"):
                    scores(ph, g, 0)
                if has_attn(f, "QK"):
                    project_qk(ph, g)
                if has_attn(f, "PTodd"):
                    weight_values(ph, g, "PTodd", g.plus(-1), 1)
                if has_attn(f, "Wo"):
                    project_out(ph, g)
                if has_attn(f, "S"):
                    scores(ph, g, 1)
                if has_attn(f, "V"):
                    project_v(ph, g)
                if has_attn(f, "tail"):
                    turn_back(ph, g)
                if has_attn(f, "PTeven"):
                    weight_values(ph, g, "PTeven", g, 0)

            def logits(ph, g):
                k = turn_of(ph, g, "L")
                o = bank(k)
                taken(turn_of(ph, g, "X"))
                b, a = (g.first + 1) % 2, 5 * D + ph // 2 * E
                for t in range(2):
                    ins = split_product(o[:, t * E:(t + 1) * E], xh[:, b, t * P:(t + 1) * P], xl[:, b, t * P:(t + 1) * P],
                                        sml_h[:, a:a + E], sml_l[:, a:a + E])
                ins.then_inc(stage_full[k.parity], 1)

            def ffn_body(ph, g):
                f, lay = g.first, ph // 2
                cn, w, bl, bn = ((CHN0, CH0, BL0, BN0), (CHN1, CH1, BL1, BN1))[lay]
                wh, wl, w2 = ((mid_h, mid_l, w2a), (big_h, big_l, w2b))[lay]
                nj, m0 = 2 * cn, lay * CHUNKS[0]
                if has_ffn(f, "X"):
                    turn_x(ph, g)
                    if f < 0:
                        logits(ph, g)
                for j in range(nj):
                    t, c = j // cn, j % cn
                    if has_ffn(f, "T0"):
                        if not (lay == 0 and f == 0 and j < 2):
                            pe.wait_ge(s.h_ready, g.times(nj, m0 + j - 1))
                        b = g.parity
                        hi, lo = xh[:, b, t * P:(t + 1) * P], xl[:, b, t * P:(t + 1) * P]
                        for r in range(2):
                            a = r * cn * w + c * w
                            ins = split_product(SC[:, j % 2, r * 512:r * 512 + w], hi, lo, wh[:, a:a + w], wl[:, a:a + w])
                        ins.then_inc(s.gy_ready, 1)
                    if has_ffn(f, "Tp" if j == 0 else "T0"):
                        k = (turn_of(ph, g, "Tp") if j == 0 else turn_of(ph, g, "T0") if j == 1
                             else turn_of(ph, g, "T", j - 2))
                        o = bank(k)
                        pe.wait_ge(s.h_ready, g.times(nj, m0 + j))
                        for q in range(bn):
                            ins = T.transpose(o[0:bl, q * P:(q + 1) * P], hbuf[:, (j - 1) % 4, q * bl:(q + 1) * bl], ident[:, :])
                        ins.then_inc(stage_full[k.parity], 1)
                    if has_ffn(f, "Tp" if j < 2 else "T0"):
                        k = (turn_of(ph, g, "X", -1) if j == 0 else turn_of(ph, g, "Tp") if j == 1
                             else turn_of(ph, g, "T0") if j == 2 else turn_of(ph, g, "T", j - 3))
                        taken(k)
                        jj = (j - 2) % nj
                        tt, cc = jj // cn, jj % cn
                        if cc == 0 and not (lay == 0 and f == 0 and j >= 2):
                            pe.wait_ge(s.x_added, g.times(2, lay * TILES + tt - (2 if j < 2 else 0)))
                        for q in range(bn):
                            ins = T.matmul(AO[:, tt, 0:D], hT[0:bl, jj % 2, q * P:(q + 1) * P], w2[0:bl, cc * bn + q, :],
                                           start=(cc == 0 and q == 0), stop=(cc == cn - 1 and q == bn - 1))
                        ins.then_inc(s.out_done, 1)
                    if f >= 0 and j == 1 and has_ffn(f, "L"):
                        logits(ph, g)

            pe.wait_ge(s.consts, 3 + E)
            pe.wait_ge(s.misc_in, MISC)
            pe.wait_ge(s.w_split, 4)
            for ph in phases:
                if ph == 1:
                    pe.wait_ge(s.w_split, 7)
                if ph == 3:
                    pe.wait_ge(s.w_split, 13)
                run_bodies(pe, -2, lambda g: (attn_body, ffn_body)[ph % 2](ph, g))


NAMES = ("x ctx_1024 mask_BxS2_fk1 mask_BxS2_if1 L0_xattn_Wq L0_xattn_Wkv L0_xattn_Wo L0_xattn_bo L0_ffn_gate_w "
         "L0_ffn_W1 L0_ffn_W2 L0_ffn_Ws1 L0_ffn_Ws2 L1_xattn_Wq L1_xattn_Wk L1_xattn_Wv L1_xattn_Wo L1_xattn_bo "
         "L1_ffn_Wg L1_ffn_W1 L1_ffn_W2 L1_ffn_W3").split()


def rope_tables():
    theta = np.float32(1.0) / np.float32(10000.0) ** (np.arange(0, DH1, 2, dtype=np.float32) / np.float32(DH1))
    angle = np.arange(S, dtype=np.float32)[None, :] * theta.astype(np.float32)[:, None]
    cos = np.repeat(np.cos(angle), 2, axis=0)
    sin = np.repeat(np.sin(angle), 2, axis=0) * np.tile(np.array([-1.0, 1.0], np.float32), DH1 // 2)[:, None]
    return np.tile(cos, (HEADS, 1)).astype(np.float32), np.tile(sin, (HEADS, 1)).astype(np.float32)


def layouts(a):
    def blocks(w, n, rows):
        return w.reshape(n, rows, D).transpose(1, 0, 2)

    swap = np.arange(D) ^ 1
    y0, g0 = a["L0_ffn_W1"][:, :HID0], a["L0_ffn_W1"][:, HID0:]
    ys, gs = a["L0_ffn_Ws1"][:2 * HID0], a["L0_ffn_Ws1"][2 * HID0:]
    wfa = np.concatenate([g0.reshape(-1, D), gs, y0.reshape(-1, D), ys]).T
    wfo = np.concatenate([a["L0_ffn_W2"].transpose(0, 2, 1).reshape(-1, D), a["L0_ffn_Ws2"].T])
    pad = ((0, 0), (0, PAD1 - HID1), (0, 0))
    wfb = np.concatenate([np.pad(a["L1_ffn_W1"], pad).reshape(-1, D), np.pad(a["L1_ffn_W2"], pad).reshape(-1, D)]).T
    wfbo = np.pad(a["L1_ffn_W3"].transpose(0, 2, 1), pad).reshape(-1, D)
    q1, k1 = a["L1_xattn_Wq"], a["L1_xattn_Wk"]
    cos, sin = rope_tables()
    dims, place = np.arange(D), np.arange(4)
    hm = (dims[:, None] // DH1 % 8 == np.arange(8)[None, :]).astype(np.float32)
    vm = np.broadcast_to(dims[None, None, :] // DH1 % 4 == place[None, :, None], (P, 4, D)).astype(np.float32)
    cz = np.where(np.arange(S)[None, :] > np.arange(P)[:, None] % S, np.float32(NEG), np.float32(0.0))
    return {
        "x": a["x"].reshape(TOK, D), "ctxT": a["ctx_1024"].reshape(TOK, D).T, "maskT": a["mask_BxS2_fk1"].T,
        "mask_rows": a["mask_BxS2_fk1"].reshape(1, TOK), "imask_rows": a["mask_BxS2_if1"].reshape(1, TOK),
        "wa": np.concatenate([a["L0_xattn_Wq"], a["L0_xattn_Wkv"]], axis=1),
        "woa": blocks(a["L0_xattn_Wo"], HP, P).reshape(P, HP * D), "boa": a["L0_xattn_bo"].reshape(D, 1),
        "wfa": wfa, "wfo": blocks(wfo, CHN0 * BN0, BL0),
        "wbg": np.concatenate([q1.T, q1[swap].T, a["L1_xattn_Wk"].T, k1[swap].T, a["L1_xattn_Wv"].T,
                               a["L0_ffn_gate_w"].T, a["L1_ffn_Wg"].T], axis=1),
        "wob": a["L1_xattn_Wo"].T, "bob": a["L1_xattn_bo"].reshape(D, 1),
        "wfb": wfb, "wfbo": blocks(wfbo, CHN1 * BN1, BL1), "cosT": cos, "sinT": sin, "hm": hm, "vm": vm, "cz": cz,
    }


UPTO = 4


def kernel(**inputs):
    import concourse.bacc as _bacc
    from concourse.bass_utils import run_bass_kernel_spmd as _run

    nc = _bacc.Bacc("TRN2", target_bir_lowering=False, num_devices=1)
    arrays, args = {}, {}
    for name, a in layouts({n: np.asarray(inputs[n]) for n in NAMES}).items():
        arrays[f"in_{name}"] = np.ascontiguousarray(a)
        args[name] = nc.dram_tensor(f"in_{name}", a.shape, mybir.dt.from_np(a.dtype), kind="ExternalInput").ap()
    out = nc.dram_tensor("out_0", (TOK, D), F32, kind="ExternalOutput").ap()
    build(nc, **args, out=out, upto=UPTO)
    r = _run(nc, [arrays], core_ids=[0])
    return r.results[0]["out_0"].reshape(B, S, D)
```

```python
from contextlib import ExitStack

import numpy as np

import concourse.bass as bass
from concourse import mybir

F32 = mybir.dt.float32
F32R = mybir.dt.float32r
I32 = mybir.dt.int32
U32 = mybir.dt.uint32
ALU = mybir.AluOpType
ACT = mybir.ActivationFunctionType
AX_X = mybir.AxisListType.X

P = 128
B, S, D = 64, 64, 128
TOK = B * S
TILES = TOK // P
GROUPS = TILES // 2
GT = 2 * P
GB = GT // S
HEADS = 16
HP = HEADS // 2
DH0 = 64
INNER = HEADS * DH0
DH1 = D // HEADS
E = 8
HID0 = 96
E0 = E + 2
HID1 = 341
PAD1 = 342
CH0, CHN0 = 5 * HID0, 2
CH1 = PAD1
BL0, BN0 = CH0 // 4, 4
BL1, BN1 = CH1 // 3, 3
REG = TOK + P
NT = 2 * TOK // P + E - 1
ROW = D + 2
NTAB = NT + 1
PADS = 2 * TOK
UNUSED = PADS + E * P
YROWS = UNUSED + (NT - 2 * TOK // P) * P
EPS = 1e-5
NEG = -1e30
MASK_TOL = 1e-8 + 1e-5


class Step:

    def __init__(self, first, reg=None, per=0):
        self.first, self.reg, self.per = first, reg, per

    def times(self, m, add=0):
        c = self.first * m + add
        return c if self.reg is None or not self.per * m else self.reg * (self.per * m) + c

    def plus(self, n):
        return Step(self.first + n, self.reg, self.per)

    def halved(self, add=0):
        c = (self.first + add) // 2
        return c if self.reg is None else self.reg * (self.per // 2) + c

    @property
    def parity(self):
        return self.first % 2


class Turn(Step):

    def __init__(self, first, reg, per, banks):
        Step.__init__(self, first, reg, per)
        self.banks = banks
        self.bank = first % banks

    def earlier(self, add=0):
        c = self.first // self.banks + add
        return c if self.reg is None else self.reg * (self.per // self.banks) + c


class Slots:

    def __init__(self, base, sizes, has, first_body, last_body, banks):
        self.sizes, self.has, self.banks, self.before = sizes, has, banks, {}
        for g in range(first_body, last_body + 1):
            self.before[g] = base
            base += sum(n for k, n in sizes if has(g, k))
        self.end = base
        self.per_body = sum(n for _, n in sizes)
        assert 2 * self.per_body % banks == 0

    def turn(self, g, part, n=0):
        k = self.before[g.first] + n
        for name, size in self.sizes:
            if name == part:
                break
            if self.has(g.first, name):
                k += size
        return Turn(k, g.reg, self.per_body * g.per, self.banks)


def has_attn(g, part):
    return {"ln": 0 <= g + 2 < GROUPS, "X": 0 <= g + 1 < GROUPS, "QKa": 0 <= g + 1 < GROUPS,
            "QKb": 0 <= g + 1 < GROUPS, "Va": 0 <= g + 1 < GROUPS, "Vb": 0 <= g + 1 < GROUPS, "S": 0 <= g < GROUPS, "PTodd": 1 <= g <= GROUPS,
            "Wo": 1 <= g <= GROUPS, "tail": 1 <= g <= GROUPS, "PTeven": 0 <= g < GROUPS}[part]


def has_ffn(g, part):
    return {"ln": 0 <= g + 2 < GROUPS, "X": 0 <= g + 1 < GROUPS, "Tp": 1 <= g <= GROUPS,
            "T0": 0 <= g < GROUPS, "L": 0 <= g + 1 < GROUPS, "T": 0 <= g < GROUPS}[part]


def has_route(g, part):
    gates, ranks = 0 <= g - 2 < GROUPS, 0 <= g - 3 < GROUPS
    return {"gates": gates, "ranks": ranks, "Xr": gates, "LR": gates or ranks}[part]


def has_attn_route(g, part):
    return has_route(g, part) if part in ("Xr", "LR") else has_attn(g, part)


def has_expert(j, part):
    return {"X": 0 <= j + 1 < NT, "U": 0 <= j < NT, "H": 0 <= j - 1 < NT, "O": 0 <= j - 2 < NT,
            "Y": 0 <= j - 3 < NT}[part]


RING = (4, 2)
LAST_BODY = (GROUPS, GROUPS, GROUPS + 2)
LOOP_FIRST, LOOP_PAIRS = (1, 1, 5), (6, 6, 4)
SLOTS = []
for _ph in range(3):
    _lay = _ph // 2
    if _ph % 2 == 0:
        _sizes = [("X", 1), ("QKa", (6, 2)[_lay]), ("PTodd", 2), ("QKb", (2, 0)[_lay]), ("Va", (2, 1)[_lay]),
                  ("Xr", _lay), ("Wo", 1), ("Vb", (2, 0)[_lay]), ("PTeven", 2), ("tail", (2, 1)[_lay]), ("LR", _lay)]
    else:
        _sizes = [("X", 1), ("Tp", 1), ("T0", 1), ("L", 1), ("T", 2 * CHN0 - 2)]
    SLOTS.append(Slots(SLOTS[_ph - 2].end if _lay else 0, _sizes, (has_attn_route, has_ffn)[_ph % 2], -2,
                       LAST_BODY[_ph], RING[_ph % 2]))
EXPERT = Slots(SLOTS[1].end, [("X", 1), ("H", 1)], has_expert, -1, NT + 2, RING[1])

TILE_FIRST, TILE_UNROLL = 5, 8
TILE_TURNS = (NT - 1 - TILE_FIRST) // TILE_UNROLL
TILE_END = TILE_FIRST + TILE_TURNS * TILE_UNROLL


def run_bodies(eng, first, body, ph):
    start, pairs = LOOP_FIRST[ph], LOOP_PAIRS[ph]
    for g in range(first, start):
        body(Step(g))
    with eng.Fori(0, pairs) as i:
        for p in range(2):
            body(Step(start + p, i, 2))
    for g in range(start + 2 * pairs, LAST_BODY[ph] + 1):
        body(Step(g))


def run_tiles(eng, body, load=None):
    def values(tile, n):
        v = load(tile, n) if load else None
        return lambda t: v[t.first - tile.first]

    def straight(bodies, lo, n):
        v = values(Step(lo), n)
        for j in bodies:
            body(Step(j), v)

    straight(range(-1, TILE_FIRST), 0, TILE_FIRST)
    with eng.Fori(0, TILE_TURNS) as i:
        v = values(Step(TILE_FIRST - 2, i, TILE_UNROLL), TILE_UNROLL + 2)
        for p in range(TILE_UNROLL):
            body(Step(TILE_FIRST + p, i, TILE_UNROLL), v)
    straight(range(TILE_END, NT + 3), TILE_END - 2, NT - TILE_END + 2)


RC_SIZES = (2 * TILES, E, E, E, TILES, E * E, NTAB, NTAB, P, P)
RC_AT = [sum(RC_SIZES[:i]) for i in range(len(RC_SIZES))]
RC_END = sum(RC_SIZES)


def build(nc, x, ctxT, maskT, mask_rows, imask_rows, wa, woa, boa, wfa, wfo,
          wbg, wob, bob, wfb, wfbo, cosT, sinT, hm, vm, cz, rc, rows_d, y_d, out, upto=4):
    phases = range(min(upto, 3))
    with ExitStack() as ctx:
        def sb(name, shape, dt=F32):
            return ctx.enter_context(nc.sbuf_tensor(name, shape, dt))

        def ps(name, shape):
            return ctx.enter_context(nc.psum_tensor(name, shape, F32))

        def sem(name):
            return ctx.enter_context(nc.semaphore(name))

        xs = sb("xs", [P, TILES, D])
        ident = sb("ident", [P, P])
        causal = sb("causal", [P, S])
        headmask = sb("headmask", [P, 8])
        vmask = sb("vmask", [P, 4, D])
        iota8 = sb("iota8", [P, E])
        mhalf = sb("mhalf", [P, 2])
        qmask = sb("qmask", [P, B])
        bo = [sb("bo0", [P, 1]), sb("bo1", [P, 1])]
        ropec = sb("ropec", [P, S])
        ropes = sb("ropes", [P, S])
        big_h = sb("big_h", [P, 2 * E * PAD1], F32R)
        big_l = sb("big_l", [P, 2 * E * PAD1], F32R)
        mid_h = sb("mid_h", [P, 2 * E0 * HID0], F32R)
        mid_l = sb("mid_l", [P, 2 * E0 * HID0], F32R)
        sml_h = sb("sml_h", [P, 5 * D + 2 * E], F32R)
        sml_l = sb("sml_l", [P, 5 * D + 2 * E], F32R)
        wob_sb = sb("wob_sb", [P, D])
        w2a = sb("w2a", [BL0, CHN0 * BN0, D])
        w2b = sb("w2b", [BL1, E * BN1, D])
        wst = sb("wst", [P, 2, 1024])
        xn = sb("xn", [P, 2, D])
        stats = sb("stats", [P, 2, 6])
        mv = sb("mv", [P, 2, 2])
        var = sb("var", [P, 2])
        rstd = sb("rstd", [P, 2])
        xh = sb("xh", [P, 2, GT], F32R)
        xl = sb("xl", [P, 2, GT], F32R)
        cst = sb("cst", [P, 2, GT])
        ch = sb("ch", [P, 2, GT], F32R)
        cl = sb("cl", [P, 2, GT], F32R)
        qT = sb("qT", [P, 2, HP, GT])
        kT = sb("kT", [P, 2, HP, GT])
        v = sb("v", [P, 2, 2, INNER])
        sm = sb("sm", [P, 2, HP, P])
        pT = sb("pT", [P, 2, HP, P])
        mx = sb("mx", [P, 2, HEADS])
        sums = sb("sums", [P, 2, HEADS])
        rinv = sb("rinv", [P, 2, HEADS])
        mrow = sb("mrow", [P, 2, GT])
        bias = sb("bias", [P, 2, GT])
        vmx = sb("vmx", [P, 2, GB])
        valid = sb("valid", [P, 2, GB])
        oh = sb("oh", [P, HP, GT], F32R)
        ol = sb("ol", [P, HP, GT], F32R)
        yT = sb("yT", [P, GT])
        lg = sb("lg", [P, 2, E])
        top = sb("top", [P, 2, E])
        topi = sb("topi", [P, 2, E], U32)
        topf = sb("topf", [P, 2, E])
        rcs = sb("rcs", [P, RC_END])
        stats_r = sb("stats_r", [P, 2, 6])
        mv_r = sb("mv_r", [P, 2, 2])
        var_r = sb("var_r", [P, 2])
        rstd_r = sb("rstd_r", [P, 2])
        ex2 = sb("ex2", [P, 2, 2])
        hot = sb("hot", [P, 2, 2, E])
        both = sb("both", [P, 2, E])
        cum = sb("cum", [P, 2, 3, E])
        rankb = sb("rankb", [P, 2, E])
        prod = sb("prod", [P, 2, 2, E])
        slotf = sb("slotf", [P, 2, 2])
        slot = sb("slot", [P, 2, 4], I32)
        count = sb("count", [P, E])
        padf = sb("padf", [P, E])
        padi = sb("padi", [P, E], I32)
        ntile = sb("ntile", [P, E])
        cume = sb("cume", [P, E])
        last = sb("last", [P, 1])
        idb = sb("idb", [P, 4], I32)
        sel0 = sb("sel0", [P, 2, E])
        sel1 = sb("sel1", [P, 2, E])
        ex = sb("ex", [P, 2, E])
        gs = sb("gs", [P, 2])
        gr = sb("gr", [P, 2])
        wts = sb("wts", [P, 2, 2, E0])
        rope_t = v[:, 0, 1, :].rearrange("p (n t) -> p n t", n=4)
        qr = v[:, 1, 1, 0:GT]
        oT1 = v[:, 1, 1, GT:2 * GT]
        hbuf = sm[:].rearrange("p a h q -> p (a h q)")[:, 0:4 * CH0].rearrange("p (n c) -> p n c", n=4)
        flat = pT[:].rearrange("p a h q -> p (a h q)")
        th = flat[:, 0:2 * CH0].rearrange("p (n c) -> p n c", n=2)
        ub = kT[:, 0].rearrange("p h t -> p (h t)")[:, 0:2 * CH0].rearrange("p (n c) -> p n c", n=2)
        vf = v[:].rearrange("p a b c -> p (a b c)")
        rows = kT[:, 0].rearrange("p h t -> p (h t)")[:, GT:GT + 8 * ROW].rearrange("p (b t k c) -> p b t k c", b=2, t=2, k=2)
        xt = vf[:, 8 * ROW:12 * ROW].rearrange("p (n c) -> p n c", n=4)
        yb = vf[:, 12 * ROW:12 * ROW + 4 * D].rearrange("p (n c) -> p n c", n=4)
        padr = kT[:, 1].rearrange("p h t -> p (h t)")[:, GT:GT + 8 * ROW].rearrange("p (e c) -> p e c", e=E)
        cmp = flat[:, 2 * CH0:2 * CH0 + NTAB * (E + 7)]
        tj, te, tb, used, alt, tab_e, tab_b = (cmp[:, NTAB * (E + i):NTAB * (E + i + 1)] for i in range(7))
        tab_e, tab_b = tab_e.bitcast(I32), tab_b.bitcast(I32)
        yl = [t[:].rearrange("p a h t -> p (a h t)").rearrange("p (n c) -> p n c", n=TILES) for t in (qT, kT)]
        hT = qT[:, 0].rearrange("p h t -> p (h t)")[:, 0:1024].rearrange("p (n c) -> p n c", n=2)

        (rc_number, rc_first, rc_pad, rc_padnum, rc_edge, rc_upto, rc_tile, rc_unused, rc_before, rc_ones) = (
            rcs[:, a:a + n] for a, n in zip(RC_AT, RC_SIZES))

        banks = ps("banks", [P, 8, 512])
        ST = banks[:, 0:4, :]
        SC = banks[:, 4:6, :]
        GY = banks[:, 2:6, :].rearrange("p (j r) c -> p j (r c)", j=2)
        AO = banks[:, 6:8, :]

        class Sems:
            pass
        s = Sems()
        s.x_first = sem("x_first")
        s.x_rest = sem("x_rest")
        s.w_landed0 = sem("w_landed0")
        s.w_landed1 = sem("w_landed1")
        s.w_high = sem("w_high")
        s.w_split = sem("w_split")
        s.consts = sem("consts")
        s.misc_in = sem("misc_in")
        s.later_in = sem("later_in")
        s.fixed = sem("fixed")
        s.bn_done = sem("bn_done")
        s.ln_stats = sem("ln_stats")
        s.var_ready = sem("var_ready")
        s.rstd_ready = sem("rstd_ready")
        s.xn_ready = sem("xn_ready")
        s.xh_ready = sem("xh_ready")
        s.ctx_in0 = sem("ctx_in0")
        s.ctx_in1 = sem("ctx_in1")
        s.ch_ready = sem("ch_ready")
        s.cl_ready = sem("cl_ready")
        s.mrow_in0 = sem("mrow_in0")
        s.mrow_in1 = sem("mrow_in1")
        s.bias_step = sem("bias_step")
        s.bias_ready = sem("bias_ready")
        s.scores = sem("scores")
        s.masked = sem("masked")
        s.maxed = sem("maxed")
        s.centred = sem("centred")
        s.expd = sem("expd")
        s.summed = sem("summed")
        s.inverted = sem("inverted")
        s.sum_ready = sem("sum_ready")
        s.probs = sem("probs")
        s.attn_out = sem("attn_out")
        s.oh_ready = sem("oh_ready")
        s.ol_ready = sem("ol_ready")
        s.rope_done = sem("rope_done")
        s.qz_ready = sem("qz_ready")
        s.gy_ready = sem("gy_ready")
        s.tanh_ready = sem("tanh_ready")
        s.gated = sem("gated")
        s.h_ready = sem("h_ready")
        s.out_done = sem("out_done")
        s.x_added = sem("x_added")
        s.pe_waited = sem("pe_waited")
        s.dve_waited = sem("dve_waited")
        s.pool_waited = sem("pool_waited")
        s.gate_step = sem("gate_step")
        s.gate_exp_in = sem("gate_exp_in")
        s.gate_exp = sem("gate_exp")
        s.w_ready = sem("w_ready")
        s.stored = sem("stored")
        s.pads_zero = sem("pads_zero")
        s.r_bn_done = sem("r_bn_done")
        s.r_stats = sem("r_stats")
        s.r_var = sem("r_var")
        s.r_rstd = sem("r_rstd")
        s.r_xn_ready = sem("r_xn_ready")
        s.r_xh_ready = sem("r_xh_ready")
        s.choices = sem("choices")
        s.route_exp_in = sem("route_exp_in")
        s.route_exp = sem("route_exp")
        s.route_step = sem("route_step")
        s.place_step = sem("place_step")
        s.rows_ready = sem("rows_ready")
        s.rows_copied = sem("rows_copied")
        s.scattered0 = sem("scattered0")
        s.scattered1 = sem("scattered1")
        s.counted = sem("counted")
        s.table_step = sem("table_step")
        s.pads_ready = sem("pads_ready")
        s.pads_stored = sem("pads_stored")
        s.tables = sem("tables")
        s.row_high = sem("row_high")
        s.e_products = sem("e_products")
        s.e_tanh = sem("e_tanh")
        s.e_gated = sem("e_gated")
        s.e_hidden = sem("e_hidden")
        s.e_out = sem("e_out")
        s.e_numbered = sem("e_numbered")
        s.e_copied = sem("e_copied")
        s.added = sem("added")
        row_in = [sem(f"row_in{i}") for i in range(4)]
        e_stored = [sem(f"e_stored{i}") for i in range(4)]
        y_in = [sem(f"y_in{i}") for i in range(4)]
        ring_full = {n: [sem(f"full_{n}_{i}") for i in range(n)] for n in RING}
        ring_free = {n: [sem(f"free_{n}_{i}") for i in range(n)] for n in RING}

        def full(k):
            return ring_full[k.banks][k.bank]

        def free(k):
            return ring_free[k.banks][k.bank]

        w_landed = [s.w_landed0, s.w_landed1]
        ctx_in = [s.ctx_in0, s.ctx_in1]
        mrow_in = [s.mrow_in0, s.mrow_in1]
        MISC, LATER = 16 * 4, 16 * 9
        scattered = [s.scattered0, s.scattered1]

        def wchunk(src, h, l, a, n, b=0):
            return src[:, b:b + n], h[:, a:a + n], l[:, a:a + n], n
        wchunks = [wchunk(wa, big_h, big_l, c * 1024, 1024, c * 1024) for c in range(3)]
        wchunks.append(wchunk(woa, big_h, big_l, 3072, 1024))
        wchunks += [wchunk(wfa, mid_h, mid_l, c * 960, 960, c * 960) for c in range(2)]
        wchunks.append(wchunk(wbg, sml_h, sml_l, 0, 5 * D + 2 * E))
        wchunks += [wchunk(wfb, big_h, big_l, c * 912, 912, c * 912) for c in range(6)]
        if upto < 4:
            wchunks = wchunks[:7]

        def chunks_at(ph, g):
            if ph == 0 and g in (-2, 0):
                return [2, 3] if g else [4, 5, 6]
            if ph == 2 and g in (-2, -1, 0):
                return [11 + 2 * g, 12 + 2 * g]
            return []

        def turn_of(ph, g, part, n=0):
            return SLOTS[ph].turn(g, part, n)

        def qk_turn(ph, g, u):
            return turn_of(ph, g, "QKa", u) if u < 6 else turn_of(ph, g, "QKb", u - 6)

        def v_turn(ph, g, u):
            return turn_of(ph, g, "Va", u) if u < 2 else turn_of(ph, g, "Vb", u - 2)

        block = ctx.enter_context(nc.Block())

        @block.sync
        def _(sp):
            def load_w(c):
                if c >= 2:
                    sp.wait_ge(s.w_split, c - 1)
                src, _, _, n = wchunks[c]
                sp.dma_start(wst[:, c % 2, 0:n], src).then_inc(w_landed[c % 2], 16)

            def loads(ph, g):
                if not has_attn(g.first, "ln"):
                    return
                p, a = g.parity, ph // 2 * GROUPS
                if g.first >= 0 or ph:
                    sp.wait_ge(s.cl_ready, g.times(1, a + 1))
                    sp.wait_ge(s.bias_ready, g.times(1, a + 1))
                sp.dma_start(cst[:, p, :], ctxT[:, bass.ds(g.times(GT, 2 * GT), GT)]).then_inc(ctx_in[p], 16)
                rows = mask_rows if ph == 0 else imask_rows
                dst = mrow[:, p, :] if ph == 0 else mrow[:, p, :].bitcast(I32)
                sp.dma_start(dst, rows[0:1, bass.ds(g.times(GT, 2 * GT), GT)].broadcast_to([P, GT])
                             ).then_inc(mrow_in[p], 16)

            xd = x.rearrange("(t p) d -> p t d", p=P)
            sp.dma_start(xs[:, 0:4, :], xd[:, 0:4, :]).then_inc(s.x_first, 16)
            load_w(0)
            load_w(1)
            loads(0, Step(-2))
            load_w(2)
            load_w(3)
            for dst, src in ((bo[0][:], boa), (bo[1][:], bob), (qmask[0:S, :], maskT), (qmask[S:P, :], maskT)):
                sp.dma_start(dst, src).then_inc(s.misc_in, 16)
            loads(0, Step(-1))
            sp.dma_start(xs[:, 4:TILES, :], xd[:, 4:TILES, :]).then_inc(s.x_rest, 16)
            load_w(4)
            load_w(5)
            for dst, src in ((ropec[:], cosT), (ropes[:], sinT), (headmask[:], hm), (causal[:], cz), (vmask[:], vm),
                             (wob_sb[:], wob), (w2a[:], wfo), (w2b[:], wfbo), (rcs[:], rc)):
                sp.dma_start(dst, src).then_inc(s.later_in, 16)
            loads(0, Step(0))
            load_w(6)
            run_bodies(sp, 1, lambda g: loads(0, g), 0)
            if upto > 2:
                if upto == 4:
                    load_w(7)
                    load_w(8)
                for g in range(-2, 1):
                    loads(2, Step(g))
                    if g >= -1:
                        load_w(2 * g + 11)
                        load_w(2 * g + 12)
                run_bodies(sp, 1, lambda g: loads(2, g), 2)
            sp.wait_ge(s.tables, 1)
            for p in range(2):
                sp.wait_ge(scattered[p], GROUPS // 2 * 4 * 16)
            sp.wait_ge(s.pads_stored, E * 16)

            def load_rows(j, base):
                if not has_expert(j.first, "U"):
                    return
                if j.first >= 4:
                    sp.wait_ge(s.e_numbered, j.times(1, -3))
                sp.dma_start(xt[:, j.first % 4, :], rows_d[bass.ds(base(j), P), :]).then_inc(row_in[j.first % 4], 16)

            def row_numbers(tile, n):
                _, r = nc.values_load_multi_w_load_instructions(
                    tab_b[0:1, bass.ds(tile.times(1), n)], engines=[mybir.EngineType.SP], min_val=0,
                    max_val=E * REG - P, skip_runtime_bounds_check_because="the table holds first rows of tiles")
                return r

            run_tiles(sp, load_rows, row_numbers)
            for i in range(4):
                sp.wait_ge(e_stored[i], 16 * len(range(i, NT, 4)))
            part = TILES // 4
            yd = y_d[0:2 * TOK, :].rearrange("(k t p) d -> k p t d", k=2, p=P)
            od = out.rearrange("(t p) d -> p t d", p=P)
            for c in range(4):
                for k in range(2):
                    sp.dma_start(yl[k][:, c * part:(c + 1) * part, :], yd[k, :, c * part:(c + 1) * part, :]
                                 ).then_inc(y_in[c], 16)
            for c in range(4):
                sp.wait_ge(s.added, 2 * (c + 1))
                sp.dma_start(od[:, c * part:(c + 1) * part, :], xs[:, c * part:(c + 1) * part, :]).then_inc(s.stored, 16)
            sp.wait_ge(s.stored, 64)

        @block.gpsimd
        def _(pool):
            nc.gpsimd.memset(ident[:], 0.0).then_inc(s.fixed, 1)
            pool.wait_ge(s.fixed, 1)
            nc.gpsimd.affine_select(out=ident[:], in_=ident[:], compare_op=ALU.not_equal, fill=1.0, base=0,
                                    pattern=[[-1, P]], channel_multiplier=1).then_inc(s.consts, 1)
            nc.gpsimd.memset(mhalf[:], -0.5).then_inc(s.consts, 1)
            for e in range(E):
                nc.gpsimd.memset(iota8[:, e:e + 1], float(e)).then_inc(s.consts, 1)
            nc.gpsimd.memset(wts[:], 0.5).then_inc(s.consts, 1)
            pool.wait_ge(s.consts, 3 + E)

            def rstd_of(ph, g):
                n = ph * GROUPS + 2
                pool.wait_ge(s.ln_stats, g.times(1, n + 1))
                pool.sem_inc(s.pool_waited, 1)
                nc.gpsimd.tensor_scalar(var[:, :], mv[:, :, 1], EPS, None, ALU.add).then_inc(s.var_ready, 1)
                pool.wait_ge(s.var_ready, g.times(1, n + 1))
                nc.gpsimd.tensor_tensor(rstd[:, :], var[:, :], mhalf[:, 0:2], ALU.pow).then_inc(s.rstd_ready, 1)

            def over_keys(t, p):
                return t[:, p, :].unsqueeze(2).broadcast_to([P, HEADS, S])

            def centre(tile, p):
                pool.wait_ge(s.maxed, tile + 1)
                t = sm[:, p].rearrange("p h (b k) -> p (h b) k", b=2)
                nc.gpsimd.tensor_tensor(t, t, over_keys(mx, p), ALU.subtract).then_inc(s.centred, 1)

            def normalise(tile, p):
                pool.wait_ge(s.sum_ready, tile + 1)
                t = sm[:, p].rearrange("p h (b k) -> p (h b) k", b=2)
                nc.gpsimd.tensor_tensor(t, t, over_keys(rinv, p), ALU.mult).then_inc(s.probs, 1)

            def attn_body(ph, g):
                f, n = g.first, ph // 2 * TILES
                if has_attn(f, "PTodd"):
                    normalise(g.times(2, n - 1), 1)
                if has_attn(f, "ln"):
                    rstd_of(ph, g)
                if ph and has_route(f, "gates"):
                    rstd_r_of(g)
                if has_attn(f, "S"):
                    centre(g.times(2, n), 0)
                if has_attn(f, "X") and ph == 2:
                    for u, dst in enumerate((qr, kT[:, (f + 1) % 2, 0, :])):
                        k = qk_turn(ph, g, u)
                        pool.wait_ge(free(k), k.earlier(1))
                        nc.gpsimd.tensor_tensor(dst, rope_t[:, 2 * u, :], rope_t[:, 2 * u + 1, :],
                                                ALU.add).then_inc(s.rope_done, 1)
                if has_attn(f, "S"):
                    normalise(g.times(2, n), 0)
                if has_attn(f, "S"):
                    centre(g.times(2, n + 1), 1)
                if ph:
                    scatter_rows(g)

            def scatter(index, row, done):
                nc.gpsimd.indirect_dma_start(rows_d, bass.IndirectOffsetOnAxis(ap=index, axis=0), row, None
                                             ).then_inc(done, 16)

            def rstd_r_of(g):
                pool.wait_ge(s.r_stats, g.times(1, -1))
                pool.sem_inc(s.pool_waited, 1)
                nc.gpsimd.tensor_scalar(var_r[:, :], mv_r[:, :, 1], EPS, None, ALU.add).then_inc(s.r_var, 1)
                pool.wait_ge(s.r_var, g.times(1, -1))
                nc.gpsimd.tensor_tensor(rstd_r[:, :], var_r[:, :], mhalf[:, 0:2], ALU.pow).then_inc(s.r_rstd, 1)

            def scatter_rows(g):
                if has_route(g.first, "ranks"):
                    b = (g.first - 3) % 2
                    pool.wait_ge(s.rows_copied, g.times(1, -2))
                    pool.wait_ge(s.rows_ready, g.times(1, -2))
                    pool.sem_inc(s.pool_waited, 1)
                    for t in range(2):
                        for k in range(2):
                            scatter(slot[:, b, 2 * t + k:2 * t + k + 1], rows[:, b, t, k, :], scattered[b])

            def expert_body(j, _):
                if has_expert(j.first, "Y"):
                    b = (j.first - 3) % 4
                    pool.wait_ge(s.e_copied, j.times(1, -2))
                    pool.sem_inc(s.pool_waited, 1)
                    nc.gpsimd.indirect_dma_start(y_d, bass.IndirectOffsetOnAxis(ap=idb[:, b:b + 1], axis=0),
                                                 yb[:, b, :], None).then_inc(e_stored[b], 16)

            for ph in phases:
                if ph % 2 == 0:
                    run_bodies(pool, -2, lambda g: attn_body(ph, g), ph)
                else:
                    run_bodies(pool, -2, lambda g: rstd_of(ph, g) if has_ffn(g.first, "ln") else None, ph)
            pool.wait_ge(s.pads_ready, 1)
            for e in range(E):
                scatter(padi[:, e:e + 1], padr[:, e, :], s.pads_stored)
            run_tiles(pool, expert_body)

        @block.scalar
        def _(act):
            def take(k):
                act.wait_ge(full(k), k.earlier(1))
                return ST[:, k.bank, :]

            def copy(o, i):
                return nc.scalar.activation(o, i, ACT.Copy)

            def split_high(c):
                _, h, _, n = wchunks[c]
                act.wait_ge(w_landed[c % 2], 16 * (c // 2 + 1))
                copy(h, wst[:, c % 2, 0:n]).then_inc(s.w_high, 1)

            def x_high(ph, g):
                k = turn_of(ph, g, "X")
                copy(xh[:, (g.first + 1) % 2, :], take(k)[:, 0:GT]).then_inc(s.xh_ready, 1)

            def exp(tile, p):
                act.wait_ge(s.centred, tile + 1)
                nc.scalar.activation(sm[:, p], sm[:, p], ACT.Exp).then_inc(s.expd, 1)

            def probs_turned(ph, g, part, p):
                for u in range(2):
                    k = turn_of(ph, g, part, u)
                    copy(pT[:, p, 4 * u:4 * u + 4, :], take(k).rearrange("p (h q) -> p h q", h=4)
                         ).then_inc(free(k), 1)

            def out_high(ph, tile, p):
                act.wait_ge(s.attn_out, tile + 1)
                if ph == 0:
                    copy(oh[:, :, p * P:(p + 1) * P].rearrange("p h (b q) -> p b h q", b=2),
                         AO[:, :, :].rearrange("p b (h q) -> p b h q", h=HP)).then_inc(s.oh_ready, 1)
                else:
                    copy(oT1[:, p * P:(p + 1) * P].rearrange("p (b q) -> p b q", b=2), AO[:, :, 0:S]
                         ).then_inc(s.oh_ready, 1)

            def queries(g, pairs):
                for u in pairs:
                    k = qk_turn(0, g, 2 * u)
                    copy(qT[:, (g.first + 1) % 2, 2 * u:2 * u + 2, :], take(k).rearrange("p (h t) -> p h t", h=2)
                         ).then_inc(free(k), 1)

            def values(g, t):
                k = v_turn(0, g, 2 * t)
                copy(v[:, (g.first + 1) % 2, t, 0:512], take(k)).then_inc(free(k), 1)

            def attn_body(ph, g):
                f, n, a = g.first, ph // 2 * TILES, ph // 2 * GROUPS
                if has_attn(f, "PTodd"):
                    exp(g.times(2, n - 1), 1)
                if has_attn(f, "X"):
                    b = (f + 1) % 2
                    x_high(ph, g)
                    act.wait_ge(ctx_in[b], g.plus(1).halved(a) * 16 + 16)
                    copy(ch[:, b, :], cst[:, b, :]).then_inc(s.ch_ready, 1)
                    if ph == 0:
                        queries(g, range(3))
                if has_attn(f, "PTodd"):
                    probs_turned(ph, g, "PTodd", 1)
                if has_attn(f, "QKb") and ph == 0:
                    queries(g, (3,))
                if has_attn(f, "PTodd"):
                    out_high(ph, g.times(2, n - 1), 1)
                if has_attn(f, "S"):
                    exp(g.times(2, n), 0)
                if ph and has_route(f, "gates"):
                    route_high(g)
                if has_attn(f, "Va") and ph == 0:
                    values(g, 0)
                if has_attn(f, "Wo"):
                    k = turn_of(ph, g, "Wo")
                    nc.scalar.activation(yT[:, :], take(k)[:, 0:GT], ACT.Identity, bias=bo[ph // 2][:, 0:1]
                                         ).then_inc(free(k), 1)
                if has_attn(f, "Vb") and ph == 0:
                    values(g, 1)
                if has_attn(f, "PTeven"):
                    probs_turned(ph, g, "PTeven", 0)
                    out_high(ph, g.times(2, n), 0)
                if ph and has_route(f, "gates"):
                    route_exp(g)
                for c in chunks_at(ph, f if g.reg is None else None):
                    split_high(c)

            def ffn_body(ph, g):
                f, lay = g.first, ph // 2
                cn, w, bl, bn = CHN0, CH0, BL0, BN0
                nj, m0 = 2 * cn, 0
                if has_ffn(f, "X"):
                    x_high(ph, g)
                    if f < 0:
                        gate_exp(lay, g)
                for j in range(nj):
                    if has_ffn(f, "T0"):
                        act.wait_ge(s.gy_ready, g.times(nj, m0 + j + 1))
                        nc.scalar.activation(th[:, j % 2, 0:w], GY[:, j % 2, 0:w], ACT.Tanh, scale=0.5
                                             ).then_inc(s.tanh_ready, 1)
                    turned = (turn_of(ph, g, "Tp") if j == 0 else turn_of(ph, g, "T0") if j == 1
                              else turn_of(ph, g, "T", j - 2))
                    if has_ffn(f, "Tp" if j == 0 else "T0"):
                        i = take(turned)
                        before = g.times(nj, m0 + j - 2)
                        if not (lay == 0 and f == 0 and j <= 2):
                            act.wait_ge(s.out_done, before)
                        copy(hT[0:bl, (j + 1) % 2, 0:bn * P], i[0:bl, 0:bn * P]).then_inc(free(turned), 1)
                    if j == 2 and has_ffn(f, "X") and f >= 0:
                        gate_exp(lay, g)

            def route_high(g):
                b = g.parity
                copy(xh[:, b, :], take(turn_of(2, g, "Xr"))[:, 0:GT]).then_inc(s.r_xh_ready, 1)
                act.wait_ge(s.r_xn_ready, g.times(1, -1))
                copy(rows[:, b, :, 1, 0:D], rows[:, b, :, 0, 0:D]).then_inc(s.rows_copied, 1)

            def route_exp(g):
                act.wait_ge(s.route_exp_in, g.times(1, -1))
                nc.scalar.activation(ex2[:], ex2[:], ACT.Exp).then_inc(s.route_exp, 1)

            def expert_body(j, _):
                f = j.first
                if has_expert(f, "X"):
                    copy(xh[:, (f + 1) % 2, 0:P], take(EXPERT.turn(j, "X"))[:, 0:P]).then_inc(s.row_high, 1)
                if has_expert(f, "U"):
                    act.wait_ge(s.e_products, j.times(1, 1))
                    nc.scalar.activation(th[:, f % 2, 0:CH1], GY[:, f % 2, 0:CH1], ACT.Tanh, scale=0.5
                                         ).then_inc(s.e_tanh, 1)
                if has_expert(f, "H"):
                    k = EXPERT.turn(j, "H")
                    if f >= 3:
                        act.wait_ge(s.e_out, j.times(1, -2))
                    copy(hT[0:BL1, (f - 1) % 2, 0:BN1 * P], take(k)[0:BL1, 0:BN1 * P]).then_inc(free(k), 1)

            def gate_exp(lay, g):
                act.wait_ge(s.gate_exp_in, g.times(1, lay * GROUPS + 2))
                nc.scalar.activation(ex[:], ex[:], ACT.Exp).then_inc(s.gate_exp, 1)

            for c in range(2):
                split_high(c)
            act.wait_ge(s.misc_in, MISC)
            for ph in phases:
                run_bodies(act, -2, lambda g: (attn_body, ffn_body)[ph % 2](ph, g), ph)
            run_tiles(act, expert_body)

        @block.vector
        def _(dve):
            V = nc.vector

            def take(k):
                dve.wait_ge(full(k), k.earlier(1))
                return ST[:, k.bank, :]

            def split_low(c):
                _, h, l, n = wchunks[c]
                dve.wait_ge(s.w_high, c + 1)
                V.tensor_tensor(l, wst[:, c % 2, 0:n], h.bitcast(F32), ALU.subtract).then_inc(s.w_split, 1)

            def ln_stats(ph, g):
                f, n = g.first, ph * GROUPS + 2
                if f == -2:
                    if ph == 0:
                        dve.wait_ge(s.x_first, 16)
                    elif ph % 2:
                        last = turn_of(ph - 1, Step(GROUPS), "tail", 2 - (ph + 1) // 2)
                        dve.wait_ge(free(last), last.earlier(1))
                    else:
                        dve.wait_ge(s.x_added, TILES * (ph // 2) + 1)
                if f == 0 and ph == 0:
                    dve.wait_ge(s.x_rest, 16)
                for t in range(2):
                    V.bn_stats(stats[:, t, :], xs[:, bass.ds(g.times(2, 4 + t), 1), :].rearrange("p a d -> p (a d)")
                               ).then_inc(s.bn_done, 1)
                dve.wait_ge(s.bn_done, g.times(2, 2 * n + 2))
                dve.sem_inc(s.dve_waited, 1)
                V.bn_aggr(mv[:, 0, :], stats[:, 0, :])
                V.bn_aggr(mv[:, 1, :], stats[:, 1, :]).then_inc(s.ln_stats, 1)

            def ln_norm(ph, g):
                n = ph * GROUPS + 2
                dve.wait_ge(s.rstd_ready, g.times(1, n + 1))
                dve.wait_ge(s.ln_stats, g.times(1, n + 1))
                for t in range(2):
                    ins = V.tensor_scalar(xn[:, t, :], xs[:, bass.ds(g.times(2, 4 + t), 1), :].rearrange("p a d -> p (a d)"),
                                          mv[:, t, 0:1], rstd[:, t:t + 1], ALU.subtract, ALU.mult)
                ins.then_inc(s.xn_ready, 1)

            def x_low(ph, g):
                k = turn_of(ph, g, "X")
                b = (g.first + 1) % 2
                dve.wait_ge(s.xh_ready, g.times(1, ph * GROUPS + 2))
                V.tensor_tensor(xl[:, b, :], take(k)[:, 0:GT], xh[:, b, :].bitcast(F32), ALU.subtract
                                ).then_inc(free(k), 1)

            def mask_and_max(ph, tile, g, p):
                b = g.parity
                dve.wait_ge(s.scores, tile + 1)
                dve.wait_ge(s.bias_ready, g.times(1, ph // 2 * GROUPS + 1))
                V.scalar_tensor_tensor(out=sm[:, p], in0=SC.rearrange("p a (h k) -> p (a h) k", h=4),
                                       scalar=float((DH0, DH1)[ph // 2]) ** -0.5,
                                       in1=bias[:, b, p * P:(p + 1) * P].unsqueeze(1).broadcast_to([P, HP, P]),
                                       op0=ALU.mult, op1=ALU.add).then_inc(s.masked, 1)
                dve.wait_ge(s.masked, tile + 1)
                V.tensor_reduce(mx[:, p, :], sm[:, p].rearrange("p h (b k) -> p (h b) k", b=2), AX_X, ALU.max
                                ).then_inc(s.maxed, 1)

            def sum_inverse(ph, tile, g, p):
                dve.wait_ge(s.expd, tile + 1)
                V.tensor_reduce(sums[:, p, :], sm[:, p].rearrange("p h (b k) -> p (h b) k", b=2), AX_X, ALU.add
                                ).then_inc(s.summed, 1)
                dve.wait_ge(s.summed, tile + 1)
                if ph:
                    V.reciprocal(rinv[:, p, :], sums[:, p, :]).then_inc(s.sum_ready, 1)
                    return
                V.reciprocal(rinv[:, p, :], sums[:, p, :]).then_inc(s.inverted, 1)
                dve.wait_ge(s.inverted, tile + 1)
                r = rinv[:, p, :].rearrange("p (h b) -> p h b", b=2)
                V.tensor_tensor(r, r, valid[:, g.parity, 2 * p:2 * p + 2].unsqueeze(1).broadcast_to([P, HP, 2]),
                                ALU.mult).then_inc(s.sum_ready, 1)

            def masks(ph, g):
                p, lay = 1 - g.parity, ph // 2
                dve.wait_ge(mrow_in[p], g.plus(1).halved(lay * GROUPS) * 16 + 16)
                m, o = mrow[:, p, :], bias[:, p, :]
                m4, o4 = (t.rearrange("p (b k) -> p b k", b=GB) for t in (m, o))
                done = [0]

                def link(ins):
                    done[0] += 1
                    ins.then_inc(s.bias_step, 1)
                    n = 6 if ph == 0 else 1
                    base = 0 if ph == 0 else 6 * GROUPS
                    dve.wait_ge(s.bias_step, g.times(n, base + n + done[0]))

                if ph == 0:
                    q = qmask[:, bass.ds(g.times(GB, GB), GB)].unsqueeze(2).broadcast_to([P, GB, S])
                    link(V.tensor_tensor(o4, m4, q, ALU.mult))
                    link(V.tensor_scalar(o, o, -1.0, 1.0, ALU.mult, ALU.add))
                    link(V.tensor_scalar(o, o, -1.0, None, ALU.add))
                    link(V.tensor_tensor(o, o, o, ALU.mult))
                    link(V.tensor_scalar(o, o, MASK_TOL ** 2, NEG, ALU.is_le, ALU.mult))
                    link(V.tensor_reduce(vmx[:, p, :], o4, AX_X, ALU.max))
                    V.tensor_scalar(valid[:, p, :], vmx[:, p, :], NEG / 2, None, ALU.is_ge).then_inc(s.bias_ready, 1)
                else:
                    link(V.tensor_scalar(o, m.bitcast(I32), 0.0, NEG, ALU.is_equal, ALU.mult))
                    V.tensor_tensor(o4, o4, causal[:, :].unsqueeze(1).broadcast_to([P, GB, S]), ALU.add
                                    ).then_inc(s.bias_ready, 1)

            def out_low(ph, tile, p):
                if ph:
                    return
                dve.wait_ge(s.oh_ready, tile + 1)
                hi = oh[:, :, p * P:(p + 1) * P].bitcast(F32).rearrange("p h (b q) -> p b h q", b=2)
                V.tensor_tensor(ol[:, :, p * P:(p + 1) * P].rearrange("p h (b q) -> p b h q", b=2),
                                AO[:, :, :].rearrange("p b (h q) -> p b h q", h=HP), hi, ALU.subtract
                                ).then_inc(s.ol_ready, 1)

            def values(g, t):
                k = v_turn(0, g, 2 * t + 1)
                V.tensor_copy(v[:, (g.first + 1) % 2, t, 512:1024], take(k)).then_inc(free(k), 1)

            def place_values(g):
                k = v_turn(2, g, 0)
                i = take(k)
                for t in range(2):
                    ins = V.tensor_tensor(
                        v[:, (g.first + 1) % 2, 0, t * 512:(t + 1) * 512].rearrange("p (j d) -> p j d", j=4),
                        i[:, t * D:(t + 1) * D].unsqueeze(1).broadcast_to([P, 4, D]), vmask[:, :, :], ALU.mult)
                ins.then_inc(free(k), 1)

            def place_queries(g):
                dve.wait_ge(s.rope_done, g.times(2, 3))
                for j in range(8):
                    ins = V.tensor_scalar(qT[:, (g.first + 1) % 2, j, :], qr, headmask[:, j:j + 1], None, ALU.mult)
                ins.then_inc(s.qz_ready, 1)

            def attn_body(ph, g):
                f, n, a = g.first, ph // 2 * TILES, ph // 2 * GROUPS
                b = (f + 1) % 2
                if has_attn(f, "PTodd"):
                    sum_inverse(ph, g.times(2, n - 1), g.plus(-1), 1)
                if has_attn(f, "X"):
                    x_low(ph, g)
                    dve.wait_ge(s.ch_ready, g.times(1, a + 2))
                    V.tensor_tensor(cl[:, b, :], cst[:, b, :], ch[:, b, :].bitcast(F32), ALU.subtract
                                    ).then_inc(s.cl_ready, 1)
                if has_attn(f, "ln"):
                    ln_stats(ph, g)
                if ph and has_route(f, "gates"):
                    route_stats(g)
                if has_attn(f, "S"):
                    mask_and_max(ph, g.times(2, n), g, 0)
                if has_attn(f, "X"):
                    if ph == 0:
                        for u in range(4):
                            k = qk_turn(0, g, 2 * u + 1)
                            V.tensor_copy(kT[:, b, 2 * u:2 * u + 2, :], take(k).rearrange("p (h t) -> p h t", h=2)
                                          ).then_inc(free(k), 1)
                    else:
                        if f >= 0:
                            dve.wait_ge(s.rope_done, g.times(2, 2))
                        for u in range(2):
                            k = qk_turn(ph, g, u)
                            i = take(k)
                            for r, tab in enumerate((ropec, ropes)):
                                ins = V.tensor_tensor(
                                    rope_t[:, 2 * u + r, :].rearrange("p (b k) -> p b k", b=GB),
                                    i[:, r * GT:(r + 1) * GT].rearrange("p (b k) -> p b k", b=GB),
                                    tab[:, :].unsqueeze(1).broadcast_to([P, GB, S]), ALU.mult)
                            ins.then_inc(free(k), 1)
                    masks(ph, g)
                if has_attn(f, "ln"):
                    ln_norm(ph, g)
                if ph and has_route(f, "gates"):
                    route_norm(g)
                if has_attn(f, "PTodd"):
                    out_low(ph, g.times(2, n - 1), 1)
                if has_attn(f, "S"):
                    sum_inverse(ph, g.times(2, n), g, 0)
                if has_attn(f, "Va"):
                    if ph == 0:
                        values(g, 0)
                    else:
                        place_values(g)
                        place_queries(g)
                if ph and has_route(f, "gates"):
                    route_low(g)
                if has_attn(f, "S"):
                    mask_and_max(ph, g.times(2, n + 1), g, 1)
                if has_attn(f, "Vb") and ph == 0:
                    values(g, 1)
                if has_attn(f, "tail"):
                    for u in range((2, 1)[ph // 2]):
                        k = turn_of(ph, g, "tail", u)
                        n_t = (1, 2)[ph // 2]
                        xg = xs[:, bass.ds(g.times(2, u - 2), n_t), :]
                        V.tensor_tensor(xg, take(k)[:, 0:n_t * D].rearrange("p (t d) -> p t d", t=n_t), xg, ALU.add
                                        ).then_inc(free(k), 1)
                if has_attn(f, "PTeven"):
                    out_low(ph, g.times(2, n), 0)
                if ph and has_route(f, "LR"):
                    route(g)
                for c in chunks_at(ph, f if g.reg is None else None):
                    split_low(c)

            def gate_top(ph, g):
                lay = ph // 2
                n0 = lay * GROUPS + 1
                k = turn_of(ph, g, "L")
                V.tensor_copy(lg[:], take(k)[:, 0:2 * E].rearrange("p (t e) -> p t e", t=2)
                              ).then_inc(free(k), 1)
                dve.wait_ge(free(k), k.earlier(1))
                dve.sem_inc(s.dve_waited, 1)
                step = gate_link(g, n0)
                for t in range(2):
                    ins = V.max(top[:, t, :], lg[:, t, :])
                step(ins)
                V.tensor_tensor(ex[:], lg[:], top[:, :, 0:1].broadcast_to([P, 2, E]), ALU.subtract
                                ).then_inc(s.gate_exp_in, 1)
                for t in range(2):
                    ins = V.max_index(topi[:, t, :], top[:, t, :], lg[:, t, :])
                step(ins)
                step(V.tensor_copy(topf[:], topi[:]))
                io = iota8[:, :].unsqueeze(1).broadcast_to([P, 2, E])
                V.tensor_tensor(sel0[:], io, topf[:, :, 0:1].broadcast_to([P, 2, E]), ALU.is_equal)
                step(V.tensor_tensor(sel1[:], io, topf[:, :, 1:2].broadcast_to([P, 2, E]), ALU.is_equal))
                step(V.tensor_tensor(sel0[:], sel0[:], sel1[:], ALU.add))
                return step

            def gate_weights(ph, g, step):
                lay = ph // 2
                dve.wait_ge(s.gate_exp, g.times(1, lay * GROUPS + 2))
                step(V.tensor_tensor(sel1[:], ex[:], sel0[:], ALU.mult))
                step(V.tensor_reduce(gs[:, :], (ex, sel1)[lay][:], AX_X, ALU.add))
                step(V.reciprocal(gr[:, :], gs[:, :]))
                V.scalar_tensor_tensor(out=wts[:, (g.first + 1) % 2, :, 0:E], in0=sel1[:], scalar=0.5,
                                       in1=gr[:, :].unsqueeze(2).broadcast_to([P, 2, E]),
                                       op0=ALU.mult, op1=ALU.mult).then_inc(s.w_ready, 1)

            GATE_STEPS = 8

            def gate_link(g, n0):
                done = [0]

                def step(ins):
                    done[0] += 1
                    ins.then_inc(s.gate_step, 1)
                    dve.wait_ge(s.gate_step, g.times(GATE_STEPS, n0 * GATE_STEPS + done[0]))
                return step

            def ffn_body(ph, g):
                f, lay = g.first, ph // 2
                cn, w = CHN0, CH0
                nj, m0 = 2 * cn, 0
                if has_ffn(f, "X"):
                    x_low(ph, g)
                    if f < 0:
                        gate_weights(ph, g, gate_top(ph, g))
                for j in range(nj):
                    t, c = j // cn, j % cn
                    if has_ffn(f, "T0"):
                        m = g.times(nj, m0 + j)
                        gate, y, u, h = GY[:, j % 2, 0:w], GY[:, j % 2, 512:512 + w], ub[:, j % 2, 0:w], hbuf[:, j % 4, 0:w]
                        if j == 0:
                            dve.wait_ge(s.w_ready, g.times(1, lay * GROUPS + 1))
                        dve.wait_ge(s.tanh_ready, m + 1)
                        V.scalar_tensor_tensor(out=u, in0=th[:, j % 2, 0:w], scalar=1.0, in1=gate,
                                               op0=ALU.add, op1=ALU.mult).then_inc(s.gated, 1)
                        dve.wait_ge(s.gated, m + 1)
                        if not (lay == 0 and f == 0):
                            dve.wait_ge(s.out_done, m - 3)
                        for q in range(w // HID0 if lay == 0 else 1):
                            a, z = (q * HID0, (q + 1) * HID0) if lay == 0 else (0, w)
                            e = c * 5 + q if lay == 0 else c
                            ins = V.scalar_tensor_tensor(out=h[:, a:z], in0=y[:, a:z],
                                                         scalar=wts[:, g.parity, t, e:e + 1], in1=u[:, a:z],
                                                         op0=ALU.mult, op1=ALU.mult)
                        ins.then_inc(s.h_ready, 1)
                    if (j == 1 and has_ffn(f, "Tp")) or (j == cn + 1 and has_ffn(f, "T0")):
                        tile = g.times(2, -1 if j == 1 else 0)
                        dve.wait_ge(s.out_done, g.times(nj, m0 + (0 if j == 1 else cn)))
                        xt = xs[:, bass.ds(tile, 1), :].rearrange("p a d -> p (a d)")
                        V.tensor_tensor(xt, AO[:, 1 if j == 1 else 0, 0:D], xt, ALU.add).then_inc(s.x_added, 1)
                    if f >= 0 and has_ffn(f, "X") and j == 1:
                        step = gate_top(ph, g)
                    if f >= 0 and has_ffn(f, "X") and j == 2:
                        gate_weights(ph, g, step)
                    if has_ffn(f, "ln") and j == 0:
                        ln_stats(ph, g)
                    if has_ffn(f, "ln") and j == 1:
                        ln_norm(ph, g)

            PLACE_STEPS, ROUTE_STEPS = 2, 8

            def route_link(counter, steps, g, ahead):
                done = [0]

                def step(ins):
                    done[0] += 1
                    ins.then_inc(counter, 1)
                    dve.wait_ge(counter, g.times(steps, ahead * steps + done[0]))
                return step, done

            def route_stats(g):
                for t in range(2):
                    V.bn_stats(stats_r[:, t, :], xs[:, bass.ds(g.times(2, t - 4), 1), :].rearrange("p a d -> p (a d)")
                               ).then_inc(s.r_bn_done, 1)
                dve.wait_ge(s.r_bn_done, g.times(2, -2))
                dve.sem_inc(s.dve_waited, 1)
                V.bn_aggr(mv_r[:, 0, :], stats_r[:, 0, :])
                V.bn_aggr(mv_r[:, 1, :], stats_r[:, 1, :]).then_inc(s.r_stats, 1)

            def route_norm(g):
                b = g.parity
                dve.wait_ge(s.r_rstd, g.times(1, -1))
                dve.wait_ge(s.r_stats, g.times(1, -1))
                if g.first >= 4:
                    dve.wait_ge(scattered[b], g.halved(-2) * 64)
                for t in range(2):
                    ins = V.tensor_scalar(rows[:, b, t, 0, 0:D],
                                          xs[:, bass.ds(g.times(2, t - 4), 1), :].rearrange("p a d -> p (a d)"),
                                          mv_r[:, t, 0:1], rstd_r[:, t:t + 1], ALU.subtract, ALU.mult)
                ins.then_inc(s.r_xn_ready, 1)

            def route_low(g):
                k = turn_of(2, g, "Xr")
                b = g.parity
                dve.wait_ge(s.r_xh_ready, g.times(1, -1))
                V.tensor_tensor(xl[:, b, :], take(k)[:, 0:GT], xh[:, b, :].bitcast(F32), ALU.subtract).then_inc(free(k), 1)

            def route(g):
                f = g.first
                k = turn_of(2, g, "LR")
                i = take(k)
                if has_route(f, "gates"):
                    ins = V.tensor_copy(lg[:], i[:, 0:2 * E].rearrange("p (t e) -> p t e", t=2))
                if has_route(f, "ranks"):
                    ins = V.tensor_tensor(rankb[:], i[:, 2 * E:4 * E].rearrange("p (t e) -> p t e", t=2),
                                          rc_first.unsqueeze(1).broadcast_to([P, 2, E]), ALU.add)
                ins.then_inc(free(k), 1)
                dve.wait_ge(free(k), k.earlier(1))
                if has_route(f, "ranks"):
                    step, done = route_link(s.place_step, PLACE_STEPS, g, -3)
                    step(V.tensor_tensor(prod[:], hot[:], rankb[:].unsqueeze(2).broadcast_to([P, 2, 2, E]), ALU.mult))
                    step(V.tensor_reduce(slotf[:], prod[:], AX_X, ALU.add))
                    V.tensor_copy(slot[:, 1 - g.parity, :], slotf[:].rearrange("p t k -> p (t k)")).then_inc(s.rows_ready, 1)
                    assert done[0] == PLACE_STEPS
                if has_route(f, "gates"):
                    b = g.parity
                    step, done = route_link(s.route_step, ROUTE_STEPS, g, -2)
                    dve.sem_inc(s.dve_waited, 1)
                    for t in range(2):
                        ins = V.max(top[:, t, :], lg[:, t, :])
                    step(ins)
                    V.tensor_tensor(ex2[:], top[:, :, 0:2], top[:, :, 0:1].broadcast_to([P, 2, 2]), ALU.subtract
                                    ).then_inc(s.route_exp_in, 1)
                    for t in range(2):
                        ins = V.max_index(topi[:, t, :], top[:, t, :], lg[:, t, :])
                    step(ins)
                    step(V.tensor_copy(topf[:], topi[:]))
                    step(V.tensor_tensor(hot[:], iota8[:, :].unsqueeze(1).unsqueeze(1).broadcast_to([P, 2, 2, E]),
                                         topf[:, :, 0:2].unsqueeze(3).broadcast_to([P, 2, 2, E]), ALU.is_equal))
                    step(V.tensor_tensor(both[:], hot[:, :, 0, :], hot[:, :, 1, :], ALU.add))
                    step(V.tensor_tensor(cum[:, b, 1, :], cum[:, 1 - b, 2, :], both[:, 0, :], ALU.add))
                    V.tensor_tensor(cum[:, b, 2, :], cum[:, b, 1, :], both[:, 1, :], ALU.add).then_inc(s.choices, 1)
                    V.tensor_copy(rows[:, b, :, :, D + 1],
                                  rc_number.rearrange("p (t k) -> p t k", k=2)[:, bass.ds(g.times(2, -4), 2), :])
                    dve.wait_ge(s.route_exp, g.times(1, -1))
                    step(V.tensor_reduce(gs[:, :], ex2[:], AX_X, ALU.add))
                    step(V.reciprocal(gr[:, :], gs[:, :]))
                    V.scalar_tensor_tensor(out=rows[:, b, :, :, D], in0=ex2[:], scalar=0.5,
                                           in1=gr[:, :].unsqueeze(2).broadcast_to([P, 2, 2]), op0=ALU.mult, op1=ALU.mult)
                    assert done[0] == ROUTE_STEPS

            def make_tables():
                done = [0]

                def step(ins):
                    done[0] += 1
                    ins.then_inc(s.table_step, 1)
                    dve.wait_ge(s.table_step, done[0])

                dve.wait_ge(s.counted, 1)
                step(V.tensor_copy(count[:], AO[:, 0, 0:E]))
                step(V.tensor_tensor(padf[:], count[:], rc_pad, ALU.add))
                V.tensor_copy(padi[:], padf[:]).then_inc(s.pads_ready, 1)
                c = cmp[:, 0:E * TILES].rearrange("p (e n) -> p e n", e=E)
                step(V.tensor_tensor(c, count[:].unsqueeze(2).broadcast_to([P, E, TILES]),
                                     rc_edge.unsqueeze(1).broadcast_to([P, E, TILES]), ALU.is_gt))
                step(V.tensor_reduce(ntile[:], c, AX_X, ALU.add))
                c = cmp[:, 0:E * E].rearrange("p (e n) -> p e n", e=E)
                step(V.tensor_tensor(c, rc_upto.rearrange("p (e n) -> p e n", e=E),
                                     ntile[:].unsqueeze(1).broadcast_to([P, E, E]), ALU.mult))
                step(V.tensor_reduce(cume[:], c, AX_X, ALU.add))
                step(V.tensor_scalar(last[:], cume[:, E - 1:E], -1.0, None, ALU.add))
                step(V.tensor_scalar(tj[:], rc_tile, last[:, 0:1], None, ALU.min))
                step(V.tensor_scalar(used[:], rc_tile, last[:, 0:1], None, ALU.is_le))
                step(V.tensor_scalar(alt[:], used[:], -1.0, 1.0, ALU.mult, ALU.add))
                step(V.tensor_tensor(alt[:], alt[:], rc_unused, ALU.mult))
                c = cmp[:, 0:NTAB * E].rearrange("p (n e) -> p n e", e=E)
                step(V.tensor_tensor(c, cume[:].unsqueeze(1).broadcast_to([P, NTAB, E]),
                                     tj[:].unsqueeze(2).broadcast_to([P, NTAB, E]), ALU.is_le))
                step(V.tensor_reduce(te[:], c, AX_X, ALU.add))
                step(V.tensor_tensor(c, c, ntile[:].unsqueeze(1).broadcast_to([P, NTAB, E]), ALU.mult))
                step(V.tensor_reduce(tb[:], c, AX_X, ALU.add))
                step(V.tensor_tensor(tb[:], tj[:], tb[:], ALU.subtract))
                step(V.tensor_scalar(tb[:], tb[:], float(P), None, ALU.mult))
                step(V.scalar_tensor_tensor(out=tb[:], in0=te[:], scalar=float(REG), in1=tb[:], op0=ALU.mult, op1=ALU.add))
                V.tensor_copy(tab_b[:], tb[:])
                V.tensor_copy(tab_e[:], te[:]).then_inc(s.tables, 1)

            def expert_body(j, _):
                f = j.first
                if has_expert(f, "Y"):
                    i = f - 3
                    dve.wait_ge(s.e_out, j.times(1, -2))
                    V.tensor_copy(yb[:, i % 4, :], AO[:, i % 2, 0:D]).then_inc(s.e_copied, 1)
                if has_expert(f, "X"):
                    k = EXPERT.turn(j, "X")
                    dve.wait_ge(s.row_high, j.times(1, 2))
                    V.tensor_tensor(xl[:, (f + 1) % 2, 0:P], take(k)[:, 0:P], xh[:, (f + 1) % 2, 0:P].bitcast(F32),
                                    ALU.subtract).then_inc(free(k), 1)
                if has_expert(f, "H"):
                    i = f - 1
                    if i >= 4:
                        dve.wait_ge(e_stored[i % 4], Turn(i, j.reg, j.per, 4).earlier() * 16)
                    V.tensor_scalar(idb[:, i % 4:i % 4 + 1], xt[:, i % 4, D + 1:D + 2], used[:, bass.ds(j.times(1, -1), 1)],
                                    alt[:, bass.ds(j.times(1, -1), 1)], ALU.mult, ALU.add).then_inc(s.e_numbered, 1)
                if has_expert(f, "U"):
                    dve.wait_ge(s.e_tanh, j.times(1, 1))
                    V.scalar_tensor_tensor(out=ub[:, f % 2, 0:CH1], in0=th[:, f % 2, 0:CH1], scalar=1.0,
                                           in1=GY[:, f % 2, 0:CH1], op0=ALU.add, op1=ALU.mult).then_inc(s.e_gated, 1)
                    dve.wait_ge(s.e_gated, j.times(1, 1))
                    if f >= 4:
                        dve.wait_ge(s.e_out, j.times(1, -3))
                    V.scalar_tensor_tensor(out=hbuf[:, f % 4, 0:CH1], in0=GY[:, f % 2, 512:512 + CH1],
                                           scalar=xt[:, f % 4, D:D + 1], in1=ub[:, f % 2, 0:CH1],
                                           op0=ALU.mult, op1=ALU.mult).then_inc(s.e_hidden, 1)

            def add_places():
                part = TILES // 4
                for c in range(4):
                    dve.wait_ge(y_in[c], 32)
                    for k in range(2):
                        xc = xs[:, c * part:(c + 1) * part, :]
                        V.tensor_tensor(xc, xc, yl[k][:, c * part:(c + 1) * part, :], ALU.add).then_inc(s.added, 1)
                        dve.wait_ge(s.added, 2 * c + k + 1)

            dve.sem_inc(s.x_added, 1)
            for c in range(2):
                split_low(c)
            dve.wait_ge(s.consts, 3 + E)
            dve.wait_ge(s.misc_in, MISC)
            for ph in phases:
                if ph == 1:
                    dve.wait_ge(s.later_in, LATER)
                if ph == 2:
                    V.memset(cum[:], 0.0)
                    V.memset(padr[:], 0.0).then_inc(s.pads_zero, 1)
                    dve.wait_ge(s.pads_zero, 1)
                    V.tensor_copy(padr[:, :, D + 1], rc_padnum).then_inc(s.pads_zero, 1)
                run_bodies(dve, -2, lambda g: (attn_body, ffn_body)[ph % 2](ph, g), ph)
            make_tables()
            run_tiles(dve, expert_body)
            add_places()

        @block.tensor
        def _(pe):
            T = nc.tensor

            def bank(k):
                if k.reg is not None or k.first >= k.banks:
                    pe.wait_ge(free(k), k.earlier())
                return ST[:, k.bank, :]

            def taken(k):
                pe.wait_ge(free(k), k.earlier(1))

            def waited():
                pe.sem_inc(s.pe_waited, 1)

            def split_product(o, wh, wl, mh, ml):
                T.matmul(o, wh, ml, start=True, stop=False)
                T.matmul(o, wh, mh, start=False, stop=False)
                return T.matmul(o, wl, mh, start=False, stop=True)

            def turn_x(ph, g):
                k = turn_of(ph, g, "X")
                o = bank(k)
                pe.wait_ge(s.xn_ready, g.times(1, ph * GROUPS + 2))
                for t in range(2):
                    ins = T.transpose(o[:, t * P:(t + 1) * P], xn[:, t, :], ident[:, :])
                ins.then_inc(full(k), 1)

            def project_qk(ph, g, turns):
                b = (g.first + 1) % 2
                for u in turns:
                    k = qk_turn(ph, g, u)
                    o = bank(k)
                    if u == 0:
                        taken(turn_of(ph, g, "X"))
                    if u == 1:
                        pe.wait_ge(s.cl_ready, g.times(1, ph // 2 * GROUPS + 2))
                    mh, ml = ((xh, xl), (ch, cl))[u % 2]
                    for r in range(2):
                        if ph == 0:
                            a, wh, wl = u % 2 * 1024 + (u // 2 * 2 + r) * P, big_h, big_l
                        else:
                            a, wh, wl = (2 * u + r) * P, sml_h, sml_l
                        ins = split_product(o[:, r * GT:(r + 1) * GT], wh[:, a:a + P], wl[:, a:a + P],
                                            mh[:, b, :], ml[:, b, :])
                    ins.then_inc(full(k), 1)

            def project_v(ph, g, tiles):
                b = (g.first + 1) % 2
                for t in tiles:
                    hi, lo = ch[:, b, t * P:(t + 1) * P], cl[:, b, t * P:(t + 1) * P]
                    if ph == 0:
                        for r in range(2):
                            k = v_turn(ph, g, 2 * t + r)
                            o = bank(k)
                            a = 2048 + r * 512
                            split_product(o, hi, lo, big_h[:, a:a + 512], big_l[:, a:a + 512]
                                          ).then_inc(full(k), 1)
                    else:
                        k = v_turn(ph, g, 0)
                        o = bank(k) if t == 0 else o
                        ins = split_product(o[:, t * D:(t + 1) * D], hi, lo, sml_h[:, 4 * D:5 * D], sml_l[:, 4 * D:5 * D])
                        if t:
                            ins.then_inc(full(k), 1)

            def scores(ph, g, t):
                b, lay = g.parity, ph // 2
                tile = g.times(2, lay * TILES + t)
                if not (ph == 0 and g.first == 0 and t == 0):
                    pe.wait_ge(s.masked, tile)
                if ph and t == 0:
                    pe.wait_ge(s.qz_ready, g.times(1, 1))
                    pe.wait_ge(s.rope_done, g.times(2, 2))
                waited()
                for i in range(HP):
                    for c in range(2):
                        for q in range(2):
                            tok = slice(t * P + c * S, t * P + (c + 1) * S)
                            if ph == 0:
                                hp, h2, row = i, q, q
                                lhsT, rhs = qT[row * 64:row * 64 + 64, b, hp, tok], kT[row * 64:row * 64 + 64, b, hp, tok]
                            else:
                                row, j = q, i
                                h = 8 * row + j
                                hp, h2 = h // 2, h % 2
                                lhsT, rhs = qT[row * 64:row * 64 + 64, b, j, tok], kT[row * 64:row * 64 + 64, b, 0, tok]
                            ins = T.matmul(SC[h2 * 64:h2 * 64 + 64, hp // 4, hp % 4 * P + c * S:hp % 4 * P + (c + 1) * S], lhsT, rhs,
                                           start=True, stop=True)
                ins.then_inc(s.scores, 1)

            def turn_probs(ph, g, part, grp, t):
                pe.wait_ge(s.probs, grp.times(2, ph // 2 * TILES + t + 1))
                for u in range(2):
                    k = turn_of(ph, g, part, u)
                    o = bank(k)
                    for i in range(4):
                        ins = T.transpose(o[:, i * P:(i + 1) * P], sm[:, t, 4 * u + i, :], ident[:, :])
                    ins.then_inc(full(k), 1)

            def weight_values(ph, g, part, grp, t):
                lay = ph // 2
                tile = grp.times(2, lay * TILES + t)
                b = grp.parity
                for u in range(2):
                    taken(turn_of(ph, g, part, u))
                if ph == 0:
                    if not (grp.first == 0 and grp.reg is None and t == 0):
                        pe.wait_ge(s.ol_ready, tile)
                    waited()
                    for hp in range(HP):
                        for h2 in range(2):
                            for c in range(2):
                                h = 2 * hp + h2
                                ins = T.matmul(AO[h2 * 64:h2 * 64 + 64, c, hp * S:(hp + 1) * S],
                                               v[c * S:c * S + S, b, t, h * 64:(h + 1) * 64],
                                               pT[c * S:c * S + S, t, hp, h2 * 64:h2 * 64 + 64], start=True, stop=True)
                else:
                    pe.wait_ge(s.oh_ready, tile)
                    waited()
                    for j in range(4):
                        for r in range(4):
                            for c in range(2):
                                h = 4 * r + j
                                ins = T.matmul(AO[32 * r:32 * r + 32, c, 0:S],
                                               v[c * S:c * S + S, b, 0, t * 512 + j * D + 32 * r:t * 512 + j * D + 32 * r + 32],
                                               pT[c * S:c * S + S, t, h // 2, h % 2 * 64:h % 2 * 64 + 64],
                                               start=(j == 0), stop=(j == 3))
                ins.then_inc(s.attn_out, 1)

            def project_out(ph, g):
                k = turn_of(ph, g, "Wo")
                o = bank(k)[:, 0:GT]
                if ph == 0:
                    pe.wait_ge(s.ol_ready, g.times(2, 0))
                    for hp in range(HP):
                        wh, wl = big_h[:, 3072 + hp * P:3072 + (hp + 1) * P], big_l[:, 3072 + hp * P:3072 + (hp + 1) * P]
                        T.matmul(o, wh, ol[:, hp, :], start=(hp == 0), stop=False)
                        T.matmul(o, wh, oh[:, hp, :], start=False, stop=False)
                        ins = T.matmul(o, wl, oh[:, hp, :], start=False, stop=(hp == HP - 1))
                else:
                    pe.wait_ge(s.oh_ready, g.times(2, TILES))
                    ins = T.matmul(o, wob_sb[:, :], oT1, start=True, stop=True)
                ins.then_inc(full(k), 1)

            def turn_back(ph, g):
                taken(turn_of(ph, g, "Wo"))
                for t in range(2):
                    if ph == 0 or t == 0:
                        k = turn_of(ph, g, "tail", t)
                        o = bank(k)
                    a = 0 if ph == 0 else t * P
                    ins = T.transpose(o[:, a:a + P], yT[:, t * P:(t + 1) * P], ident[:, :])
                    if ph == 0 or t == 1:
                        ins.then_inc(full(k), 1)

            def turn_rows(g):
                k = turn_of(2, g, "Xr")
                o = bank(k)
                pe.wait_ge(s.r_xn_ready, g.times(1, -1))
                for t in range(2):
                    ins = T.transpose(o[:, t * P:(t + 1) * P], rows[:, g.parity, t, 0, 0:D], ident[:, :])
                ins.then_inc(full(k), 1)

            def route(g):
                f, b = g.first, g.parity
                k = turn_of(2, g, "LR")
                o = bank(k)
                if has_route(f, "ranks"):
                    pe.wait_ge(s.choices, g.times(1, -2))
                    for t in range(2):
                        a = (2 + t) * E
                        T.matmul(o[:, a:a + E], rc_before, both[:, t, :], start=True, stop=False)
                        ins = T.matmul(o[:, a:a + E], rc_ones, cum[:, 1 - b, 1, :] if t else cum[:, b, 2, :],
                                       start=False, stop=True)
                if has_route(f, "gates"):
                    taken(turn_of(2, g, "Xr"))
                    a = 5 * D + E
                    for t in range(2):
                        ins = split_product(o[:, t * E:(t + 1) * E], xh[:, b, t * P:(t + 1) * P],
                                            xl[:, b, t * P:(t + 1) * P], sml_h[:, a:a + E], sml_l[:, a:a + E])
                ins.then_inc(full(k), 1)

            def attn_body(ph, g):
                f = g.first
                if has_attn(f, "X"):
                    turn_x(ph, g)
                if has_attn(f, "S"):
                    scores(ph, g, 0)
                if has_attn(f, "QKa"):
                    project_qk(ph, g, range((6, 2)[ph // 2]))
                if has_attn(f, "PTodd"):
                    turn_probs(ph, g, "PTodd", g.plus(-1), 1)
                if has_attn(f, "QKb") and ph == 0:
                    project_qk(ph, g, (6, 7))
                if has_attn(f, "Va") and ph:
                    project_v(ph, g, (0, 1))
                if has_attn(f, "PTodd"):
                    weight_values(ph, g, "PTodd", g.plus(-1), 1)
                if has_attn(f, "S"):
                    scores(ph, g, 1)
                if ph and has_route(f, "gates"):
                    turn_rows(g)
                if has_attn(f, "Va") and ph == 0:
                    project_v(ph, g, (0,))
                if has_attn(f, "Wo"):
                    project_out(ph, g)
                if has_attn(f, "Vb") and ph == 0:
                    project_v(ph, g, (1,))
                if has_attn(f, "PTeven"):
                    turn_probs(ph, g, "PTeven", g, 0)
                if has_attn(f, "tail"):
                    turn_back(ph, g)
                if ph and has_route(f, "LR"):
                    route(g)
                if has_attn(f, "PTeven"):
                    weight_values(ph, g, "PTeven", g, 0)

            def logits(ph, g):
                k = turn_of(ph, g, "L")
                o = bank(k)
                taken(turn_of(ph, g, "X"))
                b, a = (g.first + 1) % 2, 5 * D + ph // 2 * E
                for t in range(2):
                    ins = split_product(o[:, t * E:(t + 1) * E], xh[:, b, t * P:(t + 1) * P], xl[:, b, t * P:(t + 1) * P],
                                        sml_h[:, a:a + E], sml_l[:, a:a + E])
                ins.then_inc(full(k), 1)

            def ffn_body(ph, g):
                f, lay = g.first, ph // 2
                cn, w, bl, bn = CHN0, CH0, BL0, BN0
                wh, wl, w2 = mid_h, mid_l, w2a
                nj, m0 = 2 * cn, 0
                if has_ffn(f, "X"):
                    turn_x(ph, g)
                    if f < 0:
                        logits(ph, g)
                for j in range(nj):
                    t, c = j // cn, j % cn
                    if has_ffn(f, "T0"):
                        if not (lay == 0 and f == 0 and j < 2):
                            pe.wait_ge(s.h_ready, g.times(nj, m0 + j - 1))
                        b = g.parity
                        hi, lo = xh[:, b, t * P:(t + 1) * P], xl[:, b, t * P:(t + 1) * P]
                        for r in range(2):
                            a = r * cn * w + c * w
                            ins = split_product(GY[:, j % 2, r * 512:r * 512 + w], hi, lo, wh[:, a:a + w], wl[:, a:a + w])
                        ins.then_inc(s.gy_ready, 1)
                    if has_ffn(f, "Tp" if j == 0 else "T0"):
                        k = (turn_of(ph, g, "Tp") if j == 0 else turn_of(ph, g, "T0") if j == 1
                             else turn_of(ph, g, "T", j - 2))
                        o = bank(k)
                        pe.wait_ge(s.h_ready, g.times(nj, m0 + j))
                        for q in range(bn):
                            ins = T.transpose(o[0:bl, q * P:(q + 1) * P], hbuf[:, (j - 1) % 4, q * bl:(q + 1) * bl], ident[:, :])
                        ins.then_inc(full(k), 1)
                    if has_ffn(f, "Tp" if j < 2 else "T0"):
                        k = (turn_of(ph, g, "X", -1) if j == 0 else turn_of(ph, g, "Tp") if j == 1
                             else turn_of(ph, g, "T0") if j == 2 else turn_of(ph, g, "T", j - 3))
                        taken(k)
                        jj = (j - 2) % nj
                        tt, cc = jj // cn, jj % cn
                        if cc == 0 and not (lay == 0 and f == 0 and j >= 2):
                            pe.wait_ge(s.x_added, g.times(2, lay * TILES + tt - (2 if j < 2 else 0)))
                        for q in range(bn):
                            ins = T.matmul(AO[:, tt, 0:D], hT[0:bl, jj % 2, q * P:(q + 1) * P], w2[0:bl, cc * bn + q, :],
                                           start=(cc == 0 and q == 0), stop=(cc == cn - 1 and q == bn - 1))
                        ins.then_inc(s.out_done, 1)
                    if f >= 0 and j == 1 and has_ffn(f, "L"):
                        logits(ph, g)

            pe.wait_ge(s.consts, 3 + E)
            pe.wait_ge(s.w_split, 4)
            for ph in phases:
                if ph == 1:
                    pe.wait_ge(s.w_split, 7)
                    pe.wait_ge(s.later_in, LATER)
                run_bodies(pe, -2, lambda g: (attn_body, ffn_body)[ph % 2](ph, g), ph)

            def expert_body(j, expert):
                f = j.first
                if has_expert(f, "X"):
                    k = EXPERT.turn(j, "X")
                    o = bank(k)
                    b = (f + 1) % 4
                    pe.wait_ge(row_in[b], Turn(f + 1, j.reg, j.per, 4).earlier(1) * 16)
                    T.transpose(o[:, 0:P], xt[:, b, 0:D], ident[:, :]).then_inc(full(k), 1)
                if has_expert(f, "U"):
                    taken(EXPERT.turn(j.plus(-1), "X"))
                    if f >= 2:
                        pe.wait_ge(s.e_hidden, j.times(1, -1))
                    hi, lo = xh[:, f % 2, 0:P], xl[:, f % 2, 0:P]
                    e = expert(j)
                    for r in range(2):
                        wh, wl = (w[:, bass.ds(e * CH1 + r * E * CH1, CH1)] for w in (big_h, big_l))
                        ins = split_product(GY[:, f % 2, r * 512:r * 512 + CH1], hi, lo, wh, wl)
                    ins.then_inc(s.e_products, 1)
                if has_expert(f, "H"):
                    k = EXPERT.turn(j, "H")
                    o = bank(k)
                    pe.wait_ge(s.e_hidden, j.times(1))
                    for q in range(BN1):
                        ins = T.transpose(o[0:BL1, q * P:(q + 1) * P], hbuf[:, (f - 1) % 4, q * BL1:(q + 1) * BL1], ident[:, :])
                    ins.then_inc(full(k), 1)
                if has_expert(f, "O"):
                    taken(EXPERT.turn(j.plus(-1), "H"))
                    if f >= 4:
                        pe.wait_ge(s.e_copied, j.times(1, -3))
                    e = expert(j.plus(-2))
                    for q in range(BN1):
                        w = w2b[0:BL1, bass.ds(e * BN1 + q, 1), :].rearrange("p a d -> p (a d)")
                        ins = T.matmul(AO[:, f % 2, 0:D], hT[0:BL1, f % 2, q * P:(q + 1) * P], w,
                                       start=(q == 0), stop=(q == BN1 - 1))
                    ins.then_inc(s.e_out, 1)

            def experts(tile, n):
                _, r = nc.values_load_multi_w_load_instructions(
                    tab_e[0:1, bass.ds(tile.times(1), n)], engines=[mybir.EngineType.PE], min_val=0,
                    max_val=E - 1, skip_runtime_bounds_check_because="the table holds numbers of experts")
                return r

            pe.wait_ge(s.w_split, 13)
            pe.wait_ge(s.choices, GROUPS)
            T.matmul(AO[:, 0, 0:E], rc_ones, cum[:, (GROUPS - 1) % 2, 2, :], start=True, stop=True).then_inc(s.counted, 1)
            pe.wait_ge(s.tables, 1)
            run_tiles(pe, expert_body, experts)


NAMES = ("x ctx_1024 mask_BxS2_fk1 mask_BxS2_if1 L0_xattn_Wq L0_xattn_Wkv L0_xattn_Wo L0_xattn_bo L0_ffn_gate_w "
         "L0_ffn_W1 L0_ffn_W2 L0_ffn_Ws1 L0_ffn_Ws2 L1_xattn_Wq L1_xattn_Wk L1_xattn_Wv L1_xattn_Wo L1_xattn_bo "
         "L1_ffn_Wg L1_ffn_W1 L1_ffn_W2 L1_ffn_W3").split()


def rope_tables():
    theta = np.float32(1.0) / np.float32(10000.0) ** (np.arange(0, DH1, 2, dtype=np.float32) / np.float32(DH1))
    angle = np.arange(S, dtype=np.float32)[None, :] * theta.astype(np.float32)[:, None]
    cos = np.repeat(np.cos(angle), 2, axis=0)
    sin = np.repeat(np.sin(angle), 2, axis=0) * np.tile(np.array([-1.0, 1.0], np.float32), DH1 // 2)[:, None]
    return np.tile(cos, (HEADS, 1)).astype(np.float32), np.tile(sin, (HEADS, 1)).astype(np.float32)


def route_constants():
    p, e, j = np.arange(P)[:, None], np.arange(E)[None, :], np.arange(NTAB)[None, :]
    number = (np.arange(TILES)[None, :, None] * P + np.arange(2)[None, None, :] * TOK + p[:, :, None]).reshape(P, -1)
    parts = [number, e * REG, e * REG + p, PADS + e * P + p, np.arange(TILES)[None, :] * P,
             np.tril(np.ones((E, E))).reshape(1, -1), j, UNUSED + np.maximum(j - 2 * TOK // P, 0) * P + p,
             p < np.arange(P)[None, :], np.ones((1, P))]
    return np.concatenate([np.broadcast_to(t, (P, t.shape[1])) for t in parts], axis=1).astype(np.float32)


def layouts(a):
    def blocks(w, n, rows):
        return w.reshape(n, rows, D).transpose(1, 0, 2)

    swap = np.arange(D) ^ 1
    y0, g0 = a["L0_ffn_W1"][:, :HID0], a["L0_ffn_W1"][:, HID0:]
    ys, gs = a["L0_ffn_Ws1"][:2 * HID0], a["L0_ffn_Ws1"][2 * HID0:]
    wfa = np.concatenate([g0.reshape(-1, D), gs, y0.reshape(-1, D), ys]).T
    wfo = np.concatenate([a["L0_ffn_W2"].transpose(0, 2, 1).reshape(-1, D), a["L0_ffn_Ws2"].T])
    pad = ((0, 0), (0, PAD1 - HID1), (0, 0))
    wfb = np.concatenate([np.pad(a["L1_ffn_W1"], pad).reshape(-1, D), np.pad(a["L1_ffn_W2"], pad).reshape(-1, D)]).T
    wfbo = np.pad(a["L1_ffn_W3"].transpose(0, 2, 1), pad).reshape(-1, D)
    q1, k1 = a["L1_xattn_Wq"], a["L1_xattn_Wk"]
    cos, sin = rope_tables()
    dims, place = np.arange(D), np.arange(4)
    hm = (dims[:, None] // DH1 % 8 == np.arange(8)[None, :]).astype(np.float32)
    vm = np.broadcast_to(dims[None, None, :] // DH1 % 4 == place[None, :, None], (P, 4, D)).astype(np.float32)
    cz = np.where(np.arange(S)[None, :] > np.arange(P)[:, None] % S, np.float32(NEG), np.float32(0.0))
    return {
        "x": a["x"].reshape(TOK, D), "ctxT": a["ctx_1024"].reshape(TOK, D).T, "maskT": a["mask_BxS2_fk1"].T,
        "mask_rows": a["mask_BxS2_fk1"].reshape(1, TOK), "imask_rows": a["mask_BxS2_if1"].reshape(1, TOK),
        "wa": np.concatenate([a["L0_xattn_Wq"], a["L0_xattn_Wkv"]], axis=1),
        "woa": blocks(a["L0_xattn_Wo"], HP, P).reshape(P, HP * D), "boa": a["L0_xattn_bo"].reshape(D, 1),
        "wfa": wfa, "wfo": blocks(wfo, CHN0 * BN0, BL0),
        "wbg": np.concatenate([q1.T, q1[swap].T, a["L1_xattn_Wk"].T, k1[swap].T, a["L1_xattn_Wv"].T,
                               a["L0_ffn_gate_w"].T, a["L1_ffn_Wg"].T], axis=1),
        "wob": a["L1_xattn_Wo"].T, "bob": a["L1_xattn_bo"].reshape(D, 1),
        "wfb": wfb, "wfbo": blocks(wfbo, E * BN1, BL1), "cosT": cos, "sinT": sin, "hm": hm, "vm": vm, "cz": cz,
        "rc": route_constants(),
    }


UPTO = 4


def kernel(**inputs):
    import concourse.bacc as _bacc
    from concourse.bass_utils import run_bass_kernel_spmd as _run

    nc = _bacc.Bacc("TRN2", target_bir_lowering=False, num_devices=1)
    arrays, args = {}, {}
    for name, a in layouts({n: np.asarray(inputs[n]) for n in NAMES}).items():
        arrays[f"in_{name}"] = np.ascontiguousarray(a)
        args[name] = nc.dram_tensor(f"in_{name}", a.shape, mybir.dt.from_np(a.dtype), kind="ExternalInput").ap()
    out = nc.dram_tensor("out_0", (TOK, D), F32, kind="ExternalOutput").ap()
    rows_d = nc.dram_tensor("rows_d", (E * REG, ROW), F32, kind="Internal").ap()
    y_d = nc.dram_tensor("y_d", (YROWS, D), F32, kind="Internal").ap()
    build(nc, **args, rows_d=rows_d, y_d=y_d, out=out, upto=UPTO)
    r = _run(nc, [arrays], core_ids=[0])
    return r.results[0]["out_0"].reshape(B, S, D)
```

```python
from contextlib import ExitStack

import numpy as np

import concourse.bass as bass
from concourse import mybir

F32 = mybir.dt.float32
F32R = mybir.dt.float32r
I32 = mybir.dt.int32
U32 = mybir.dt.uint32
ALU = mybir.AluOpType
ACT = mybir.ActivationFunctionType
AX_X = mybir.AxisListType.X

P = 128
B, S, D = 64, 64, 128
TOK = B * S
TILES = TOK // P
GROUPS = TILES // 2
GT = 2 * P
GB = GT // S
HEADS = 16
HP = HEADS // 2
DH0 = 64
INNER = HEADS * DH0
DH1 = D // HEADS
E = 8
HID0 = 96
E0 = E + 2
HID1 = 341
PAD1 = 342
CH0, CHN0 = 5 * HID0, 2
CH1 = PAD1
BL0, BN0 = CH0 // 4, 4
BL1, BN1 = CH1 // 3, 3
REG = TOK + P
NT = 2 * TOK // P + E - 1
ROW = D + 2
NTAB = NT + 1
PADS = 2 * TOK
UNUSED = PADS + E * P
YROWS = UNUSED + (NT - 2 * TOK // P) * P
EPS = 1e-5
NEG = -1e30
MASK_TOL = 1e-8 + 1e-5


class Step:

    def __init__(self, first, reg=None, per=0):
        self.first, self.reg, self.per = first, reg, per

    def times(self, m, add=0):
        c = self.first * m + add
        return c if self.reg is None or not self.per * m else self.reg * (self.per * m) + c

    def plus(self, n):
        return Step(self.first + n, self.reg, self.per)

    def halved(self, add=0):
        c = (self.first + add) // 2
        return c if self.reg is None else self.reg * (self.per // 2) + c

    @property
    def parity(self):
        return self.first % 2


class Turn(Step):

    def __init__(self, first, reg, per, banks):
        Step.__init__(self, first, reg, per)
        self.banks = banks
        self.bank = first % banks

    def earlier(self, add=0):
        c = self.first // self.banks + add
        return c if self.reg is None else self.reg * (self.per // self.banks) + c


class Slots:

    def __init__(self, base, sizes, has, first_body, last_body, banks):
        self.sizes, self.has, self.banks, self.before = sizes, has, banks, {}
        for g in range(first_body, last_body + 1):
            self.before[g] = base
            base += sum(n for k, n in sizes if has(g, k))
        self.end = base
        self.per_body = sum(n for _, n in sizes)
        assert 2 * self.per_body % banks == 0

    def turn(self, g, part, n=0):
        k = self.before[g.first] + n
        for name, size in self.sizes:
            if name == part:
                break
            if self.has(g.first, name):
                k += size
        return Turn(k, g.reg, self.per_body * g.per, self.banks)


def has_attn(g, part):
    return {"ln": 0 <= g + 2 < GROUPS, "X": 0 <= g + 1 < GROUPS, "QKa": 0 <= g + 1 < GROUPS,
            "QKb": 0 <= g + 1 < GROUPS, "Va": 0 <= g + 1 < GROUPS, "Vb": 0 <= g + 1 < GROUPS,
            "S": 0 <= g < GROUPS, "PTodd": 1 <= g <= GROUPS, "Wo": 1 <= g <= GROUPS, "tail": 1 <= g <= GROUPS, "PTeven": 0 <= g < GROUPS}[part]


def has_ffn(g, part):
    return {"ln": 0 <= g + 2 < GROUPS, "X": 0 <= g + 1 < GROUPS, "Tp": 1 <= g <= GROUPS,
            "T0": 0 <= g < GROUPS, "L": 0 <= g + 1 < GROUPS, "T": 0 <= g < GROUPS}[part]


def has_route(g, part):
    gates, ranks, places = 0 <= g - 2 < GROUPS, 0 <= g - 3 < GROUPS, 0 <= g - 4 < GROUPS
    return {"gates": gates, "ranks": ranks, "places": places, "Xr": gates, "LR": gates or ranks}[part]


def has_attn_route(g, part):
    return has_route(g, part) if part in ("Xr", "LR") else has_attn(g, part)


def has_expert(j, part):
    return {"X": 0 <= j + 1 < NT, "U": 0 <= j < NT, "H": 0 <= j - 1 < NT, "O": 0 <= j - 2 < NT,
            "Y": 0 <= j - 3 < NT}[part]


RING = (4, 2)
LAST_BODY = (GROUPS, GROUPS, GROUPS + 3)
LOOPS = ((1, 6, 2), (1, 6, 2), (6, 2, 4))
SLOTS = []
for _ph in range(3):
    _lay = _ph // 2
    if _ph % 2 == 0:
        _sizes = [("X", 1), ("QKa", (6, 2)[_lay]), ("PTodd", 2), ("QKb", (2, 0)[_lay]), ("Va", (2, 1)[_lay]),
                  ("Wo", 1), ("PTeven", 2), ("Vb", (2, 0)[_lay]), ("Xr", _lay), ("tail", (2, 1)[_lay]), ("LR", _lay)]
    else:
        _sizes = [("X", 1), ("Tp", 1), ("L", 1), ("T0", 1), ("T", 2 * CHN0 - 2)]
    SLOTS.append(Slots(SLOTS[_ph - 2].end if _lay else 0, _sizes, (has_attn_route, has_ffn)[_ph % 2], -2,
                       LAST_BODY[_ph], RING[_ph % 2]))
EXPERT = Slots(SLOTS[1].end, [("X", 1), ("H", 1)], has_expert, -1, NT + 2, RING[1])

TILE_FIRST, TILE_UNROLL = 5, 8
TILE_TURNS = (NT - 1 - TILE_FIRST) // TILE_UNROLL
TILE_END = TILE_FIRST + TILE_TURNS * TILE_UNROLL


def run_bodies(eng, first, body, ph):
    start, turns, unroll = LOOPS[ph]
    for g in range(first, start):
        body(Step(g))
    with eng.Fori(0, turns) as i:
        for p in range(unroll):
            body(Step(start + p, i, unroll))
    for g in range(start + turns * unroll, LAST_BODY[ph] + 1):
        if g == LAST_BODY[ph] and ph < 2 and first < 0:
            body(Step(-2), ph + 1)
        body(Step(g))


def run_tiles(eng, body, load=None):
    def values(tile, n):
        v = load(tile, n) if load else None
        return lambda t: v[t.first - tile.first]

    def straight(bodies, lo, n):
        v = values(Step(lo), n)
        for j in bodies:
            body(Step(j), v)

    straight(range(-1, TILE_FIRST), 0, TILE_FIRST)
    with eng.Fori(0, TILE_TURNS) as i:
        v = values(Step(TILE_FIRST - 2, i, TILE_UNROLL), TILE_UNROLL + 2)
        for p in range(TILE_UNROLL):
            body(Step(TILE_FIRST + p, i, TILE_UNROLL), v)
    straight(range(TILE_END, NT + 3), TILE_END - 2, NT - TILE_END + 2)


RC_SIZES = (2 * TILES, E, E, E, TILES, E * E, NTAB, NTAB, P, P)
RC_AT = [sum(RC_SIZES[:i]) for i in range(len(RC_SIZES))]
RC_END = sum(RC_SIZES)


def build(nc, x, ctxT, maskT, mask_rows, imask_rows, wa, woa, boa, wfa, wfo,
          wbg, wob, bob, wfb, wfbo, cosT, sinT, hm, vm, cz, rc, rows_d, y_d, out):
    phases = range(3)
    with ExitStack() as ctx:
        def sb(name, shape, dt=F32):
            return ctx.enter_context(nc.sbuf_tensor(name, shape, dt))

        def ps(name, shape):
            return ctx.enter_context(nc.psum_tensor(name, shape, F32))

        def sem(name):
            return ctx.enter_context(nc.semaphore(name))

        xs = sb("xs", [P, TILES, D])
        ident = sb("ident", [P, P])
        causal = sb("causal", [P, S])
        headmask = sb("headmask", [P, 8])
        vmask = sb("vmask", [P, 4, D])
        iota8 = sb("iota8", [P, E])
        mhalf = sb("mhalf", [P, 2])
        qmask = sb("qmask", [P, B])
        bo = [sb("bo0", [P, 1]), sb("bo1", [P, 1])]
        ropec = sb("ropec", [P, S])
        ropes = sb("ropes", [P, S])
        big_h = sb("big_h", [P, 2 * E * PAD1], F32R)
        big_l = sb("big_l", [P, 2 * E * PAD1], F32R)
        mid_h = sb("mid_h", [P, 2 * E0 * HID0], F32R)
        mid_l = sb("mid_l", [P, 2 * E0 * HID0], F32R)
        sml_h = sb("sml_h", [P, 5 * D + 2 * E], F32R)
        sml_l = sb("sml_l", [P, 5 * D + 2 * E], F32R)
        wob_sb = sb("wob_sb", [P, D])
        w2a = sb("w2a", [BL0, CHN0 * BN0, D])
        w2b = sb("w2b", [BL1, E * BN1, D])
        wst = sb("wst", [P, 2, 1024])
        xn = sb("xn", [P, 2, D])
        stats = sb("stats", [P, 2, 6])
        mv = sb("mv", [P, 2, 2])
        var = sb("var", [P, 2])
        rstd = sb("rstd", [P, 2])
        xh = sb("xh", [P, 2, GT], F32R)
        xl = sb("xl", [P, 2, GT], F32R)
        cst = sb("cst", [P, 2, GT])
        ch = sb("ch", [P, 2, GT], F32R)
        cl = sb("cl", [P, 2, GT], F32R)
        qT = sb("qT", [P, 2, HP, GT])
        kT = sb("kT", [P, 2, HP, GT])
        v = sb("v", [P, 2, 2, INNER])
        sm = sb("sm", [P, 2, HP, P])
        pT = sb("pT", [P, 2, HP, P])
        mx = sb("mx", [P, 2, HEADS])
        sums = sb("sums", [P, 2, HEADS])
        rinv = sb("rinv", [P, 2, HEADS])
        mrow = sb("mrow", [P, 2, GT])
        bias = sb("bias", [P, 2, GT])
        vmx = sb("vmx", [P, 2, GB])
        valid = sb("valid", [P, 2, GB])
        oh = sb("oh", [P, HP, GT], F32R)
        ol = sb("ol", [P, HP, GT], F32R)
        yT = sb("yT", [P, GT])
        lg = sb("lg", [P, 2, E])
        top = sb("top", [P, 2, E])
        topi = sb("topi", [P, 2, E], U32)
        topf = sb("topf", [P, 2, E])
        rcs = sb("rcs", [P, RC_END])
        stats_r = sb("stats_r", [P, 2, 6])
        mv_r = sb("mv_r", [P, 2, 2])
        var_r = sb("var_r", [P, 2])
        rstd_r = sb("rstd_r", [P, 2])
        ex2 = sb("ex2", [P, 2, 2])
        hot = sb("hot", [P, 2, 2, E])
        both = sb("both", [P, 2, E])
        cum = sb("cum", [P, 2, 2, E])
        rankb = sb("rankb", [P, 2, E])
        prod = sb("prod", [P, 2, 2, E])
        slotf = sb("slotf", [P, 2, 2])
        slot = sb("slot", [P, 4, 4], I32)
        count = sb("count", [P, E])
        padf = sb("padf", [P, E])
        padi = sb("padi", [P, E], I32)
        ntile = sb("ntile", [P, E])
        cume = sb("cume", [P, E])
        last = sb("last", [P, 1])
        idb = sb("idb", [P, 4], I32)
        sel0 = sb("sel0", [P, 2, E])
        sel1 = sb("sel1", [P, 2, E])
        ex = sb("ex", [P, 2, E])
        gs = sb("gs", [P, 2])
        gr = sb("gr", [P, 2])
        wts = sb("wts", [P, 2, 2, E0])
        rope_t = v[:, 0, 1, :].rearrange("p (n t) -> p n t", n=4)
        qr = v[:, 1, 1, 0:GT]
        oT1 = v[:, 1, 1, GT:2 * GT]
        hbuf = sm[:].rearrange("p a h q -> p (a h q)")[:, 0:4 * CH0].rearrange("p (n c) -> p n c", n=4)
        flat = pT[:].rearrange("p a h q -> p (a h q)")
        th = flat[:, 0:2 * CH0].rearrange("p (n c) -> p n c", n=2)
        ub = kT[:, 0].rearrange("p h t -> p (h t)")[:, 0:2 * CH0].rearrange("p (n c) -> p n c", n=2)
        lgt = yT[0:E, :]
        vf = v[:].rearrange("p a b c -> p (a b c)")
        rows = kT[:].rearrange("p a h t -> p a (h t)")[:, :, GT:GT + 8 * ROW].rearrange(
            "p a (b t k c) -> p a b t k c", b=2, t=2, k=2)
        xt = vf[:, 8 * ROW:12 * ROW].rearrange("p (n c) -> p n c", n=4)
        yb = vf[:, 12 * ROW:12 * ROW + 4 * D].rearrange("p (n c) -> p n c", n=4)
        padr = vf[:, 12 * ROW + 4 * D:20 * ROW + 4 * D].rearrange("p (e c) -> p e c", e=E)
        cmp = flat[:, 2 * CH0:2 * CH0 + NTAB * (E + 7)]
        tj, te, tb, used, alt, tab_e, tab_b = (cmp[:, NTAB * (E + i):NTAB * (E + i + 1)] for i in range(7))
        tab_e, tab_b = tab_e.bitcast(I32), tab_b.bitcast(I32)
        yl = [t[:].rearrange("p a h t -> p (a h t)").rearrange("p (n c) -> p n c", n=TILES) for t in (qT, kT)]
        hT = qT[:, 0].rearrange("p h t -> p (h t)")[:, 0:1024].rearrange("p (n c) -> p n c", n=2)

        (rc_number, rc_first, rc_pad, rc_padnum, rc_edge, rc_upto, rc_tile, rc_unused, rc_before, rc_ones) = (
            rcs[:, a:a + n] for a, n in zip(RC_AT, RC_SIZES))

        banks = ps("banks", [P, 8, 512])
        ST = banks[:, 0:4, :]
        SC = banks[:, 4:6, :]
        GY = banks[:, 2:6, :].rearrange("p (j r) c -> p j (r c)", j=2)
        AO = banks[:, 6:8, :]

        class Sems:
            pass
        s = Sems()
        s.x_first = sem("x_first")
        s.x_rest = sem("x_rest")
        s.w_landed0 = sem("w_landed0")
        s.w_landed1 = sem("w_landed1")
        s.w_high = sem("w_high")
        s.w_split = sem("w_split")
        s.consts = sem("consts")
        s.misc_in = sem("misc_in")
        s.later_in = sem("later_in")
        s.fixed = sem("fixed")
        s.bn_done = sem("bn_done")
        s.ln_stats = sem("ln_stats")
        s.var_ready = sem("var_ready")
        s.rstd_ready = sem("rstd_ready")
        s.xn_ready = sem("xn_ready")
        s.xh_ready = sem("xh_ready")
        s.ctx_in0 = sem("ctx_in0")
        s.ctx_in1 = sem("ctx_in1")
        s.ch_ready = sem("ch_ready")
        s.cl_ready = sem("cl_ready")
        s.mrow_in0 = sem("mrow_in0")
        s.mrow_in1 = sem("mrow_in1")
        s.bias_step = sem("bias_step")
        s.bias_ready = sem("bias_ready")
        s.scores = sem("scores")
        s.masked = sem("masked")
        s.maxed = sem("maxed")
        s.centred = sem("centred")
        s.expd = sem("expd")
        s.summed = sem("summed")
        s.inverted = sem("inverted")
        s.sum_ready = sem("sum_ready")
        s.probs = sem("probs")
        s.attn_out = sem("attn_out")
        s.oh_ready = sem("oh_ready")
        s.ol_ready = sem("ol_ready")
        s.rope_done = sem("rope_done")
        s.qz_ready = sem("qz_ready")
        s.gy_ready = sem("gy_ready")
        s.tanh_ready = sem("tanh_ready")
        s.gated = sem("gated")
        s.h_ready = sem("h_ready")
        s.out_done = sem("out_done")
        s.x_added = sem("x_added")
        s.pe_waited = sem("pe_waited")
        s.dve_waited = sem("dve_waited")
        s.pool_waited = sem("pool_waited")
        s.lgt_ready = sem("lgt_ready")
        s.lgt_copied = sem("lgt_copied")
        s.gate_step = sem("gate_step")
        s.gate_exp_in = sem("gate_exp_in")
        s.gate_exp = sem("gate_exp")
        s.w_ready = sem("w_ready")
        s.stored = sem("stored")
        s.pads_zero = sem("pads_zero")
        s.r_bn_done = sem("r_bn_done")
        s.r_stats = sem("r_stats")
        s.r_var = sem("r_var")
        s.r_rstd = sem("r_rstd")
        s.r_xn_ready = sem("r_xn_ready")
        s.r_xh_ready = sem("r_xh_ready")
        s.choices = sem("choices")
        s.route_exp_in = sem("route_exp_in")
        s.route_exp = sem("route_exp")
        s.route_step = sem("route_step")
        s.place_step = sem("place_step")
        s.rows_ready = sem("rows_ready")
        s.rows_copied = sem("rows_copied")
        s.counted = sem("counted")
        s.table_step = sem("table_step")
        s.pads_ready = sem("pads_ready")
        s.pads_stored = sem("pads_stored")
        s.tables = sem("tables")
        s.row_high = sem("row_high")
        s.e_products = sem("e_products")
        s.e_tanh = sem("e_tanh")
        s.e_gated = sem("e_gated")
        s.e_hidden = sem("e_hidden")
        s.e_out = sem("e_out")
        s.e_numbered = sem("e_numbered")
        s.e_copied = sem("e_copied")
        s.added = sem("added")
        row_in = [sem(f"row_in{i}") for i in range(4)]
        e_stored = [sem(f"e_stored{i}") for i in range(4)]
        y_in = [sem(f"y_in{i}") for i in range(4)]
        ring_full = {n: [sem(f"full_{n}_{i}") for i in range(n)] for n in RING}
        ring_free = {n: [sem(f"free_{n}_{i}") for i in range(n)] for n in RING}

        def full(k):
            return ring_full[k.banks][k.bank]

        def free(k):
            return ring_free[k.banks][k.bank]

        w_landed = [s.w_landed0, s.w_landed1]
        ctx_in = [s.ctx_in0, s.ctx_in1]
        mrow_in = [s.mrow_in0, s.mrow_in1]
        MISC, LATER = 16 * 4, 16 * 9
        scattered = [sem(f"scattered{i}") for i in range(4)]

        def rows_of(n):
            return rows[:, n % 2, n // 2 % 2]

        def wchunk(src, h, l, a, n, b=0):
            return src[:, b:b + n], h[:, a:a + n], l[:, a:a + n], n
        wchunks = [wchunk(wa, big_h, big_l, c * 1024, 1024, c * 1024) for c in range(3)]
        wchunks.append(wchunk(woa, big_h, big_l, 3072, 1024))
        wchunks += [wchunk(wfa, mid_h, mid_l, c * 960, 960, c * 960) for c in range(2)]
        wchunks.append(wchunk(wbg, sml_h, sml_l, 0, 5 * D + 2 * E))
        wchunks += [wchunk(wfb, big_h, big_l, c * 912, 912, c * 912) for c in range(6)]

        def chunks_at(ph, g):
            if ph == 0 and g in (-2, 0):
                return [2, 3] if g else [4, 5, 6]
            if ph == 2 and g in (-2, -1, 0):
                return [11 + 2 * g, 12 + 2 * g]
            return []

        def turn_of(ph, g, part, n=0):
            return SLOTS[ph].turn(g, part, n)

        def qk_turn(ph, g, u):
            return turn_of(ph, g, "QKa", u) if u < 6 else turn_of(ph, g, "QKb", u - 6)

        def v_turn(ph, g, u):
            return turn_of(ph, g, "Va", u) if u < 2 else turn_of(ph, g, "Vb", u - 2)

        block = ctx.enter_context(nc.Block())

        @block.sync
        def _(sp):
            def load_w(c):
                if c >= 2:
                    sp.wait_ge(s.w_split, c - 1)
                src, _, _, n = wchunks[c]
                sp.dma_start(wst[:, c % 2, 0:n], src).then_inc(w_landed[c % 2], 16)

            def loads(ph, g):
                if not has_attn(g.first, "ln"):
                    return
                p, a = g.parity, ph // 2 * GROUPS
                if g.first >= 0 or ph:
                    sp.wait_ge(s.cl_ready, g.times(1, a + 1))
                    sp.wait_ge(s.bias_ready, g.times(1, a + 1))
                sp.dma_start(cst[:, p, :], ctxT[:, bass.ds(g.times(GT, 2 * GT), GT)]).then_inc(ctx_in[p], 16)
                rows = mask_rows if ph == 0 else imask_rows
                dst = mrow[:, p, :] if ph == 0 else mrow[:, p, :].bitcast(I32)
                sp.dma_start(dst, rows[0:1, bass.ds(g.times(GT, 2 * GT), GT)].broadcast_to([P, GT])
                             ).then_inc(mrow_in[p], 16)

            xd = x.rearrange("(t p) d -> p t d", p=P)
            sp.dma_start(xs[:, 0:4, :], xd[:, 0:4, :]).then_inc(s.x_first, 16)
            load_w(0)
            load_w(1)
            loads(0, Step(-2))
            load_w(2)
            load_w(3)
            for dst, src in ((bo[0][:], boa), (bo[1][:], bob), (qmask[0:S, :], maskT), (qmask[S:P, :], maskT)):
                sp.dma_start(dst, src).then_inc(s.misc_in, 16)
            loads(0, Step(-1))
            sp.dma_start(xs[:, 4:TILES, :], xd[:, 4:TILES, :]).then_inc(s.x_rest, 16)
            load_w(4)
            load_w(5)
            for dst, src in ((ropec[:], cosT), (ropes[:], sinT), (headmask[:], hm), (causal[:], cz), (vmask[:], vm),
                             (wob_sb[:], wob), (w2a[:], wfo), (w2b[:], wfbo), (rcs[:], rc)):
                sp.dma_start(dst, src).then_inc(s.later_in, 16)
            loads(0, Step(0))
            load_w(6)
            run_bodies(sp, 1, lambda g: loads(0, g), 0)
            load_w(7)
            load_w(8)
            for g in range(-2, 1):
                loads(2, Step(g))
                if g >= -1:
                    load_w(2 * g + 11)
                    load_w(2 * g + 12)
            run_bodies(sp, 1, lambda g: loads(2, g), 2)
            sp.wait_ge(s.pads_ready, 1)
            _, behind = nc.values_load_multi_w_load_instructions(
                padi[0:1, 0:E], engines=[mybir.EngineType.SP], min_val=0, max_val=E * REG - P,
                skip_runtime_bounds_check_because="a place behind an expert's tokens")
            for e in range(E):
                sp.dma_start(rows_d[bass.ds(behind[e], P), :], padr[:, e, :]).then_inc(s.pads_stored, 16)
            sp.wait_ge(s.tables, 1)
            for n in range(4):
                sp.wait_ge(scattered[n], GROUPS // 4 * 4 * 16)
            sp.wait_ge(s.pads_stored, E * 16)

            def load_rows(j, base):
                if not has_expert(j.first, "U"):
                    return
                if j.first >= 4:
                    sp.wait_ge(s.e_numbered, j.times(1, -3))
                sp.dma_start(xt[:, j.first % 4, :], rows_d[bass.ds(base(j), P), :]).then_inc(row_in[j.first % 4], 16)

            def row_numbers(tile, n):
                _, r = nc.values_load_multi_w_load_instructions(
                    tab_b[0:1, bass.ds(tile.times(1), n)], engines=[mybir.EngineType.SP], min_val=0,
                    max_val=E * REG - P, skip_runtime_bounds_check_because="the table holds first rows of tiles")
                return r

            run_tiles(sp, load_rows, row_numbers)
            for i in range(4):
                sp.wait_ge(e_stored[i], 16 * len(range(i, NT, 4)))
            part = TILES // 4
            yd = y_d[0:2 * TOK, :].rearrange("(k t p) d -> k p t d", k=2, p=P)
            od = out.rearrange("(t p) d -> p t d", p=P)
            for c in range(4):
                for k in range(2):
                    sp.dma_start(yl[k][:, c * part:(c + 1) * part, :], yd[k, :, c * part:(c + 1) * part, :]
                                 ).then_inc(y_in[c], 16)
            for c in range(4):
                sp.wait_ge(s.added, 2 * (c + 1))
                sp.dma_start(od[:, c * part:(c + 1) * part, :], xs[:, c * part:(c + 1) * part, :]).then_inc(s.stored, 16)
            sp.wait_ge(s.stored, 64)

        @block.gpsimd
        def _(pool):
            nc.gpsimd.memset(ident[:], 0.0).then_inc(s.fixed, 1)
            pool.wait_ge(s.fixed, 1)
            nc.gpsimd.affine_select(out=ident[:], in_=ident[:], compare_op=ALU.not_equal, fill=1.0, base=0,
                                    pattern=[[-1, P]], channel_multiplier=1).then_inc(s.consts, 1)
            nc.gpsimd.memset(mhalf[:], -0.5).then_inc(s.consts, 1)
            for e in range(E):
                nc.gpsimd.memset(iota8[:, e:e + 1], float(e)).then_inc(s.consts, 1)
            nc.gpsimd.memset(wts[:], 0.5).then_inc(s.consts, 1)
            pool.wait_ge(s.consts, 3 + E)

            def rstd_of(ph, g):
                n = ph * GROUPS + 2
                pool.wait_ge(s.ln_stats, g.times(1, n + 1))
                pool.sem_inc(s.pool_waited, 1)
                nc.gpsimd.tensor_scalar(var[:, :], mv[:, :, 1], EPS, None, ALU.add).then_inc(s.var_ready, 1)
                pool.wait_ge(s.var_ready, g.times(1, n + 1))
                nc.gpsimd.tensor_tensor(rstd[:, :], var[:, :], mhalf[:, 0:2], ALU.pow).then_inc(s.rstd_ready, 1)

            def over_keys(t, p):
                return t[:, p, :].unsqueeze(2).broadcast_to([P, HEADS, S])

            def centre(tile, p):
                pool.wait_ge(s.maxed, tile + 1)
                t = sm[:, p].rearrange("p h (b k) -> p (h b) k", b=2)
                nc.gpsimd.tensor_tensor(t, t, over_keys(mx, p), ALU.subtract).then_inc(s.centred, 1)

            def normalise(tile, p):
                pool.wait_ge(s.sum_ready, tile + 1)
                t = sm[:, p].rearrange("p h (b k) -> p (h b) k", b=2)
                nc.gpsimd.tensor_tensor(t, t, over_keys(rinv, p), ALU.mult).then_inc(s.probs, 1)

            def attn_body(ph, g):
                f, n = g.first, ph // 2 * TILES
                if has_attn(f, "PTodd"):
                    normalise(g.times(2, n - 1), 1)
                if has_attn(f, "ln"):
                    rstd_of(ph, g)
                if ph and has_route(f, "gates"):
                    rstd_r_of(g)
                if has_attn(f, "S"):
                    centre(g.times(2, n), 0)
                if has_attn(f, "X") and ph == 2:
                    for u, dst in enumerate((qr, kT[:, (f + 1) % 2, 0, :])):
                        k = qk_turn(ph, g, u)
                        pool.wait_ge(free(k), k.earlier(1))
                        nc.gpsimd.tensor_tensor(dst, rope_t[:, 2 * u, :], rope_t[:, 2 * u + 1, :],
                                                ALU.add).then_inc(s.rope_done, 1)
                if has_attn(f, "S"):
                    normalise(g.times(2, n), 0)
                if ph:
                    scatter_rows(g)
                if has_attn(f, "S"):
                    centre(g.times(2, n + 1), 1)
            def scatter(index, row, done):
                nc.gpsimd.indirect_dma_start(rows_d, bass.IndirectOffsetOnAxis(ap=index, axis=0), row, None
                                             ).then_inc(done, 16)

            def rstd_r_of(g):
                pool.wait_ge(s.r_stats, g.times(1, -1))
                pool.sem_inc(s.pool_waited, 1)
                nc.gpsimd.tensor_scalar(var_r[:, :], mv_r[:, :, 1], EPS, None, ALU.add).then_inc(s.r_var, 1)
                pool.wait_ge(s.r_var, g.times(1, -1))
                nc.gpsimd.tensor_tensor(rstd_r[:, :], var_r[:, :], mhalf[:, 0:2], ALU.pow).then_inc(s.r_rstd, 1)

            def scatter_rows(g):
                if has_route(g.first, "places"):
                    n = (g.first - 4) % 4
                    pool.wait_ge(s.rows_copied, g.times(1, -3))
                    pool.wait_ge(s.rows_ready, g.times(1, -3))
                    pool.sem_inc(s.pool_waited, 1)
                    for t in range(2):
                        for k in range(2):
                            scatter(slot[:, n, 2 * t + k:2 * t + k + 1], rows_of(n)[:, t, k, :], scattered[n])

            def ffn_body(ph, g):
                if has_ffn(g.first, "ln"):
                    rstd_of(ph, g)

            def expert_body(j, _):
                if has_expert(j.first, "Y"):
                    b = (j.first - 3) % 4
                    pool.wait_ge(s.e_copied, j.times(1, -2))
                    pool.sem_inc(s.pool_waited, 1)
                    nc.gpsimd.indirect_dma_start(y_d, bass.IndirectOffsetOnAxis(ap=idb[:, b:b + 1], axis=0),
                                                 yb[:, b, :], None).then_inc(e_stored[b], 16)

            for ph in phases:
                run_bodies(pool, -1 if ph else -2, lambda g, p=ph: (attn_body, ffn_body)[p % 2](p, g), ph)
            run_tiles(pool, expert_body)

        @block.scalar
        def _(act):
            def take(k):
                act.wait_ge(full(k), k.earlier(1))
                return ST[:, k.bank, :]

            def copy(o, i):
                return nc.scalar.activation(o, i, ACT.Copy)

            def split_high(c):
                _, h, _, n = wchunks[c]
                act.wait_ge(w_landed[c % 2], 16 * (c // 2 + 1))
                copy(h, wst[:, c % 2, 0:n]).then_inc(s.w_high, 1)

            def x_high(ph, g):
                k = turn_of(ph, g, "X")
                copy(xh[:, (g.first + 1) % 2, :], take(k)[:, 0:GT]).then_inc(s.xh_ready, 1)

            def context_high(ph, g):
                b = 1 - g.parity
                act.wait_ge(ctx_in[b], g.plus(1).halved(ph // 2 * GROUPS) * 16 + 16)
                copy(ch[:, b, :], cst[:, b, :]).then_inc(s.ch_ready, 1)

            def exp(tile, p):
                act.wait_ge(s.centred, tile + 1)
                nc.scalar.activation(sm[:, p], sm[:, p], ACT.Exp).then_inc(s.expd, 1)

            def probs_turned(ph, g, part, p):
                for u in range(2):
                    k = turn_of(ph, g, part, u)
                    copy(pT[:, p, 4 * u:4 * u + 4, :], take(k).rearrange("p (h q) -> p h q", h=4)
                         ).then_inc(free(k), 1)

            def out_high(ph, tile, p):
                act.wait_ge(s.attn_out, tile + 1)
                if ph == 0:
                    copy(oh[:, :, p * P:(p + 1) * P].rearrange("p h (b q) -> p b h q", b=2),
                         AO[:, :, :].rearrange("p b (h q) -> p b h q", h=HP)).then_inc(s.oh_ready, 1)
                else:
                    copy(oT1[:, p * P:(p + 1) * P].rearrange("p (b q) -> p b q", b=2), AO[:, :, 0:S]
                         ).then_inc(s.oh_ready, 1)

            def queries(g, pairs):
                for u in pairs:
                    k = qk_turn(0, g, 2 * u)
                    copy(qT[:, (g.first + 1) % 2, 2 * u:2 * u + 2, :], take(k).rearrange("p (h t) -> p h t", h=2)
                         ).then_inc(free(k), 1)

            def values(g, t):
                k = v_turn(0, g, 2 * t)
                copy(v[:, (g.first + 1) % 2, t, 0:512], take(k)).then_inc(free(k), 1)

            def attn_body(ph, g):
                f, n, a = g.first, ph // 2 * TILES, ph // 2 * GROUPS
                if has_attn(f, "X") and ph == 0:
                    context_high(ph, g)
                    x_high(ph, g)
                if has_attn(f, "PTodd"):
                    exp(g.times(2, n - 1), 1)
                if has_attn(f, "X"):
                    if ph:
                        x_high(ph, g)
                        context_high(ph, g)
                    if ph == 0:
                        queries(g, range(3))
                if has_attn(f, "PTodd"):
                    probs_turned(ph, g, "PTodd", 1)
                if has_attn(f, "QKb") and ph == 0:
                    queries(g, (3,))
                if has_attn(f, "PTodd"):
                    out_high(ph, g.times(2, n - 1), 1)
                if has_attn(f, "S"):
                    exp(g.times(2, n), 0)
                if ph and has_route(f, "ranks"):
                    route_exp(g)
                if has_attn(f, "Va") and ph == 0:
                    values(g, 0)
                if has_attn(f, "Wo"):
                    k = turn_of(ph, g, "Wo")
                    nc.scalar.activation(yT[:, :], take(k)[:, 0:GT], ACT.Identity, bias=bo[ph // 2][:, 0:1]
                                         ).then_inc(free(k), 1)
                if has_attn(f, "PTeven"):
                    probs_turned(ph, g, "PTeven", 0)
                if has_attn(f, "Vb") and ph == 0:
                    values(g, 1)
                if ph and has_route(f, "gates"):
                    route_high(g)
                if has_attn(f, "PTeven"):
                    out_high(ph, g.times(2, n), 0)
                if ph and has_route(f, "gates"):
                    logits_out(ST[:, turn_of(ph, g, "LR").bank, :], g.times(1, GROUPS - 1))
                for c in chunks_at(ph, f if g.reg is None else None):
                    split_high(c)

            def ffn_body(ph, g):
                f = g.first
                cn, w, bl, bn = CHN0, CH0, BL0, BN0
                nj = 2 * cn
                if has_ffn(f, "X"):
                    x_high(ph, g)
                    if f < 0:
                        logits_out(ST[:, turn_of(ph, g, "L").bank, :], g.times(1, 2))
                        gate_exp(g, 1)
                for j in range(nj):
                    if has_ffn(f, "T0"):
                        act.wait_ge(s.gy_ready, g.times(nj, j + 1))
                        nc.scalar.activation(th[:, j % 2, 0:w], GY[:, j % 2, 0:w], ACT.Tanh, scale=0.5
                                             ).then_inc(s.tanh_ready, 1)
                    turned = (turn_of(ph, g, "Tp") if j == 0 else turn_of(ph, g, "T0") if j == 1
                              else turn_of(ph, g, "T", j - 2))
                    if has_ffn(f, "Tp" if j == 0 else "T0"):
                        i = take(turned)
                        before = g.times(nj, j - 2)
                        if not (f == 0 and j <= 2):
                            act.wait_ge(s.out_done, before)
                        copy(hT[0:bl, (j + 1) % 2, 0:bn * P], i[0:bl, 0:bn * P]).then_inc(free(turned), 1)
                    if j == 0 and has_ffn(f, "X") and f >= 0:
                        logits_out(ST[:, turn_of(ph, g, "L").bank, :], g.times(1, 2))
                    if j == 3 and has_ffn(f, "X") and f >= 0:
                        gate_exp(g, 1)

            def route_high(g):
                b = g.parity
                copy(xh[:, b, :], take(turn_of(2, g, "Xr"))[:, 0:GT]).then_inc(s.r_xh_ready, 1)
                act.wait_ge(s.r_xn_ready, g.times(1, -1))
                r = rows_of(g.first - 2)
                copy(r[:, :, 1, 0:D], r[:, :, 0, 0:D]).then_inc(s.rows_copied, 1)

            def route_exp(g):
                act.wait_ge(s.route_exp_in, g.times(1, -2))
                nc.scalar.activation(ex2[:], ex2[:], ACT.Exp).then_inc(s.route_exp, 1)

            def expert_body(j, _):
                f = j.first
                if has_expert(f, "X"):
                    copy(xh[:, (f + 1) % 2, 0:P], take(EXPERT.turn(j, "X"))[:, 0:P]).then_inc(s.row_high, 1)
                if has_expert(f, "U"):
                    act.wait_ge(s.e_products, j.times(1, 1))
                    nc.scalar.activation(th[:, f % 2, 0:CH1], GY[:, f % 2, 0:CH1], ACT.Tanh, scale=0.5
                                         ).then_inc(s.e_tanh, 1)
                if has_expert(f, "H"):
                    k = EXPERT.turn(j, "H")
                    if f >= 3:
                        act.wait_ge(s.e_out, j.times(1, -2))
                    copy(hT[0:BL1, (f - 1) % 2, 0:BN1 * P], take(k)[0:BL1, 0:BN1 * P]).then_inc(free(k), 1)

            def logits_out(o, ready):
                act.wait_ge(s.lgt_ready, ready)
                copy(lgt[:, :], o[0:E, GT:2 * GT]).then_inc(s.lgt_copied, 1)

            def gate_exp(g, ahead):
                act.wait_ge(s.gate_exp_in, g.times(1, ahead + 1))
                nc.scalar.activation(ex[:], ex[:], ACT.Exp).then_inc(s.gate_exp, 1)

            for c in range(2):
                split_high(c)
            act.wait_ge(s.misc_in, MISC)
            for ph in phases:
                run_bodies(act, -1 if ph else -2, lambda g, p=ph: (attn_body, ffn_body)[p % 2](p, g), ph)
            run_tiles(act, expert_body)

        @block.vector
        def _(dve):
            V = nc.vector

            def take(k):
                dve.wait_ge(full(k), k.earlier(1))
                return ST[:, k.bank, :]

            def split_low(c):
                _, h, l, n = wchunks[c]
                dve.wait_ge(s.w_high, c + 1)
                V.tensor_tensor(l, wst[:, c % 2, 0:n], h.bitcast(F32), ALU.subtract).then_inc(s.w_split, 1)

            def ln_stats(ph, g):
                f, n = g.first, ph * GROUPS + 2
                if f == -2:
                    if ph == 0:
                        dve.wait_ge(s.x_first, 16)
                    elif ph % 2:
                        last = turn_of(ph - 1, Step(GROUPS - 1), "tail", 1)
                        dve.wait_ge(free(last), last.earlier(1))
                    else:
                        dve.wait_ge(s.x_added, 4 + 1)
                if f == 0 and ph == 0:
                    dve.wait_ge(s.x_rest, 16)
                for t in range(2):
                    V.bn_stats(stats[:, t, :], xs[:, bass.ds(g.times(2, 4 + t), 1), :].rearrange("p a d -> p (a d)")
                               ).then_inc(s.bn_done, 1)
                dve.wait_ge(s.bn_done, g.times(2, 2 * n + 2))
                dve.sem_inc(s.dve_waited, 1)
                V.bn_aggr(mv[:, 0, :], stats[:, 0, :])
                V.bn_aggr(mv[:, 1, :], stats[:, 1, :]).then_inc(s.ln_stats, 1)

            def ln_norm(ph, g):
                n = ph * GROUPS + 2
                dve.wait_ge(s.rstd_ready, g.times(1, n + 1))
                dve.wait_ge(s.ln_stats, g.times(1, n + 1))
                for t in range(2):
                    ins = V.tensor_scalar(xn[:, t, :], xs[:, bass.ds(g.times(2, 4 + t), 1), :].rearrange("p a d -> p (a d)"),
                                          mv[:, t, 0:1], rstd[:, t:t + 1], ALU.subtract, ALU.mult)
                ins.then_inc(s.xn_ready, 1)

            def x_low(ph, g):
                k = turn_of(ph, g, "X")
                b = (g.first + 1) % 2
                dve.wait_ge(s.xh_ready, g.times(1, ph * GROUPS + 2))
                V.tensor_tensor(xl[:, b, :], take(k)[:, 0:GT], xh[:, b, :].bitcast(F32), ALU.subtract
                                ).then_inc(free(k), 1)

            def context_low(ph, g):
                b = 1 - g.parity
                dve.wait_ge(s.ch_ready, g.times(1, ph // 2 * GROUPS + 2))
                V.tensor_tensor(cl[:, b, :], cst[:, b, :], ch[:, b, :].bitcast(F32), ALU.subtract
                                ).then_inc(s.cl_ready, 1)

            def mask_and_max(ph, tile, g, p):
                b = g.parity
                dve.wait_ge(s.scores, tile + 1)
                dve.wait_ge(s.bias_ready, g.times(1, ph // 2 * GROUPS + 1))
                V.scalar_tensor_tensor(out=sm[:, p], in0=SC.rearrange("p a (h k) -> p (a h) k", h=4),
                                       scalar=float((DH0, DH1)[ph // 2]) ** -0.5,
                                       in1=bias[:, b, p * P:(p + 1) * P].unsqueeze(1).broadcast_to([P, HP, P]),
                                       op0=ALU.mult, op1=ALU.add).then_inc(s.masked, 1)
                dve.wait_ge(s.masked, tile + 1)
                V.tensor_reduce(mx[:, p, :], sm[:, p].rearrange("p h (b k) -> p (h b) k", b=2), AX_X, ALU.max
                                ).then_inc(s.maxed, 1)

            def sum_inverse(ph, tile, g, p):
                dve.wait_ge(s.expd, tile + 1)
                V.tensor_reduce(sums[:, p, :], sm[:, p].rearrange("p h (b k) -> p (h b) k", b=2), AX_X, ALU.add
                                ).then_inc(s.summed, 1)
                dve.wait_ge(s.summed, tile + 1)
                if ph:
                    V.reciprocal(rinv[:, p, :], sums[:, p, :]).then_inc(s.sum_ready, 1)
                    return
                V.reciprocal(rinv[:, p, :], sums[:, p, :]).then_inc(s.inverted, 1)
                dve.wait_ge(s.inverted, tile + 1)
                r = rinv[:, p, :].rearrange("p (h b) -> p h b", b=2)
                V.tensor_tensor(r, r, valid[:, g.parity, 2 * p:2 * p + 2].unsqueeze(1).broadcast_to([P, HP, 2]),
                                ALU.mult).then_inc(s.sum_ready, 1)

            def masks(ph, g):
                p, lay = 1 - g.parity, ph // 2
                dve.wait_ge(mrow_in[p], g.plus(1).halved(lay * GROUPS) * 16 + 16)
                m, o = mrow[:, p, :], bias[:, p, :]
                m4, o4 = (t.rearrange("p (b k) -> p b k", b=GB) for t in (m, o))
                done = [0]

                def link(ins):
                    done[0] += 1
                    ins.then_inc(s.bias_step, 1)
                    n = 6 if ph == 0 else 1
                    base = 0 if ph == 0 else 6 * GROUPS
                    dve.wait_ge(s.bias_step, g.times(n, base + n + done[0]))

                if ph == 0:
                    q = qmask[:, bass.ds(g.times(GB, GB), GB)].unsqueeze(2).broadcast_to([P, GB, S])
                    link(V.tensor_tensor(o4, m4, q, ALU.mult))
                    link(V.tensor_scalar(o, o, -1.0, 1.0, ALU.mult, ALU.add))
                    link(V.tensor_scalar(o, o, -1.0, None, ALU.add))
                    link(V.tensor_tensor(o, o, o, ALU.mult))
                    link(V.tensor_scalar(o, o, MASK_TOL ** 2, NEG, ALU.is_le, ALU.mult))
                    link(V.tensor_reduce(vmx[:, p, :], o4, AX_X, ALU.max))
                    V.tensor_scalar(valid[:, p, :], vmx[:, p, :], NEG / 2, None, ALU.is_ge).then_inc(s.bias_ready, 1)
                else:
                    link(V.tensor_scalar(o, m.bitcast(I32), 0.0, NEG, ALU.is_equal, ALU.mult))
                    V.tensor_tensor(o4, o4, causal[:, :].unsqueeze(1).broadcast_to([P, GB, S]), ALU.add
                                    ).then_inc(s.bias_ready, 1)

            def out_low(ph, tile, p):
                if ph:
                    return
                dve.wait_ge(s.oh_ready, tile + 1)
                hi = oh[:, :, p * P:(p + 1) * P].bitcast(F32).rearrange("p h (b q) -> p b h q", b=2)
                V.tensor_tensor(ol[:, :, p * P:(p + 1) * P].rearrange("p h (b q) -> p b h q", b=2),
                                AO[:, :, :].rearrange("p b (h q) -> p b h q", h=HP), hi, ALU.subtract
                                ).then_inc(s.ol_ready, 1)

            def values(g, t):
                k = v_turn(0, g, 2 * t + 1)
                V.tensor_copy(v[:, (g.first + 1) % 2, t, 512:1024], take(k)).then_inc(free(k), 1)

            def place_values(g):
                k = v_turn(2, g, 0)
                i = take(k)
                for t in range(2):
                    ins = V.tensor_tensor(
                        v[:, (g.first + 1) % 2, 0, t * 512:(t + 1) * 512].rearrange("p (j d) -> p j d", j=4),
                        i[:, t * D:(t + 1) * D].unsqueeze(1).broadcast_to([P, 4, D]), vmask[:, :, :], ALU.mult)
                ins.then_inc(free(k), 1)

            def place_queries(g):
                dve.wait_ge(s.rope_done, g.times(2, 3))
                for j in range(8):
                    ins = V.tensor_scalar(qT[:, (g.first + 1) % 2, j, :], qr, headmask[:, j:j + 1], None, ALU.mult)
                ins.then_inc(s.qz_ready, 1)

            def attn_body(ph, g):
                f, n, a = g.first, ph // 2 * TILES, ph // 2 * GROUPS
                b = (f + 1) % 2
                if has_attn(f, "X") and ph == 0:
                    context_low(ph, g)
                    x_low(ph, g)
                if has_attn(f, "PTodd"):
                    sum_inverse(ph, g.times(2, n - 1), g.plus(-1), 1)
                if has_attn(f, "X") and ph:
                    x_low(ph, g)
                    context_low(ph, g)
                if ph and has_route(f - 1, "LR"):
                    route_take(g)
                if has_attn(f, "ln"):
                    ln_stats(ph, g)
                if ph and has_route(f, "gates"):
                    route_stats(g)
                if has_attn(f, "S"):
                    mask_and_max(ph, g.times(2, n), g, 0)
                if has_attn(f, "X"):
                    if ph == 0:
                        for u in range(4):
                            k = qk_turn(0, g, 2 * u + 1)
                            V.tensor_copy(kT[:, b, 2 * u:2 * u + 2, :], take(k).rearrange("p (h t) -> p h t", h=2)
                                          ).then_inc(free(k), 1)
                    else:
                        if f >= 0:
                            dve.wait_ge(s.rope_done, g.times(2, 2))
                        for u in range(2):
                            k = qk_turn(ph, g, u)
                            i = take(k)
                            for r, tab in enumerate((ropec, ropes)):
                                ins = V.tensor_tensor(
                                    rope_t[:, 2 * u + r, :].rearrange("p (b k) -> p b k", b=GB),
                                    i[:, r * GT:(r + 1) * GT].rearrange("p (b k) -> p b k", b=GB),
                                    tab[:, :].unsqueeze(1).broadcast_to([P, GB, S]), ALU.mult)
                            ins.then_inc(free(k), 1)
                    masks(ph, g)
                if ph and has_route(f, "places"):
                    route_places(g)
                if has_attn(f, "ln"):
                    ln_norm(ph, g)
                if has_attn(f, "PTodd"):
                    out_low(ph, g.times(2, n - 1), 1)
                if ph and has_route(f, "ranks"):
                    route_choose(g)
                if has_attn(f, "S"):
                    sum_inverse(ph, g.times(2, n), g, 0)
                if has_attn(f, "Va"):
                    if ph == 0:
                        values(g, 0)
                    else:
                        place_values(g)
                        place_queries(g)
                if ph and has_route(f, "gates"):
                    route_norm(g)
                if has_attn(f, "S"):
                    mask_and_max(ph, g.times(2, n + 1), g, 1)
                if ph and has_route(f, "ranks"):
                    route_weights(g)
                if ph and has_route(f, "gates"):
                    route_low(g)
                if has_attn(f, "Vb") and ph == 0:
                    values(g, 1)
                if has_attn(f, "tail"):
                    for u in range((2, 1)[ph // 2]):
                        k = turn_of(ph, g, "tail", u)
                        n_t = (1, 2)[ph // 2]
                        xg = xs[:, bass.ds(g.times(2, u - 2), n_t), :]
                        V.tensor_tensor(xg, take(k)[:, 0:n_t * D].rearrange("p (t d) -> p t d", t=n_t), xg, ALU.add
                                        ).then_inc(free(k), 1)
                if has_attn(f, "PTeven"):
                    out_low(ph, g.times(2, n), 0)
                for c in chunks_at(ph, f if g.reg is None else None):
                    split_low(c)

            def gate_logits(ph, g):
                k = turn_of(ph, g, "L")
                V.tensor_copy(lg[:], take(k)[:, 0:2 * E].rearrange("p (t e) -> p t e", t=2)
                              ).then_inc(free(k), 1)

            def gate_top(ph, g):
                k = turn_of(ph, g, "L")
                dve.wait_ge(free(k), k.earlier(1))
                dve.sem_inc(s.dve_waited, 1)
                step = gate_link(g, 1, 0)
                for t in range(2):
                    ins = V.max(top[:, t, :], lg[:, t, :])
                step(ins)
                V.tensor_tensor(ex[:], lg[:], top[:, :, 0:1].broadcast_to([P, 2, E]), ALU.subtract
                                ).then_inc(s.gate_exp_in, 1)
                for t in range(2):
                    ins = V.max_index(topi[:, t, :], top[:, t, :], lg[:, t, :])
                step(ins)
                step(V.tensor_copy(topf[:], topi[:]))
                io = iota8[:, :].unsqueeze(1).broadcast_to([P, 2, E])
                V.tensor_tensor(sel0[:], io, topf[:, :, 0:1].broadcast_to([P, 2, E]), ALU.is_equal)
                step(V.tensor_tensor(sel1[:], io, topf[:, :, 1:2].broadcast_to([P, 2, E]), ALU.is_equal))
                step(V.tensor_tensor(sel0[:], sel0[:], sel1[:], ALU.add))

            def gate_weights(g, ahead):
                step = gate_link(g, ahead, GATE_TOP_STEPS)
                dve.wait_ge(s.gate_exp, g.times(1, ahead + 1))
                step(V.tensor_tensor(sel1[:], ex[:], sel0[:], ALU.mult))
                step(V.tensor_reduce(gs[:, :], ex[:], AX_X, ALU.add))
                step(V.reciprocal(gr[:, :], gs[:, :]))
                V.scalar_tensor_tensor(out=wts[:, (g.first + ahead) % 2, :, 0:E], in0=sel1[:], scalar=0.5,
                                       in1=gr[:, :].unsqueeze(2).broadcast_to([P, 2, E]),
                                       op0=ALU.mult, op1=ALU.mult).then_inc(s.w_ready, 1)

            GATE_TOP_STEPS, GATE_STEPS = 5, 8

            def gate_link(g, ahead, before):
                done = [before]

                def step(ins):
                    done[0] += 1
                    ins.then_inc(s.gate_step, 1)
                    dve.wait_ge(s.gate_step, g.times(GATE_STEPS, ahead * GATE_STEPS + done[0]))
                return step

            def ffn_body(ph, g):
                f = g.first
                cn, w = CHN0, CH0
                nj = 2 * cn
                if has_ffn(f, "X"):
                    x_low(ph, g)
                if has_ffn(f, "ln") and f < 0:
                    ln_stats(ph, g)
                    ln_norm(ph, g)
                if has_ffn(f, "X") and f < 0:
                    gate_logits(ph, g)
                    gate_top(ph, g)
                    gate_weights(g, 1)
                for j in range(nj):
                    t, c = j // cn, j % cn
                    if f >= 0 and has_ffn(f, "X") and j == 2:
                        gate_logits(ph, g)
                    if has_ffn(f, "T0"):
                        m = g.times(nj, j)
                        gate, y, u, h = GY[:, j % 2, 0:w], GY[:, j % 2, 512:512 + w], ub[:, j % 2, 0:w], hbuf[:, j % 4, 0:w]
                        if j == 0:
                            dve.wait_ge(s.w_ready, g.times(1, 1))
                        dve.wait_ge(s.tanh_ready, m + 1)
                        V.scalar_tensor_tensor(out=u, in0=th[:, j % 2, 0:w], scalar=1.0, in1=gate,
                                               op0=ALU.add, op1=ALU.mult).then_inc(s.gated, 1)
                        dve.wait_ge(s.gated, m + 1)
                        if f:
                            dve.wait_ge(s.out_done, m - 3)
                        for q in range(w // HID0):
                            a, z = q * HID0, (q + 1) * HID0
                            e = c * (w // HID0) + q
                            ins = V.scalar_tensor_tensor(out=h[:, a:z], in0=y[:, a:z],
                                                         scalar=wts[:, g.parity, t, e:e + 1], in1=u[:, a:z],
                                                         op0=ALU.mult, op1=ALU.mult)
                        ins.then_inc(s.h_ready, 1)
                    if (j == 1 and has_ffn(f, "Tp")) or (j == cn + 1 and has_ffn(f, "T0")):
                        tile = g.times(2, -1 if j == 1 else 0)
                        dve.wait_ge(s.out_done, g.times(nj, (0 if j == 1 else cn)))
                        xt = xs[:, bass.ds(tile, 1), :].rearrange("p a d -> p (a d)")
                        V.tensor_tensor(xt, AO[:, 1 if j == 1 else 0, 0:D], xt, ALU.add).then_inc(s.x_added, 1)
                    if has_ffn(f, "ln") and f >= 0 and j == 0:
                        ln_stats(ph, g)
                    if has_ffn(f, "ln") and f >= 0 and j == 1:
                        ln_norm(ph, g)
                    if f >= 0 and has_ffn(f, "X") and j == 2:
                        gate_top(ph, g)
                    if f >= 0 and has_ffn(f, "X") and j == 3:
                        gate_weights(g, 1)

            PLACE_STEPS, CHOOSE_STEPS, ROUTE_STEPS = 2, 6, 8

            def route_link(counter, steps, g, ahead, before=0):
                done = [before]

                def step(ins):
                    done[0] += 1
                    ins.then_inc(counter, 1)
                    dve.wait_ge(counter, g.times(steps, ahead * steps + done[0]))
                return step, done

            def route_stats(g):
                k = turn_of(2, g.plus(-1), "tail")
                dve.wait_ge(free(k), k.earlier(1))
                dve.sem_inc(s.dve_waited, 1)
                for t in range(2):
                    V.bn_stats(stats_r[:, t, :], xs[:, bass.ds(g.times(2, t - 4), 1), :].rearrange("p a d -> p (a d)")
                               ).then_inc(s.r_bn_done, 1)
                dve.wait_ge(s.r_bn_done, g.times(2, -2))
                dve.sem_inc(s.dve_waited, 1)
                V.bn_aggr(mv_r[:, 0, :], stats_r[:, 0, :])
                V.bn_aggr(mv_r[:, 1, :], stats_r[:, 1, :]).then_inc(s.r_stats, 1)

            def route_norm(g):
                b = g.parity
                dve.wait_ge(s.r_rstd, g.times(1, -1))
                dve.wait_ge(s.r_stats, g.times(1, -1))
                n = g.first - 2
                if n >= 4:
                    dve.wait_ge(scattered[n % 4], Turn(n, g.reg, g.per, 4).earlier() * 64)
                for t in range(2):
                    ins = V.tensor_scalar(rows_of(n)[:, t, 0, 0:D],
                                          xs[:, bass.ds(g.times(2, t - 4), 1), :].rearrange("p a d -> p (a d)"),
                                          mv_r[:, t, 0:1], rstd_r[:, t:t + 1], ALU.subtract, ALU.mult)
                ins.then_inc(s.r_xn_ready, 1)

            def route_low(g):
                k = turn_of(2, g, "Xr")
                b = g.parity
                dve.wait_ge(s.r_xh_ready, g.times(1, -1))
                V.tensor_tensor(xl[:, b, :], take(k)[:, 0:GT], xh[:, b, :].bitcast(F32), ALU.subtract).then_inc(free(k), 1)

            def route_take(g):
                k = turn_of(2, g.plus(-1), "LR")
                i = take(k)
                if has_route(g.first - 1, "gates"):
                    ins = V.tensor_copy(lg[:], i[:, 0:2 * E].rearrange("p (t e) -> p t e", t=2))
                if has_route(g.first - 1, "ranks"):
                    ins = V.tensor_tensor(rankb[:], i[:, 2 * E:4 * E].rearrange("p (t e) -> p t e", t=2),
                                          rc_first.unsqueeze(1).broadcast_to([P, 2, E]), ALU.add)
                ins.then_inc(free(k), 1)

            def route_places(g):
                k = turn_of(2, g.plus(-1), "LR")
                dve.wait_ge(free(k), k.earlier(1))
                step, done = route_link(s.place_step, PLACE_STEPS, g, -4)
                step(V.tensor_tensor(prod[:], hot[:], rankb[:].unsqueeze(2).broadcast_to([P, 2, 2, E]), ALU.mult))
                step(V.tensor_reduce(slotf[:], prod[:], AX_X, ALU.add))
                V.tensor_copy(slot[:, (g.first - 4) % 4, :], slotf[:].rearrange("p t k -> p (t k)")).then_inc(s.rows_ready, 1)
                assert done[0] == PLACE_STEPS

            def route_choose(g):
                k = turn_of(2, g.plus(-1), "LR")
                dve.wait_ge(free(k), k.earlier(1))
                b = 1 - g.parity
                step, done = route_link(s.route_step, ROUTE_STEPS, g, -3)
                dve.sem_inc(s.dve_waited, 1)
                for t in range(2):
                    ins = V.max(top[:, t, :], lg[:, t, :])
                step(ins)
                V.tensor_tensor(ex2[:], top[:, :, 0:2], top[:, :, 0:1].broadcast_to([P, 2, 2]), ALU.subtract
                                ).then_inc(s.route_exp_in, 1)
                for t in range(2):
                    ins = V.max_index(topi[:, t, :], top[:, t, :], lg[:, t, :])
                step(ins)
                step(V.tensor_copy(topf[:], topi[:]))
                step(V.tensor_tensor(hot[:], iota8[:, :].unsqueeze(1).unsqueeze(1).broadcast_to([P, 2, 2, E]),
                                     topf[:, :, 0:2].unsqueeze(3).broadcast_to([P, 2, 2, E]), ALU.is_equal))
                step(V.tensor_tensor(both[:], hot[:, :, 0, :], hot[:, :, 1, :], ALU.add))
                step(V.tensor_tensor(cum[:, b, 1, :], cum[:, b, 0, :], both[:, 0, :], ALU.add))
                V.tensor_tensor(cum[:, 1 - b, 0, :], cum[:, b, 1, :], both[:, 1, :], ALU.add).then_inc(s.choices, 1)
                V.tensor_copy(rows_of(g.first - 3)[:, :, :, D + 1],
                              rc_number.rearrange("p (t k) -> p t k", k=2)[:, bass.ds(g.times(2, -6), 2), :])
                assert done[0] == CHOOSE_STEPS

            def route_weights(g):
                step, done = route_link(s.route_step, ROUTE_STEPS, g, -3, CHOOSE_STEPS)
                dve.wait_ge(s.route_exp, g.times(1, -2))
                step(V.tensor_reduce(gs[:, :], ex2[:], AX_X, ALU.add))
                step(V.reciprocal(gr[:, :], gs[:, :]))
                V.scalar_tensor_tensor(out=rows_of(g.first - 3)[:, :, :, D], in0=ex2[:], scalar=0.5,
                                       in1=gr[:, :].unsqueeze(2).broadcast_to([P, 2, 2]), op0=ALU.mult, op1=ALU.mult)
                assert done[0] == ROUTE_STEPS

            def make_tables():
                done = [0]

                def step(ins):
                    done[0] += 1
                    ins.then_inc(s.table_step, 1)
                    dve.wait_ge(s.table_step, done[0])

                V.memset(padr[:], 0.0).then_inc(s.pads_zero, 1)
                dve.wait_ge(s.pads_zero, 2)
                V.tensor_copy(padr[:, :, D + 1], rc_padnum)
                dve.wait_ge(s.counted, 1)
                step(V.tensor_copy(count[:], AO[:, 0, 0:E]))
                step(V.tensor_tensor(padf[:], count[:], rc_pad, ALU.add))
                V.tensor_copy(padi[:], padf[:]).then_inc(s.pads_ready, 1)
                c = cmp[:, 0:E * TILES].rearrange("p (e n) -> p e n", e=E)
                step(V.tensor_tensor(c, count[:].unsqueeze(2).broadcast_to([P, E, TILES]),
                                     rc_edge.unsqueeze(1).broadcast_to([P, E, TILES]), ALU.is_gt))
                step(V.tensor_reduce(ntile[:], c, AX_X, ALU.add))
                c = cmp[:, 0:E * E].rearrange("p (e n) -> p e n", e=E)
                step(V.tensor_tensor(c, rc_upto.rearrange("p (e n) -> p e n", e=E),
                                     ntile[:].unsqueeze(1).broadcast_to([P, E, E]), ALU.mult))
                step(V.tensor_reduce(cume[:], c, AX_X, ALU.add))
                step(V.tensor_scalar(last[:], cume[:, E - 1:E], -1.0, None, ALU.add))
                step(V.tensor_scalar(tj[:], rc_tile, last[:, 0:1], None, ALU.min))
                step(V.tensor_scalar(used[:], rc_tile, last[:, 0:1], None, ALU.is_le))
                step(V.tensor_scalar(alt[:], used[:], -1.0, 1.0, ALU.mult, ALU.add))
                step(V.tensor_tensor(alt[:], alt[:], rc_unused, ALU.mult))
                c = cmp[:, 0:NTAB * E].rearrange("p (n e) -> p n e", e=E)
                step(V.tensor_tensor(c, cume[:].unsqueeze(1).broadcast_to([P, NTAB, E]),
                                     tj[:].unsqueeze(2).broadcast_to([P, NTAB, E]), ALU.is_le))
                step(V.tensor_reduce(te[:], c, AX_X, ALU.add))
                step(V.tensor_tensor(c, c, ntile[:].unsqueeze(1).broadcast_to([P, NTAB, E]), ALU.mult))
                step(V.tensor_reduce(tb[:], c, AX_X, ALU.add))
                step(V.tensor_tensor(tb[:], tj[:], tb[:], ALU.subtract))
                step(V.tensor_scalar(tb[:], tb[:], float(P), None, ALU.mult))
                step(V.scalar_tensor_tensor(out=tb[:], in0=te[:], scalar=float(REG), in1=tb[:], op0=ALU.mult, op1=ALU.add))
                V.tensor_copy(tab_b[:], tb[:])
                V.tensor_copy(tab_e[:], te[:]).then_inc(s.tables, 1)

            def expert_body(j, _):
                f = j.first
                if has_expert(f, "Y"):
                    i = f - 3
                    dve.wait_ge(s.e_out, j.times(1, -2))
                    V.tensor_copy(yb[:, i % 4, :], AO[:, i % 2, 0:D]).then_inc(s.e_copied, 1)
                if has_expert(f, "X"):
                    k = EXPERT.turn(j, "X")
                    dve.wait_ge(s.row_high, j.times(1, 2))
                    V.tensor_tensor(xl[:, (f + 1) % 2, 0:P], take(k)[:, 0:P], xh[:, (f + 1) % 2, 0:P].bitcast(F32),
                                    ALU.subtract).then_inc(free(k), 1)
                if has_expert(f, "H"):
                    i = f - 1
                    if i >= 4:
                        dve.wait_ge(e_stored[i % 4], Turn(i, j.reg, j.per, 4).earlier() * 16)
                    V.tensor_scalar(idb[:, i % 4:i % 4 + 1], xt[:, i % 4, D + 1:D + 2], used[:, bass.ds(j.times(1, -1), 1)],
                                    alt[:, bass.ds(j.times(1, -1), 1)], ALU.mult, ALU.add).then_inc(s.e_numbered, 1)
                if has_expert(f, "U"):
                    dve.wait_ge(s.e_tanh, j.times(1, 1))
                    V.scalar_tensor_tensor(out=ub[:, f % 2, 0:CH1], in0=th[:, f % 2, 0:CH1], scalar=1.0,
                                           in1=GY[:, f % 2, 0:CH1], op0=ALU.add, op1=ALU.mult).then_inc(s.e_gated, 1)
                    dve.wait_ge(s.e_gated, j.times(1, 1))
                    if f >= 4:
                        dve.wait_ge(s.e_out, j.times(1, -3))
                    V.scalar_tensor_tensor(out=hbuf[:, f % 4, 0:CH1], in0=GY[:, f % 2, 512:512 + CH1],
                                           scalar=xt[:, f % 4, D:D + 1], in1=ub[:, f % 2, 0:CH1],
                                           op0=ALU.mult, op1=ALU.mult).then_inc(s.e_hidden, 1)

            def add_places():
                part = TILES // 4
                for c in range(4):
                    dve.wait_ge(y_in[c], 32)
                    for k in range(2):
                        xc = xs[:, c * part:(c + 1) * part, :]
                        V.tensor_tensor(xc, xc, yl[k][:, c * part:(c + 1) * part, :], ALU.add).then_inc(s.added, 1)
                        dve.wait_ge(s.added, 2 * c + k + 1)

            dve.sem_inc(s.x_added, 1)
            for c in range(2):
                split_low(c)
            dve.wait_ge(s.consts, 3 + E)
            dve.wait_ge(s.misc_in, MISC)
            for ph in phases:
                if ph == 1:
                    dve.wait_ge(s.later_in, LATER)
                if ph == 2:
                    V.memset(cum[:], 0.0).then_inc(s.pads_zero, 1)
                    dve.wait_ge(s.pads_zero, 1)
                run_bodies(dve, -1 if ph else -2, lambda g, p=ph: (attn_body, ffn_body)[p % 2](p, g), ph)
            make_tables()
            run_tiles(dve, expert_body)
            add_places()

        @block.tensor
        def _(pe):
            T = nc.tensor

            def bank(k):
                if k.reg is not None or k.first >= k.banks:
                    pe.wait_ge(free(k), k.earlier())
                return ST[:, k.bank, :]

            def taken(k):
                pe.wait_ge(free(k), k.earlier(1))

            def waited():
                pe.sem_inc(s.pe_waited, 1)

            def split_product(o, wh, wl, mh, ml):
                T.matmul(o, wh, ml, start=True, stop=False)
                T.matmul(o, wh, mh, start=False, stop=False)
                return T.matmul(o, wl, mh, start=False, stop=True)

            def turn_x(ph, g):
                k = turn_of(ph, g, "X")
                o = bank(k)
                pe.wait_ge(s.xn_ready, g.times(1, ph * GROUPS + 2))
                for t in range(2):
                    ins = T.transpose(o[:, t * P:(t + 1) * P], xn[:, t, :], ident[:, :])
                ins.then_inc(full(k), 1)

            def project_qk(ph, g, turns):
                b = (g.first + 1) % 2
                for u in turns:
                    k = qk_turn(ph, g, u)
                    o = bank(k)
                    if u == 0:
                        taken(turn_of(ph, g, "X"))
                    if u == 1:
                        pe.wait_ge(s.cl_ready, g.times(1, ph // 2 * GROUPS + 2))
                    mh, ml = ((xh, xl), (ch, cl))[u % 2]
                    for r in range(2):
                        if ph == 0:
                            a, wh, wl = u % 2 * 1024 + (u // 2 * 2 + r) * P, big_h, big_l
                        else:
                            a, wh, wl = (2 * u + r) * P, sml_h, sml_l
                        ins = split_product(o[:, r * GT:(r + 1) * GT], wh[:, a:a + P], wl[:, a:a + P],
                                            mh[:, b, :], ml[:, b, :])
                    ins.then_inc(full(k), 1)

            def project_v(ph, g, tiles):
                b = (g.first + 1) % 2
                for t in tiles:
                    hi, lo = ch[:, b, t * P:(t + 1) * P], cl[:, b, t * P:(t + 1) * P]
                    if ph == 0:
                        for r in range(2):
                            k = v_turn(ph, g, 2 * t + r)
                            o = bank(k)
                            a = 2048 + r * 512
                            split_product(o, hi, lo, big_h[:, a:a + 512], big_l[:, a:a + 512]
                                          ).then_inc(full(k), 1)
                    else:
                        k = v_turn(ph, g, 0)
                        o = bank(k) if t == 0 else o
                        ins = split_product(o[:, t * D:(t + 1) * D], hi, lo, sml_h[:, 4 * D:5 * D], sml_l[:, 4 * D:5 * D])
                        if t:
                            ins.then_inc(full(k), 1)

            def scores(ph, g, t):
                b, lay = g.parity, ph // 2
                tile = g.times(2, lay * TILES + t)
                if not (ph == 0 and g.first == 0 and t == 0):
                    pe.wait_ge(s.masked, tile)
                if ph and t == 0:
                    pe.wait_ge(s.qz_ready, g.times(1, 1))
                    pe.wait_ge(s.rope_done, g.times(2, 2))
                waited()
                for i in range(HP):
                    for c in range(2):
                        for q in range(2):
                            tok = slice(t * P + c * S, t * P + (c + 1) * S)
                            if ph == 0:
                                hp, h2, row = i, q, q
                                lhsT, rhs = qT[row * 64:row * 64 + 64, b, hp, tok], kT[row * 64:row * 64 + 64, b, hp, tok]
                            else:
                                row, j = q, i
                                h = 8 * row + j
                                hp, h2 = h // 2, h % 2
                                lhsT, rhs = qT[row * 64:row * 64 + 64, b, j, tok], kT[row * 64:row * 64 + 64, b, 0, tok]
                            ins = T.matmul(SC[h2 * 64:h2 * 64 + 64, hp // 4, hp % 4 * P + c * S:hp % 4 * P + (c + 1) * S], lhsT, rhs,
                                           start=True, stop=True)
                ins.then_inc(s.scores, 1)

            def turn_probs(ph, g, part, grp, t):
                pe.wait_ge(s.probs, grp.times(2, ph // 2 * TILES + t + 1))
                for u in range(2):
                    k = turn_of(ph, g, part, u)
                    o = bank(k)
                    for i in range(4):
                        ins = T.transpose(o[:, i * P:(i + 1) * P], sm[:, t, 4 * u + i, :], ident[:, :])
                    ins.then_inc(full(k), 1)

            def weight_values(ph, g, part, grp, t):
                lay = ph // 2
                tile = grp.times(2, lay * TILES + t)
                b = grp.parity
                for u in range(2):
                    taken(turn_of(ph, g, part, u))
                if ph == 0:
                    if not (grp.first == 0 and grp.reg is None and t == 0):
                        pe.wait_ge(s.ol_ready, tile)
                    waited()
                    for hp in range(HP):
                        for h2 in range(2):
                            for c in range(2):
                                h = 2 * hp + h2
                                ins = T.matmul(AO[h2 * 64:h2 * 64 + 64, c, hp * S:(hp + 1) * S],
                                               v[c * S:c * S + S, b, t, h * 64:(h + 1) * 64],
                                               pT[c * S:c * S + S, t, hp, h2 * 64:h2 * 64 + 64], start=True, stop=True)
                else:
                    pe.wait_ge(s.oh_ready, tile)
                    waited()
                    for j in range(4):
                        for r in range(4):
                            for c in range(2):
                                h = 4 * r + j
                                ins = T.matmul(AO[32 * r:32 * r + 32, c, 0:S],
                                               v[c * S:c * S + S, b, 0, t * 512 + j * D + 32 * r:t * 512 + j * D + 32 * r + 32],
                                               pT[c * S:c * S + S, t, h // 2, h % 2 * 64:h % 2 * 64 + 64],
                                               start=(j == 0), stop=(j == 3))
                ins.then_inc(s.attn_out, 1)

            def project_out(ph, g):
                k = turn_of(ph, g, "Wo")
                o = bank(k)[:, 0:GT]
                if ph == 0:
                    pe.wait_ge(s.ol_ready, g.times(2, 0))
                    for hp in range(HP):
                        wh, wl = big_h[:, 3072 + hp * P:3072 + (hp + 1) * P], big_l[:, 3072 + hp * P:3072 + (hp + 1) * P]
                        T.matmul(o, wh, ol[:, hp, :], start=(hp == 0), stop=False)
                        T.matmul(o, wh, oh[:, hp, :], start=False, stop=False)
                        ins = T.matmul(o, wl, oh[:, hp, :], start=False, stop=(hp == HP - 1))
                else:
                    pe.wait_ge(s.oh_ready, g.times(2, TILES))
                    ins = T.matmul(o, wob_sb[:, :], oT1, start=True, stop=True)
                ins.then_inc(full(k), 1)

            def turn_back(ph, g):
                taken(turn_of(ph, g, "Wo"))
                for t in range(2):
                    if ph == 0 or t == 0:
                        k = turn_of(ph, g, "tail", t)
                        o = bank(k)
                    a = 0 if ph == 0 else t * P
                    ins = T.transpose(o[:, a:a + P], yT[:, t * P:(t + 1) * P], ident[:, :])
                    if ph == 0 or t == 1:
                        ins.then_inc(full(k), 1)

            def turn_rows(g):
                k = turn_of(2, g, "Xr")
                o = bank(k)
                pe.wait_ge(s.r_xn_ready, g.times(1, -1))
                for t in range(2):
                    ins = T.transpose(o[:, t * P:(t + 1) * P], rows_of(g.first - 2)[:, t, 0, 0:D], ident[:, :])
                ins.then_inc(full(k), 1)

            def route(g):
                f, b = g.first, g.parity
                k = turn_of(2, g, "LR")
                o = bank(k)
                if has_route(f, "ranks"):
                    pe.wait_ge(s.choices, g.times(1, -2))
                    T.matmul(o[:, 2 * E:4 * E], rc_before, both[:].rearrange("p t e -> p (t e)"), start=True, stop=False)
                    ins = T.matmul(o[:, 2 * E:4 * E], rc_ones, cum[:, 1 - b].rearrange("p t e -> p (t e)"),
                                   start=False, stop=True)
                if has_route(f, "gates"):
                    taken(turn_of(2, g, "Xr"))
                    logits_turned(o, b, 5 * D + E)
                else:
                    ins.then_inc(full(k), 1)

            def attn_body(ph, g):
                f = g.first
                if has_attn(f, "X"):
                    turn_x(ph, g)
                if ph and has_route(f - 1, "gates"):
                    k = turn_of(2, g.plus(-1), "LR")
                    logits_back(ST[:, k.bank, :], g.times(1, GROUPS - 2)).then_inc(full(k), 1)
                if has_attn(f, "S"):
                    scores(ph, g, 0)
                if has_attn(f, "QKa"):
                    project_qk(ph, g, range((6, 2)[ph // 2]))
                if has_attn(f, "PTodd"):
                    turn_probs(ph, g, "PTodd", g.plus(-1), 1)
                if has_attn(f, "QKb") and ph == 0:
                    project_qk(ph, g, (6, 7))
                if has_attn(f, "Va") and ph:
                    project_v(ph, g, (0, 1))
                if has_attn(f, "PTodd"):
                    weight_values(ph, g, "PTodd", g.plus(-1), 1)
                if has_attn(f, "S"):
                    scores(ph, g, 1)
                if has_attn(f, "Va") and ph == 0:
                    project_v(ph, g, (0,))
                if has_attn(f, "Wo"):
                    project_out(ph, g)
                if has_attn(f, "PTeven"):
                    turn_probs(ph, g, "PTeven", g, 0)
                if has_attn(f, "Vb") and ph == 0:
                    project_v(ph, g, (1,))
                if ph and has_route(f, "gates"):
                    turn_rows(g)
                if has_attn(f, "tail"):
                    turn_back(ph, g)
                if has_attn(f, "PTeven"):
                    weight_values(ph, g, "PTeven", g, 0)
                if ph and has_route(f, "LR"):
                    route(g)

            def logits_turned(o, b, a):
                split_product(o[0:E, GT:2 * GT], sml_h[:, a:a + E], sml_l[:, a:a + E], xh[:, b, :], xl[:, b, :]
                              ).then_inc(s.lgt_ready, 1)

            def logits_back(o, copied):
                pe.wait_ge(s.lgt_copied, copied)
                waited()
                for t in range(2):
                    ins = T.transpose(o[:, t * E:(t + 1) * E], lgt[:, t * P:(t + 1) * P], ident[0:E, 0:E])
                return ins

            def ffn_body(ph, g):
                f = g.first
                cn, w, bl, bn = CHN0, CH0, BL0, BN0
                wh, wl, w2 = mid_h, mid_l, w2a
                nj = 2 * cn
                if has_ffn(f, "X"):
                    turn_x(ph, g)
                kl = turn_of(ph, g, "L") if has_ffn(f, "L") else None
                if kl and f < 0:
                    gate_bank = bank(kl)
                    taken(turn_of(ph, g, "X"))
                    logits_turned(gate_bank, (f + 1) % 2, 5 * D)
                    logits_back(gate_bank, g.times(1, 2)).then_inc(full(kl), 1)
                for j in range(nj):
                    t, c = j // cn, j % cn
                    if has_ffn(f, "T0"):
                        if not (f == 0 and j < 2):
                            pe.wait_ge(s.h_ready, g.times(nj, j - 1))
                        b = g.parity
                        hi, lo = xh[:, b, t * P:(t + 1) * P], xl[:, b, t * P:(t + 1) * P]
                        for r in range(2):
                            a = r * cn * w + c * w
                            ins = split_product(GY[:, j % 2, r * 512:r * 512 + w], hi, lo, wh[:, a:a + w], wl[:, a:a + w])
                        ins.then_inc(s.gy_ready, 1)
                    if has_ffn(f, "Tp" if j == 0 else "T0"):
                        k = (turn_of(ph, g, "Tp") if j == 0 else turn_of(ph, g, "T0") if j == 1
                             else turn_of(ph, g, "T", j - 2))
                        o = bank(k)
                        pe.wait_ge(s.h_ready, g.times(nj, j))
                        for q in range(bn):
                            ins = T.transpose(o[0:bl, q * P:(q + 1) * P], hbuf[:, (j - 1) % 4, q * bl:(q + 1) * bl], ident[:, :])
                        ins.then_inc(full(k), 1)
                    if has_ffn(f, "Tp" if j < 2 else "T0"):
                        k = (turn_of(ph, g, "X", -1) if j == 0 else turn_of(ph, g, "Tp") if j == 1
                             else turn_of(ph, g, "T0") if j == 2 else turn_of(ph, g, "T", j - 3))
                        taken(k)
                        jj = (j - 2) % nj
                        tt, cc = jj // cn, jj % cn
                        if cc == 0 and not (f == 0 and j >= 2):
                            pe.wait_ge(s.x_added, g.times(2, tt - (2 if j < 2 else 0)))
                        for q in range(bn):
                            ins = T.matmul(AO[:, tt, 0:D], hT[0:bl, jj % 2, q * P:(q + 1) * P], w2[0:bl, cc * bn + q, :],
                                           start=(cc == 0 and q == 0), stop=(cc == cn - 1 and q == bn - 1))
                        ins.then_inc(s.out_done, 1)
                    if kl and f >= 0 and j == 0:
                        gate_bank = bank(kl)
                        taken(turn_of(ph, g, "X"))
                        logits_turned(gate_bank, (f + 1) % 2, 5 * D)
                    if kl and f >= 0 and j == 1:
                        logits_back(gate_bank, g.times(1, 2)).then_inc(full(kl), 1)

            pe.wait_ge(s.consts, 3 + E)
            pe.wait_ge(s.w_split, 4)
            for ph in phases:
                if ph == 1:
                    pe.wait_ge(s.w_split, 7)
                    pe.wait_ge(s.later_in, LATER)
                run_bodies(pe, -1 if ph else -2, lambda g, p=ph: (attn_body, ffn_body)[p % 2](p, g), ph)

            def expert_body(j, expert):
                f = j.first
                if has_expert(f, "X"):
                    k = EXPERT.turn(j, "X")
                    o = bank(k)
                    b = (f + 1) % 4
                    pe.wait_ge(row_in[b], Turn(f + 1, j.reg, j.per, 4).earlier(1) * 16)
                    T.transpose(o[:, 0:P], xt[:, b, 0:D], ident[:, :]).then_inc(full(k), 1)
                if has_expert(f, "U"):
                    taken(EXPERT.turn(j.plus(-1), "X"))
                    if f >= 2:
                        pe.wait_ge(s.e_hidden, j.times(1, -1))
                    hi, lo = xh[:, f % 2, 0:P], xl[:, f % 2, 0:P]
                    e = expert(j)
                    for r in range(2):
                        wh, wl = (w[:, bass.ds(e * CH1 + r * E * CH1, CH1)] for w in (big_h, big_l))
                        ins = split_product(GY[:, f % 2, r * 512:r * 512 + CH1], hi, lo, wh, wl)
                    ins.then_inc(s.e_products, 1)
                if has_expert(f, "H"):
                    k = EXPERT.turn(j, "H")
                    o = bank(k)
                    pe.wait_ge(s.e_hidden, j.times(1))
                    for q in range(BN1):
                        ins = T.transpose(o[0:BL1, q * P:(q + 1) * P], hbuf[:, (f - 1) % 4, q * BL1:(q + 1) * BL1], ident[:, :])
                    ins.then_inc(full(k), 1)
                if has_expert(f, "O"):
                    taken(EXPERT.turn(j.plus(-1), "H"))
                    if f >= 4:
                        pe.wait_ge(s.e_copied, j.times(1, -3))
                    e = expert(j.plus(-2))
                    for q in range(BN1):
                        w = w2b[0:BL1, bass.ds(e * BN1 + q, 1), :].rearrange("p a d -> p (a d)")
                        ins = T.matmul(AO[:, f % 2, 0:D], hT[0:BL1, f % 2, q * P:(q + 1) * P], w,
                                       start=(q == 0), stop=(q == BN1 - 1))
                    ins.then_inc(s.e_out, 1)

            def experts(tile, n):
                _, r = nc.values_load_multi_w_load_instructions(
                    tab_e[0:1, bass.ds(tile.times(1), n)], engines=[mybir.EngineType.PE], min_val=0,
                    max_val=E - 1, skip_runtime_bounds_check_because="the table holds numbers of experts")
                return r

            pe.wait_ge(s.w_split, 13)
            pe.wait_ge(s.choices, GROUPS)
            T.matmul(AO[:, 0, 0:E], rc_ones, cum[:, GROUPS % 2, 0, :], start=True, stop=True).then_inc(s.counted, 1)
            pe.wait_ge(s.tables, 1)
            run_tiles(pe, expert_body, experts)


NAMES = ("x ctx_1024 mask_BxS2_fk1 mask_BxS2_if1 L0_xattn_Wq L0_xattn_Wkv L0_xattn_Wo L0_xattn_bo L0_ffn_gate_w "
         "L0_ffn_W1 L0_ffn_W2 L0_ffn_Ws1 L0_ffn_Ws2 L1_xattn_Wq L1_xattn_Wk L1_xattn_Wv L1_xattn_Wo L1_xattn_bo "
         "L1_ffn_Wg L1_ffn_W1 L1_ffn_W2 L1_ffn_W3").split()


def rope_tables():
    theta = np.float32(1.0) / np.float32(10000.0) ** (np.arange(0, DH1, 2, dtype=np.float32) / np.float32(DH1))
    angle = np.arange(S, dtype=np.float32)[None, :] * theta.astype(np.float32)[:, None]
    cos = np.repeat(np.cos(angle), 2, axis=0)
    sin = np.repeat(np.sin(angle), 2, axis=0) * np.tile(np.array([-1.0, 1.0], np.float32), DH1 // 2)[:, None]
    return np.tile(cos, (HEADS, 1)).astype(np.float32), np.tile(sin, (HEADS, 1)).astype(np.float32)


def route_constants():
    p, e, j = np.arange(P)[:, None], np.arange(E)[None, :], np.arange(NTAB)[None, :]
    number = (np.arange(TILES)[None, :, None] * P + np.arange(2)[None, None, :] * TOK + p[:, :, None]).reshape(P, -1)
    parts = [number, e * REG, e * REG + p, PADS + e * P + p, np.arange(TILES)[None, :] * P,
             np.tril(np.ones((E, E))).reshape(1, -1), j, UNUSED + np.maximum(j - 2 * TOK // P, 0) * P + p,
             p < np.arange(P)[None, :], np.ones((1, P))]
    return np.concatenate([np.broadcast_to(t, (P, t.shape[1])) for t in parts], axis=1).astype(np.float32)


def layouts(a):
    def blocks(w, n, rows):
        return w.reshape(n, rows, D).transpose(1, 0, 2)

    swap = np.arange(D) ^ 1
    y0, g0 = a["L0_ffn_W1"][:, :HID0], a["L0_ffn_W1"][:, HID0:]
    ys, gs = a["L0_ffn_Ws1"][:2 * HID0], a["L0_ffn_Ws1"][2 * HID0:]
    wfa = np.concatenate([g0.reshape(-1, D), gs, y0.reshape(-1, D), ys]).T
    wfo = np.concatenate([a["L0_ffn_W2"].transpose(0, 2, 1).reshape(-1, D), a["L0_ffn_Ws2"].T])
    pad = ((0, 0), (0, PAD1 - HID1), (0, 0))
    wfb = np.concatenate([np.pad(a["L1_ffn_W1"], pad).reshape(-1, D), np.pad(a["L1_ffn_W2"], pad).reshape(-1, D)]).T
    wfbo = np.pad(a["L1_ffn_W3"].transpose(0, 2, 1), pad).reshape(-1, D)
    q1, k1 = a["L1_xattn_Wq"], a["L1_xattn_Wk"]
    cos, sin = rope_tables()
    dims, place = np.arange(D), np.arange(4)
    hm = (dims[:, None] // DH1 % 8 == np.arange(8)[None, :]).astype(np.float32)
    vm = np.broadcast_to(dims[None, None, :] // DH1 % 4 == place[None, :, None], (P, 4, D)).astype(np.float32)
    cz = np.where(np.arange(S)[None, :] > np.arange(P)[:, None] % S, np.float32(NEG), np.float32(0.0))
    return {
        "x": a["x"].reshape(TOK, D), "ctxT": a["ctx_1024"].reshape(TOK, D).T, "maskT": a["mask_BxS2_fk1"].T,
        "mask_rows": a["mask_BxS2_fk1"].reshape(1, TOK), "imask_rows": a["mask_BxS2_if1"].reshape(1, TOK),
        "wa": np.concatenate([a["L0_xattn_Wq"], a["L0_xattn_Wkv"]], axis=1),
        "woa": blocks(a["L0_xattn_Wo"], HP, P).reshape(P, HP * D), "boa": a["L0_xattn_bo"].reshape(D, 1),
        "wfa": wfa, "wfo": blocks(wfo, CHN0 * BN0, BL0),
        "wbg": np.concatenate([q1.T, q1[swap].T, a["L1_xattn_Wk"].T, k1[swap].T, a["L1_xattn_Wv"].T,
                               a["L0_ffn_gate_w"].T, a["L1_ffn_Wg"].T], axis=1),
        "wob": a["L1_xattn_Wo"].T, "bob": a["L1_xattn_bo"].reshape(D, 1),
        "wfb": wfb, "wfbo": blocks(wfbo, E * BN1, BL1), "cosT": cos, "sinT": sin, "hm": hm, "vm": vm, "cz": cz,
        "rc": route_constants(),
    }


def kernel(**inputs):
    import concourse.bacc as _bacc
    from concourse.bass_utils import run_bass_kernel_spmd as _run

    nc = _bacc.Bacc("TRN2", target_bir_lowering=False, num_devices=1)
    arrays, args = {}, {}
    for name, a in layouts({n: np.asarray(inputs[n]) for n in NAMES}).items():
        arrays[f"in_{name}"] = np.ascontiguousarray(a)
        args[name] = nc.dram_tensor(f"in_{name}", a.shape, mybir.dt.from_np(a.dtype), kind="ExternalInput").ap()
    out = nc.dram_tensor("out_0", (TOK, D), F32, kind="ExternalOutput").ap()
    rows_d = nc.dram_tensor("rows_d", (E * REG, ROW), F32, kind="Internal").ap()
    y_d = nc.dram_tensor("y_d", (YROWS, D), F32, kind="Internal").ap()
    build(nc, **args, rows_d=rows_d, y_d=y_d, out=out)
    r = _run(nc, [arrays], core_ids=[0])
    return r.results[0]["out_0"].reshape(B, S, D)
```
